# Optimizing a Trainium2 kernel written in Bass

```python
import numpy as np
import jax
import jax.numpy as jnp

def _softmax(x, axis=-1):
    return jax.nn.softmax(x, axis=axis)

def _gelu(x):
    return jax.nn.gelu(x, approximate=True)

def _silu(x):
    return jax.nn.silu(x)

def _sigmoid(x):
    return jax.nn.sigmoid(x)

def _layernorm(x, axis=-1, eps=1e-05):
    m = jnp.mean(x, axis=axis, keepdims=True)
    v = jnp.var(x, axis=axis, keepdims=True)
    return (x - m) / jnp.sqrt(v + eps)

def _scatter_add(tgt, idx, src, axis=0):
    return tgt.at[idx].add(src)

def _segment_sum(src, seg, n):
    return jax.ops.segment_sum(src, seg, n)
kernel_name = 'mk_macaron_d2_jaxref_r8_574181'

def setup_inputs(seed: int=0):
    np.random.seed(seed)
    _w = jnp.asarray

    def _L0_attn_setup():
        import jax, jax.numpy as jnp
        import numpy as np
        D = 128
        HS = 128
        NKV = 2

        def apply_rope(x):
            d = x.shape[-1]
            T = x.shape[-2]
            positions = jnp.arange(0, d, 2, dtype=jnp.float32)
            theta = 10000.0 ** (-2.0 * positions / d)
            angles = jnp.arange(T, dtype=jnp.float32)[:, None] * theta[None, :]
            cos, sin = (jnp.cos(angles), jnp.sin(angles))
            xr = x.reshape(x.shape[:-1] + (d // 2, 2))
            out = jnp.stack([xr[..., 0] * cos - xr[..., 1] * sin, xr[..., 1] * cos + xr[..., 0] * sin], axis=-1)
            return out.reshape(x.shape)
        key = jax.random.key(seed)
        k1, k2, k3, k4, k5 = jax.random.split(key, 5)
        B, T = (4, 256)
        x = jax.random.normal(k1, (B, T, D), dtype=jnp.float32)
        s = 1.0 / np.sqrt(D)
        Wq = jax.random.normal(k2, (NKV, HS, D), dtype=jnp.float32) * s
        Wk = jax.random.normal(k3, (HS, D), dtype=jnp.float32) * s
        Wv = jax.random.normal(k4, (HS, D), dtype=jnp.float32) * s
        Wo = jax.random.normal(k5, (D, NKV * HS), dtype=jnp.float32) * (1.0 / np.sqrt(NKV * HS))
        return {'x': x, 'Wq': Wq, 'Wk': Wk, 'Wv': Wv, 'Wo': Wo}
    _L0_attn_in = _L0_attn_setup()

    def _L0_ffn_setup():
        import jax, jax.numpy as jnp
        import numpy as np
        LN_EPS = 1e-05

        def layer_norm(x, g, b):
            mu = jnp.mean(x, axis=-1, keepdims=True)
            var = jnp.var(x, axis=-1, keepdims=True)
            return (x - mu) / jnp.sqrt(var + LN_EPS) * g + b

        def balanced_assignment(scores):
            T, E = scores.shape
            C = T // E
            taken = jnp.zeros((T,), dtype=bool)
            parts = []
            for e in range(E):
                s = jnp.where(taken, -jnp.inf, scores[:, e])
                _, idx = jax.lax.top_k(s, C)
                parts.append(idx)
                taken = taken.at[idx].set(True)
            return jnp.concatenate(parts)
        key = jax.random.key(seed)
        ks = jax.random.split(key, 4)
        B, S, D, F, E = (4, 256, 128, 512, 8)
        return {'x': jax.random.normal(ks[0], (B, S, D), dtype=jnp.float32), 'centroids': jax.random.normal(ks[1], (E, D), dtype=jnp.float32) * 0.1, 'ln_g': jnp.ones((D,), dtype=jnp.float32), 'ln_b': jnp.zeros((D,), dtype=jnp.float32), 'w1': jax.random.normal(ks[2], (E, D, F), dtype=jnp.float32) * 0.02, 'b1': jnp.zeros((E, F), dtype=jnp.float32), 'w2': jax.random.normal(ks[3], (E, F, D), dtype=jnp.float32) * 0.02, 'b2': jnp.zeros((E, D), dtype=jnp.float32)}
    _L0_ffn_in = _L0_ffn_setup()

    def _L1_attn_setup():
        import jax, jax.numpy as jnp
        import numpy as np
        B, S, D = (2, 256, 128)
        H, DQ, DV = (16, 64, 64)
        key = jax.random.key(seed)
        k1, k2, k3, k4, k5 = jax.random.split(key, 5)
        scale = 0.02
        return {'x': jax.random.normal(k1, (B, S, D), dtype=jnp.float32), 'w_q': jax.random.normal(k2, (H, DQ, D), dtype=jnp.float32) * scale, 'w_k': jax.random.normal(k3, (H, DQ, D), dtype=jnp.float32) * scale, 'w_v': jax.random.normal(k4, (H, DV, D), dtype=jnp.float32) * scale, 'w_o': jax.random.normal(k5, (D, H * DV), dtype=jnp.float32) * scale}
    _L1_attn_in = _L1_attn_setup()

    def _L1_ffn_setup():
        import jax, jax.numpy as jnp
        import numpy as np
        B, S, D, E = (2, 256, 128, 8)
        key = jax.random.key(seed)
        ks = jax.random.split(key, 5)
        x = jax.random.normal(ks[0], (B, S, D), dtype=jnp.float32)
        router_w = jax.random.normal(ks[1], (E, D), dtype=jnp.float32) * 0.02
        router_b = jnp.zeros((E,), dtype=jnp.float32)
        expert_w = jax.random.normal(ks[2], (E, D, D), dtype=jnp.float32) * 0.02
        expert_b = jnp.zeros((E, D), dtype=jnp.float32)
        return {'x': x, 'router_w': router_w, 'router_b': router_b, 'expert_w': expert_w, 'expert_b': expert_b}
    _L1_ffn_in = _L1_ffn_setup()
    _d = {'L0_attn_x': _L0_attn_in['x'], 'L0_attn_Wq': _L0_attn_in['Wq'], 'L0_attn_Wk': _L0_attn_in['Wk'], 'L0_attn_Wv': _L0_attn_in['Wv'], 'L0_attn_Wo': _L0_attn_in['Wo'], 'L0_ffn_centroids': _L0_ffn_in['centroids'], 'L0_ffn_ln_g': _L0_ffn_in['ln_g'], 'L0_ffn_ln_b': _L0_ffn_in['ln_b'], 'L0_ffn_w1': _L0_ffn_in['w1'], 'L0_ffn_b1': _L0_ffn_in['b1'], 'L0_ffn_w2': _L0_ffn_in['w2'], 'L0_ffn_b2': _L0_ffn_in['b2'], 'L1_attn_w_q': _L1_attn_in['w_q'], 'L1_attn_w_k': _L1_attn_in['w_k'], 'L1_attn_w_v': _L1_attn_in['w_v'], 'L1_attn_w_o': _L1_attn_in['w_o'], 'L1_ffn_router_w': _L1_ffn_in['router_w'], 'L1_ffn_router_b': _L1_ffn_in['router_b'], 'L1_ffn_expert_w': _L1_ffn_in['expert_w'], 'L1_ffn_expert_b': _L1_ffn_in['expert_b']}
    _x0 = _d['L0_attn_x']
    _d['L0_attn_x'] = jax.random.normal(jax.random.fold_in(jax.random.key(seed), 1), (1, 2048, 128), dtype=_x0.dtype)
    del _x0
    return _d

def reference(L0_attn_x, L0_attn_Wq, L0_attn_Wk, L0_attn_Wv, L0_attn_Wo, L0_ffn_centroids, L0_ffn_ln_g, L0_ffn_ln_b, L0_ffn_w1, L0_ffn_b1, L0_ffn_w2, L0_ffn_b2, L1_attn_w_q, L1_attn_w_k, L1_attn_w_v, L1_attn_w_o, L1_ffn_router_w, L1_ffn_router_b, L1_ffn_expert_w, L1_ffn_expert_b):

    def _L0_attn_ref(x, Wq, Wk, Wv, Wo):
        import jax, jax.numpy as jnp
        import numpy as np
        D = 128
        HS = 128
        NKV = 2

        def apply_rope(x):
            d = x.shape[-1]
            T = x.shape[-2]
            positions = jnp.arange(0, d, 2, dtype=jnp.float32)
            theta = 10000.0 ** (-2.0 * positions / d)
            angles = jnp.arange(T, dtype=jnp.float32)[:, None] * theta[None, :]
            cos, sin = (jnp.cos(angles), jnp.sin(angles))
            xr = x.reshape(x.shape[:-1] + (d // 2, 2))
            out = jnp.stack([xr[..., 0] * cos - xr[..., 1] * sin, xr[..., 1] * cos + xr[..., 0] * sin], axis=-1)
            return out.reshape(x.shape)
        B, T, _ = x.shape
        k = apply_rope(x @ Wk.T)
        v = x @ Wv.T
        q = jnp.einsum('btd,hkd->bhtk', x, Wq)
        q = apply_rope(q)
        scale = HS ** (-0.5)
        scores = jnp.einsum('bhtk,bsk->bhts', q, k) * scale
        causal = jnp.tril(jnp.ones((T, T), dtype=bool))
        scores = jnp.where(causal, scores, -jnp.inf)
        w = jax.nn.softmax(scores, axis=-1)
        out = jnp.einsum('bhts,bsk->bhtk', w, v)
        out = out.transpose(0, 2, 1, 3).reshape(B, T, NKV * HS)
        return out @ Wo.T

    def _L0_ffn_ref(x, centroids, ln_g, ln_b, w1, b1, w2, b2):
        import jax, jax.numpy as jnp
        import numpy as np
        LN_EPS = 1e-05

        def layer_norm(x, g, b):
            mu = jnp.mean(x, axis=-1, keepdims=True)
            var = jnp.var(x, axis=-1, keepdims=True)
            return (x - mu) / jnp.sqrt(var + LN_EPS) * g + b

        def balanced_assignment(scores):
            T, E = scores.shape
            C = T // E
            taken = jnp.zeros((T,), dtype=bool)
            parts = []
            for e in range(E):
                s = jnp.where(taken, -jnp.inf, scores[:, e])
                _, idx = jax.lax.top_k(s, C)
                parts.append(idx)
                taken = taken.at[idx].set(True)
            return jnp.concatenate(parts)
        D = x.shape[-1]
        feat = x.reshape(-1, D)
        T = feat.shape[0]
        E = centroids.shape[0]
        C = T // E
        norm = layer_norm(feat, ln_g, ln_b)
        scores = jax.lax.stop_gradient(norm @ centroids.T)
        sort_by_expert = balanced_assignment(scores)
        routed = feat[sort_by_expert].reshape(E, C, D)
        h = layer_norm(routed, ln_g, ln_b)
        h = jax.nn.gelu(jnp.einsum('ecd,edf->ecf', h, w1) + b1[:, None, :])
        h = jnp.einsum('ecf,efd->ecd', h, w2) + b2[:, None, :]
        out = routed + h
        inv = jnp.zeros((T,), dtype=jnp.int32).at[sort_by_expert].set(jnp.arange(T, dtype=jnp.int32))
        return out.reshape(T, D)[inv].reshape(x.shape)

    def _L1_attn_ref(x, w_q, w_k, w_v, w_o):
        import jax, jax.numpy as jnp
        import numpy as np
        B, S, D = (2, 256, 128)
        H, DQ, DV = (16, 64, 64)
        b, s, d = x.shape
        q = jnp.einsum('bsd,hqd->bhsq', x, w_q)
        k = jnp.einsum('bsd,hqd->bhsq', x, w_k)
        v = jnp.einsum('bsd,hvd->bhsv', x, w_v)
        scores = jnp.einsum('bhsq,bhtq->bhst', q, k)
        causal = jnp.triu(jnp.ones((s, s), dtype=bool), k=1)
        masked = jnp.where(causal, -jnp.inf, scores)
        dq = w_q.shape[1]
        weights = jax.nn.softmax(masked / jnp.sqrt(jnp.float32(dq)), axis=-1)
        out = jnp.einsum('bhst,bhtv->bhsv', weights, v)
        cat = out.transpose(0, 2, 1, 3).reshape(b, s, -1)
        return jnp.einsum('bsf,df->bsd', cat, w_o)

    def _L1_ffn_ref(x, router_w, router_b, expert_w, expert_b):
        import jax, jax.numpy as jnp
        import numpy as np
        B, S, D, E = (2, 256, 128, 8)
        logits = jnp.einsum('bsd,ed->bse', x, router_w) + router_b
        probs = jax.nn.softmax(logits, axis=-1)
        weights = jnp.max(probs, axis=-1)
        top1 = jnp.argmax(probs, axis=-1)
        y_all = jnp.einsum('bsd,eod->bseo', x, expert_w) + expert_b
        y = jnp.take_along_axis(y_all, top1[:, :, None, None], axis=2)[:, :, 0, :]
        out = y * weights[:, :, None]
        return out
    x = L0_attn_x
    x = x + 0.5 * _L0_ffn_ref(_layernorm(x, axis=-1), L0_ffn_centroids, L0_ffn_ln_g, L0_ffn_ln_b, L0_ffn_w1, L0_ffn_b1, L0_ffn_w2, L0_ffn_b2)
    x = x + _L0_attn_ref(_layernorm(x, axis=-1), L0_attn_Wq, L0_attn_Wk, L0_attn_Wv, L0_attn_Wo)
    x = x + 0.5 * _L0_ffn_ref(_layernorm(x, axis=-1), L0_ffn_centroids, L0_ffn_ln_g, L0_ffn_ln_b, L0_ffn_w1, L0_ffn_b1, L0_ffn_w2, L0_ffn_b2)
    x = x + 0.5 * _L1_ffn_ref(_layernorm(x, axis=-1), L1_ffn_router_w, L1_ffn_router_b, L1_ffn_expert_w, L1_ffn_expert_b)
    x = x + _L1_attn_ref(_layernorm(x, axis=-1), L1_attn_w_q, L1_attn_w_k, L1_attn_w_v, L1_attn_w_o)
    x = x + 0.5 * _L1_ffn_ref(_layernorm(x, axis=-1), L1_ffn_router_w, L1_ffn_router_b, L1_ffn_expert_w, L1_ffn_expert_b)
    return x

_drawn_inputs = setup_inputs


def setup_inputs(seed=0):
    import zlib

    import numpy as np

    out = dict(_drawn_inputs(seed))
    spreads = {'L0_ffn_ln_g': (1.0, 0.2),
     'L0_ffn_ln_b': (0.0, 0.8),
     'L0_ffn_b1': (0.0, 0.552),
     'L0_ffn_b2': (0.0, 0.1),
     'L1_ffn_router_b': (0.0, 0.482),
     'L1_ffn_expert_b': (0.0, 0.8)}
    factors = {'L1_attn_w_q': 8.0,
     'L1_attn_w_k': 8.0,
     'L1_attn_w_v': 8.0,
     'L1_attn_w_o': 8.0,
     'L1_ffn_router_w': 2.799,
     'L1_ffn_expert_w': 2.766}
    for name, (base, spread) in spreads.items():
        noise = np.random.default_rng([zlib.crc32(name.encode()), seed]).standard_normal(out[name].shape)
        drawn = base * np.exp(spread * noise) if base else spread * noise
        out[name] = jnp.asarray(drawn.astype(out[name].dtype))
    for name, factor in factors.items():
        out[name] = (out[name] * factor).astype(out[name].dtype)
    return out
```

```python
from contextlib import ExitStack

import concourse.bass as bass
from concourse import mybir

F32 = mybir.dt.float32
F32R = mybir.dt.float32r
BF16 = mybir.dt.bfloat16
U32 = mybir.dt.uint32
I32 = mybir.dt.int32
ALU = mybir.AluOpType
ACT = mybir.ActivationFunctionType
AX = mybir.AxisListType

P = 128
BANK = 512
EPS = 1e-5
MASKED = -1e30
LOWEST = -3e38

class Shared:

    def __init__(self, nc, ctx, tokens, width):
        self.tiles = tokens // P
        self.width = width
        self.x = ctx.enter_context(nc.sbuf_tensor("residual", [P, self.tiles, width], F32))
        self.ident = ctx.enter_context(nc.sbuf_tensor("ident", [P, P], F32))
        self.identb = ctx.enter_context(nc.sbuf_tensor("identb", [P, P], BF16))
        self.mask_qk = ctx.enter_context(nc.sbuf_tensor("mask_qk", [P, P], BF16))
        self.mask_kq = ctx.enter_context(nc.sbuf_tensor("mask_kq", [P, P], BF16))

def load_stage(nc, sh, x_dram):
    with nc.cleanup_on_exit(), ExitStack() as ctx:
        x_loaded = nc.alloc_semaphore("x_loaded")
        zeroed = nc.alloc_semaphore("zeroed")
        made = nc.alloc_semaphore("made")
        block = ctx.enter_context(nc.Block())

        @block.sync
        def _(sp):
            sp.dma_start(sh.x[:], x_dram.rearrange("b (t p) d -> p (b t) d", p=P)).then_inc(x_loaded, 16)
            sp.wait_ge(x_loaded, 16)

        @block.gpsimd
        def _(pool):
            for m in (sh.ident, sh.identb, sh.mask_qk, sh.mask_kq):
                pool.memset(m[:], 0.0).then_inc(zeroed, 1)
            pool.wait_ge(zeroed, 4)
            for m in (sh.ident, sh.identb):
                pool.affine_select(out=m[:], in_=m[:], compare_op=ALU.not_equal, fill=1.0, base=0,
                                   pattern=[[-1, P]], channel_multiplier=1).then_inc(made, 1)
            pool.affine_select(out=sh.mask_qk[:], in_=sh.mask_qk[:], compare_op=ALU.is_ge, fill=MASKED, base=0,
                               pattern=[[-1, P]], channel_multiplier=1).then_inc(made, 1)
            pool.affine_select(out=sh.mask_kq[:], in_=sh.mask_kq[:], compare_op=ALU.is_ge, fill=MASKED, base=0,
                               pattern=[[1, P]], channel_multiplier=-1).then_inc(made, 1)
            pool.wait_ge(made, 4)

def store_stage(nc, sh, out_dram):
    with nc.cleanup_on_exit(), ExitStack() as ctx:
        stored = nc.alloc_semaphore("out_stored")
        block = ctx.enter_context(nc.Block())

        @block.sync
        def _(sp):
            sp.dma_start(out_dram.rearrange("b (t p) d -> p (b t) d", p=P), sh.x[:]).then_inc(stored, 16)
            sp.wait_ge(stored, 16)

class Norm:

    def __init__(self, nc, ctx, tag, tiles):
        self.tiles = tiles
        self.stats = ctx.enter_context(nc.sbuf_tensor(f"{tag}_stats", [P, tiles, 6], F32))
        self.moments = ctx.enter_context(nc.sbuf_tensor(f"{tag}_moments", [P, tiles, 2], F32))
        self.var = ctx.enter_context(nc.sbuf_tensor(f"{tag}_var", [P, tiles], F32))
        self.std = ctx.enter_context(nc.sbuf_tensor(f"{tag}_std", [P, tiles], F32))
        self.rstd = ctx.enter_context(nc.sbuf_tensor(f"{tag}_rstd", [P, tiles], F32))
        self.stats_done = nc.alloc_semaphore(f"{tag}_stats_done")
        self.var_ready = nc.alloc_semaphore(f"{tag}_var_ready")
        self.std_ready = nc.alloc_semaphore(f"{tag}_std_ready")
        self.rstd_ready = nc.alloc_semaphore(f"{tag}_rstd_ready")

def norm_vector(dve, n, src):
    for t in range(n.tiles):
        dve.bn_stats(n.stats[:, t, :], src[:, t, :]).then_inc(n.stats_done, 1)
    for t in range(n.tiles):
        dve.wait_ge(n.stats_done, t + 1)
        dve.bn_aggr(n.moments[:, t, :], n.stats[:, t, :]).then_inc(n.stats_done, 1)
    dve.wait_ge(n.stats_done, 2 * n.tiles)
    dve.tensor_scalar(n.var[:], n.moments[:, :, 1], EPS, None, ALU.add).then_inc(n.var_ready, 1)
    dve.wait_ge(n.std_ready, 1)
    dve.reciprocal(n.rstd[:], n.std[:]).then_inc(n.rstd_ready, 1)
    dve.wait_ge(n.rstd_ready, 1)

def norm_scalar(act, n):
    act.wait_ge(n.var_ready, 1)
    act.activation(n.std[:], n.var[:], ACT.Sqrt).then_inc(n.std_ready, 1)

def standardize(dve, n, dst, src, ready):
    for t in range(n.tiles):
        dve.tensor_scalar(dst[:, t, :], src[:, t, :], n.moments[:, t, 0:1], n.rstd[:, t:t + 1],
                          ALU.subtract, ALU.mult).then_inc(ready, 1)

def turn_tensor(pe, sh, u, banks, tiles, u_ready, ut_psum, ut_ready):
    per = BANK // P
    for g in range(tiles // per):
        pe.wait_ge(u_ready, per * (g + 1))
        if g >= 2:
            pe.wait_ge(ut_ready, g - 1)
        for j in range(per):
            mm = pe.transpose(banks[g % 2][:, j * P:(j + 1) * P], u[:, per * g + j, :], sh.ident[:])
        mm.then_inc(ut_psum, 1)

def turn_scalar(act, ut, banks, tiles, ut_psum, ut_ready):
    for g in range(tiles * P // BANK):
        act.wait_ge(ut_psum, g + 1)
        act.activation(ut[:, g * BANK:(g + 1) * BANK], banks[g % 2][:], ACT.Copy).then_inc(ut_ready, 1)


def causal_steps(tiles, per):
    return [(qb, k, max(0, k - per * qb)) for qb in range(tiles // per) for k in range(per * qb + per)]

def head_order(steps, per, halves, prep, first, last):
    n = len(steps)
    blocks = steps[-1][0] + 1
    at = {}
    for qb in range(blocks):
        end = max(i for i, s in enumerate(steps) if s[0] == qb)
        carried = end + 1 == n
        if carried and first:
            continue
        begin = 0 if carried else end + 1
        at.setdefault(begin + 1, []).append(("fin", qb, -1 if carried else 0))
        for half in range(halves):
            at.setdefault(begin + 3 + half, []).append(("out", halves * qb + half, -1 if carried else 0))
    order, used, done, spent = [], 0, 0.0, 0.0
    widths = [per - s[2] for s in steps]
    for i in range(n):
        done += widths[i] / sum(widths[:n - 5])
        while used < len(prep) and not last and spent <= done * sum(p[2] for p in prep):
            order.append((prep[used][0], prep[used][1], 1))
            spent += prep[used][2]
            used += 1
        order.append(("pv", i, 0))
        if i + 2 < n:
            order.append(("qk", i + 2, 0))
        elif not last:
            order.append(("qk", i + 2 - n, 1))
        order += at.get(i, [])
    if last:
        order.append(("fin", blocks - 1, 0))
        order += [("out", halves * (blocks - 1) + half, 0) for half in range(halves)]
    return order

def known(h):
    return isinstance(h, int)


def heads_stage(nc, sh, wqk_dram, wv_dram, wo_dram, heads):
    T = sh.tiles
    DH = 64
    PER = BANK // P
    N = T * P
    STEPS = causal_steps(T, PER)
    NS = len(STEPS)
    BLOCKS = T // PER
    HALVES = 2
    HT = PER // HALVES
    CHUNKS = [(t, c) for t in range(T) for c in range(t // PER + 1)]
    NC = len(CHUNKS)
    USES = BLOCKS + 1
    VW = BANK // DH
    SCALE = float(DH) ** -0.5
    CONSTS = 13
    AHEAD = 4
    PREP = [("proj", 0, 4.0)]
    for b in range(BLOCKS):
        PREP += [("proj", b + 1, 2.6)] if b + 1 < BLOCKS else []
        PREP += [("max", m, 0.6) for m, (t, c) in enumerate(CHUNKS) if t // PER == b]
    PREP += [("rowmax", 0, 1.5), ("mrow", 0, 1.0)]
    with nc.cleanup_on_exit(), ExitStack() as ctx:
        sb = lambda name, shape, dt=F32: ctx.enter_context(nc.sbuf_tensor("a1_" + name, shape, dt))
        psum = lambda name, shape: ctx.enter_context(nc.psum_tensor("a1_" + name, shape, F32))
        sem = lambda name: nc.alloc_semaphore("a1_" + name)
        norm = Norm(nc, ctx, "a1n", T)
        u = sb("u", [P, T, P])
        ut = sb("ut", [P, N])
        w = [sb(f"w{i}", [P, 2 * DH]) for i in range(2)]
        wv = sb("wv", [P, heads * DH])
        v_all = sb("v_all", [P, T, heads * DH])
        wo = [sb(f"wo{i}", [DH + 1, P + 1]) for i in range(2)]
        q_hh = [sb(f"q_hh{i}", [P, N], F32R) for i in range(2)]
        q_lm = [sb(f"q_lm{i}", [P, N], F32R) for i in range(2)]
        k_lh = [sb(f"k_lh{i}", [P, N], F32R) for i in range(2)]
        k_h1 = [sb(f"k_h1{i}", [P, N], F32R) for i in range(2)]
        v = [sb(f"v{i}", [P, T, DH + 1]) for i in range(2)]
        part_max = sb("part_max", [P, T, T // PER])
        row_max = sb("row_max", [P, T])
        max_row = [sb(f"max_row{i}", [T, P], F32R) for i in range(2)]
        probs = [sb(f"probs{i}", [P, BANK]) for i in range(AHEAD)]
        block_out = [sb(f"block_out{i}", [DH + 1, BANK]) for i in range(2)]
        rden = sb("rden", [P, HT])
        s1 = [psum(f"s1_{i}", [P, BANK]) for i in range(2)]
        s2 = [psum(f"s2_{i}", [P, BANK]) for i in range(2)]
        o = [psum(f"o{i}", [P, BANK]) for i in range(2)]
        pj = psum("pj", [P, BANK])
        ob = psum("ob", [P, HT, BANK // HT])

        u_ready = sem("u_ready")
        ut_psum = sem("ut_psum")
        ut_ready = sem("ut_ready")
        consts = sem("consts")
        w_loaded = [sem(f"w_loaded{i}") for i in range(2)]
        wo_loaded = [sem(f"wo_loaded{i}") for i in range(2)]
        proj_ready = sem("proj_ready")
        proj_free = sem("proj_free")
        split_hi = sem("split_hi")
        kh_copied = [sem(f"kh_copied{c}") for c in range(BLOCKS)]
        qh_copied = [sem(f"qh_copied{c}") for c in range(BLOCKS)]
        wv_loaded = sem("wv_loaded")
        v_psum = sem("v_psum")
        v_out = sem("v_out")
        v_ready = sem("v_ready")
        s1_ready = sem("s1_ready")
        max_done = sem("max_done")
        m_ready = sem("m_ready")
        mrow_loaded = [sem(f"mrow_loaded{i}") for i in range(2)]
        s2_ready = sem("s2_ready")
        exp_done = sem("exp_done")
        pv_done = sem("pv_done")
        fin_done = sem("fin_done")
        out_ready = sem("out_ready")
        rden_done = sem("rden_done")
        out_free = sem("out_free")
        block = ctx.enter_context(nc.Block())

        def run(emit):
            for what, n, _ in PREP:
                emit(what, n, 0, 0)
            emit("qk", 0, 0, 0)
            emit("qk", 1, 0, 0)

            def head(h, par):
                for what, n, d in head_order(STEPS, PER, HALVES, PREP, known(h) and h == 0,
                                                 known(h) and h == heads - 1):
                    emit(what, n, h + d, (par + d) % 2)

            return head

        def loads(h, par):
            return 8 * (h - par) + 16

        @block.sync
        def _(sp):
            def weights(h, par):
                if not known(h) or h >= 2:
                    sp.wait_ge(proj_ready, USES * (h - 2) + BLOCKS)
                sp.dma_start(w[par][:], wqk_dram[bass.ds(h, 1)].rearrange("a p n -> (a p) n"))\
                  .then_inc(w_loaded[par], 16)

            def out_weights(h, par):
                if not known(h) or h >= 2:
                    sp.wait_ge(out_ready, BLOCKS * HALVES * (h - 1))
                sp.dma_start(wo[par][0:DH, 0:P], wo_dram[bass.ds(h, 1)].rearrange("a p n -> (a p) n"))\
                  .then_inc(wo_loaded[par], 16)

            def maxima(h, par):
                sp.wait_ge(proj_free, USES * (h + 1))
                sp.dma_start(q_lm[par][DH:DH + 1, :].bitcast(F32), max_row[par][:, :].bitcast(F32))\
                  .then_inc(mrow_loaded[par], 16)

            def copies(h, par):
                for c in range(BLOCKS):
                    cs = slice(c * BANK, (c + 1) * BANK)
                    sp.wait_ge(split_hi, BLOCKS * h + c + 1)
                    sp.dma_start(k_h1[par][0:DH, cs].bitcast(F32), k_lh[par][DH:P, cs].bitcast(F32))\
                      .then_inc(kh_copied[c], 16)
                    sp.dma_start(q_hh[par][DH:P, cs].bitcast(F32), q_hh[par][0:DH, cs].bitcast(F32))\
                      .then_inc(qh_copied[c], 16)

            def head(h, par):
                if not known(h) or h + 2 < heads:
                    weights(h + 2, par)
                if not known(h) or h + 1 < heads:
                    copies(h + 1, 1 - par)
                    out_weights(h + 1, 1 - par)
                    maxima(h + 1, 1 - par)

            sp.wait_ge(consts, CONSTS)
            weights(0, 0)
            weights(1, 1)
            sp.dma_start(wv[:], wv_dram).then_inc(wv_loaded, 16)
            out_weights(0, 0)
            copies(0, 0)
            maxima(0, 0)
            head(0, 0)
            with sp.Fori(0, heads // 2 - 2) as i:
                head(2 * i + 1, 1)
                head(2 * i + 2, 0)
            for h in range(heads - 3, heads):
                head(h, h % 2)

        @block.gpsimd
        def _(pool):
            count = 0
            for i in range(2):
                for part, value in ((q_lm[i][DH:P, :].bitcast(F32), 0.0), (k_h1[i][DH:P, :].bitcast(F32), 0.0),
                                    (k_h1[i][DH:DH + 1, :].bitcast(F32), -1.0), (v[i][:, :, DH:DH + 1], 1.0),
                                    (wo[i][:], 0.0), (wo[i][DH:DH + 1, P:P + 1], 1.0)):
                    pool.memset(part, value).then_inc(consts, 1)
                    count += 1
                    pool.wait_ge(consts, count)
            pool.memset(part_max[:], LOWEST).then_inc(consts, 1)

            def values(h, par):
                if not (known(h) and h < 2):
                    pool.wait_ge(pv_done, NS * (h - 1))
                pool.tensor_copy(v[par][:, :, 0:DH], v_all[:, :, bass.ds(h * DH, DH)]).then_inc(v_ready, 1)

            pool.wait_ge(v_out, T * heads // VW)
            values(0, 0)
            values(1, 1)
            with pool.Fori(1, heads // 2) as i:
                values(2 * i, 0)
                values(2 * i + 1, 1)

        @block.scalar
        def _(act):
            norm_scalar(act, norm)
            turn_scalar(act, ut, s1, T, ut_psum, ut_ready)
            for t in range(T):
                for g in range(heads // VW):
                    use = t * heads // VW + g
                    act.wait_ge(v_psum, use + 1)
                    act.activation(v_all[:, t, g * BANK:(g + 1) * BANK], s2[use % 2][:], ACT.Copy).then_inc(v_out, 1)

            def emit(what, n, h, par):
                if what == "qk":
                    width = BANK - P * STEPS[n][2]
                    act.wait_ge(s2_ready, NS * h + n + 1)
                    if n >= AHEAD or not (known(h) and h == 0):
                        act.wait_ge(pv_done, NS * h + n - AHEAD + 1)
                    act.activation(probs[n % AHEAD][:, 0:width], s2[n % 2][:, 0:width], ACT.Exp,
                                   scale=SCALE).then_inc(exp_done, 1)
                if what == "fin":
                    last = max(i for i, s in enumerate(STEPS) if s[0] == n)
                    act.wait_ge(pv_done, NS * h + last + 1)
                    if n >= 2 or not (known(h) and h == 0):
                        act.wait_ge(out_ready, HALVES * (BLOCKS * h + n - 1))
                    act.activation(block_out[n % 2][:], o[n % 2][0:DH + 1, :], ACT.Copy).then_inc(fin_done, 1)

            head = run(emit)
            head(0, 0)
            with act.Fori(0, heads // 2 - 1) as i:
                head(2 * i + 1, 1)
                head(2 * i + 2, 0)
            head(heads - 1, 1)

        @block.tensor
        def _(pe):
            turn_tensor(pe, sh, u, s1, T, u_ready, ut_psum, ut_ready)
            pe.wait_ge(ut_ready, T // PER)
            pe.wait_ge(consts, CONSTS)
            pe.wait_ge(wv_loaded, 16)
            for t in range(T):
                for g in range(heads // VW):
                    use = t * heads // VW + g
                    if use >= 2:
                        pe.wait_ge(v_out, use - 1)
                    pe.matmul(s2[use % 2][:], ut[:, t * P:(t + 1) * P], wv[:, g * BANK:(g + 1) * BANK],
                              start=True, stop=True).then_inc(v_psum, 1)
            pe.wait_ge(v_out, T * heads // VW)

            def emit(what, n, h, par):
                if what == "proj":
                    if n == 0:
                        pe.wait_ge(w_loaded[par], loads(h, par))
                    pe.wait_ge(proj_free, USES * h + n)
                    pe.matmul(pj[:], w[par][:, 0:2 * DH], ut[:, n * BANK:(n + 1) * BANK],
                              start=True, stop=True).then_inc(proj_ready, 1)
                if what == "max":
                    t, c = CHUNKS[n]
                    width = min(BANK, (t + 1) * P - c * BANK)
                    diag = c == t // PER
                    if t % PER == 0 and c == 0:
                        pe.wait_ge(kh_copied[t // PER], 16 * h + 16)
                    if n >= 2:
                        pe.wait_ge(max_done, NC * h + n - 1)
                    mm = pe.matmul(s1[n % 2][:, 0:width], q_hh[par][0:DH, t * P:(t + 1) * P],
                                   k_h1[par][0:DH, c * BANK:c * BANK + width], start=True, stop=not diag)
                    if diag:
                        mm = pe.matmul(s1[n % 2][:, width - P:width], sh.identb[:], sh.mask_qk[:],
                                       start=False, stop=True)
                    mm.then_inc(s1_ready, 1)
                if what == "mrow":
                    pe.wait_ge(m_ready, h + 1)
                    pe.wait_ge(proj_free, USES * h + USES - 1)
                    pe.transpose(pj[0:T, 0:P], row_max[:], sh.ident[:]).then_inc(proj_ready, 1)
                if what == "qk":
                    qb, k, r = STEPS[n]
                    qs = slice((PER * qb + r) * P, (qb + 1) * BANK)
                    ks = slice(k * P, (k + 1) * P)
                    width = BANK - P * r
                    diag = k >= PER * qb
                    if k == 0:
                        pe.wait_ge(qh_copied[qb], 16 * h + 16)
                    if n == 0:
                        pe.wait_ge(mrow_loaded[par], loads(h, par))
                    if n >= 2 or not (known(h) and h == 0):
                        pe.wait_ge(exp_done, NS * h + n - 1)
                    dst = s2[n % 2]
                    pe.matmul(dst[:, 0:width], k_lh[par][:, ks], q_hh[par][:, qs], start=True, stop=False)
                    mm = pe.matmul(dst[:, 0:width], k_h1[par][:, ks], q_lm[par][:, qs], start=False, stop=not diag)
                    if diag:
                        mm = pe.matmul(dst[:, 0:P], sh.identb[:], sh.mask_kq[:], start=False, stop=True)
                    mm.then_inc(s2_ready, 1)
                if what == "pv":
                    qb, k, r = STEPS[n]
                    if n == 0:
                        pe.wait_ge(v_ready, h + 1)
                    pe.wait_ge(exp_done, NS * h + n + 1)
                    if k == 0 and (qb >= 2 or not (known(h) and h == 0)):
                        pe.wait_ge(fin_done, BLOCKS * h + qb - 1)
                    pe.matmul(o[qb % 2][0:DH + 1, P * r:BANK], v[par][:, k, :], probs[n % AHEAD][:, 0:BANK - P * r],
                              start=(k == 0), stop=(k == PER * qb + PER - 1)).then_inc(pv_done, 1)
                if what == "out":
                    qb = n // HALVES
                    if n == 0:
                        pe.wait_ge(wo_loaded[par], loads(h, par))
                    pe.wait_ge(fin_done, BLOCKS * h + qb + 1)
                    pe.wait_ge(out_free, BLOCKS * HALVES * h + n)
                    for j in range(HT):
                        q = (n % HALVES) * HT + j
                        mm = pe.matmul(ob[:, j, 0:P + 1], block_out[qb % 2][:, q * P:(q + 1) * P], wo[par][:],
                                       start=True, stop=True)
                    mm.then_inc(out_ready, 1)

            head = run(emit)
            head(0, 0)
            with pe.Fori(0, heads // 2 - 1) as i:
                head(2 * i + 1, 1)
                head(2 * i + 2, 0)
            head(heads - 1, 1)

        @block.vector
        def _(dve):
            norm_vector(dve, norm, sh.x)
            standardize(dve, norm, u, sh.x, u_ready)
            dve.wait_ge(consts, CONSTS)

            def emit(what, n, h, par):
                if what == "proj":
                    cs = slice(n * BANK, (n + 1) * BANK)
                    if n == 0 and not (known(h) and h < 2):
                        dve.wait_ge(pv_done, NS * (h - 1))
                    dve.wait_ge(proj_ready, USES * h + n + 1)
                    dve.tensor_copy(q_hh[par][0:DH, cs], pj[0:DH, :])
                    dve.tensor_copy(k_lh[par][DH:P, cs], pj[DH:P, :]).then_inc(split_hi, 1)
                    dve.wait_ge(split_hi, BLOCKS * h + n + 1)
                    dve.tensor_tensor(q_lm[par][0:DH, cs], pj[0:DH, :], q_hh[par][0:DH, cs].bitcast(F32),
                                      ALU.subtract)
                    dve.tensor_tensor(k_lh[par][0:DH, cs], pj[DH:P, :], k_lh[par][DH:P, cs].bitcast(F32),
                                      ALU.subtract).then_inc(proj_free, 1)
                if what == "max":
                    t, c = CHUNKS[n]
                    width = min(BANK, (t + 1) * P - c * BANK)
                    dve.wait_ge(s1_ready, NC * h + n + 1)
                    dve.reduce_max(part_max[:, t, c:c + 1], s1[n % 2][:, 0:width], AX.X).then_inc(max_done, 1)
                if what == "rowmax":
                    dve.wait_ge(max_done, NC * (h + 1))
                    dve.tensor_reduce(row_max[:], part_max[:], AX.X, ALU.max).then_inc(m_ready, 1)
                if what == "mrow":
                    dve.wait_ge(proj_ready, USES * (h + 1))
                    dve.tensor_copy(max_row[par][:], pj[0:T, 0:P]).then_inc(proj_free, 1)
                if what == "out":
                    use = BLOCKS * HALVES * h + n
                    dve.wait_ge(out_ready, use + 1)
                    dve.reciprocal(rden[:], ob[:, :, P]).then_inc(rden_done, 1)
                    dve.wait_ge(rden_done, use + 1)
                    for j in range(HT):
                        t = n * HT + j
                        mm = dve.scalar_tensor_tensor(out=sh.x[:, t, :], in0=ob[:, j, 0:P], scalar=rden[:, j:j + 1],
                                                      in1=sh.x[:, t, :], op0=ALU.mult, op1=ALU.add)
                    mm.then_inc(out_free, 1)

            head = run(emit)
            head(0, 0)
            with dve.Fori(0, heads // 2 - 1) as i:
                head(2 * i + 1, 1)
                head(2 * i + 2, 0)
            head(heads - 1, 1)

def rotary_stage(nc, sh, w_dram, wv_dram, wo_dram, table_dram, heads):
    T = sh.tiles
    D = P
    PER = BANK // P
    N = T * P
    STEPS = causal_steps(T, PER)
    NS = len(STEPS)
    BLOCKS = T // PER
    HALVES = 2
    HT = PER // HALVES
    CHUNKS = [(t, c) for t in range(T) for c in range(t // PER + 1)]
    NC = len(CHUNKS)
    RW = BANK // 2
    RC = N // RW
    RB = BANK // RW
    SCALE = float(D) ** -0.5
    AHEAD = 4
    PREP = [("rotate", 0, 1.5), ("rotate", 1, 1.5)]
    for b in range(BLOCKS):
        PREP += [("rotate", RB * (b + 1) + r, 1.5) for r in range(RB)] if b + 1 < BLOCKS else []
        PREP += [("max", m, 0.6) for m, (t, c) in enumerate(CHUNKS) if t // PER == b]
    PREP += [("rowmax", 0, 1.0), ("mrow", 0, 1.0)]
    with nc.cleanup_on_exit(), ExitStack() as ctx:
        sb = lambda name, shape, dt=F32: ctx.enter_context(nc.sbuf_tensor("a0_" + name, shape, dt))
        psum = lambda name, shape: ctx.enter_context(nc.psum_tensor("a0_" + name, shape, F32))
        sem = lambda name: nc.alloc_semaphore("a0_" + name)
        norm = Norm(nc, ctx, "a0n", T)
        u = sb("u", [P, T, P])
        ut = sb("ut", [P, N])
        w = sb("w", [P, heads + 1, 2, D])
        wv = sb("wv", [P, D])
        wo = sb("wo", [P, heads, P])
        table = sb("table", [P, RC, 2, RW])
        hi = sb("hi", [P, heads + 1, N], F32R)
        lo = sb("lo", [P, heads + 1, N], F32R)
        product = [sb(f"product{i}", [P, 2, RW]) for i in range(2)]
        rotated = [sb(f"rotated{i}", [P, RW]) for i in range(2)]
        v = sb("v", [P, T, D])
        part_max = sb("part_max", [P, T, T // PER])
        row_max = sb("row_max", [P, T])
        turned_max = [sb(f"turned_max{i}", [T, P], F32R) for i in range(heads)]
        max_row = [sb(f"max_row{i}", [1, N], F32R) for i in range(heads)]
        minus_one = sb("minus_one", [1, P], F32R)
        one = sb("one", [P, 1])
        probs = [sb(f"probs{i}", [P, BANK]) for i in range(AHEAD)]
        prob_sum = [sb(f"prob_sum{i}", [P, BANK]) for i in range(2)]
        block_out = [sb(f"block_out{i}", [P, BANK]) for i in range(2)]
        rden = sb("rden", [P, HT])
        s1 = [psum(f"s1_{i}", [P, BANK]) for i in range(2)]
        s2 = [psum(f"s2_{i}", [P, BANK]) for i in range(2)]
        o = [psum(f"o{i}", [P, BANK]) for i in range(2)]
        pj = psum("pj", [P, 2, RW])
        ob = psum("ob", [P, HT, BANK // HT])

        u_ready = sem("u_ready")
        ut_psum = sem("ut_psum")
        ut_ready = sem("ut_ready")
        consts = sem("consts")
        w_loaded = sem("w_loaded")
        wv_loaded = sem("wv_loaded")
        wo_loaded = sem("wo_loaded")
        table_loaded = sem("table_loaded")
        v_psum = sem("v_psum")
        v_ready = sem("v_ready")
        pair_ready = sem("pair_ready")
        product_done = sem("product_done")
        rotated_done = sem("rotated_done")
        hi_ready = sem("hi_ready")
        lo_ready = sem("lo_ready")
        s1_ready = sem("s1_ready")
        max_done = sem("max_done")
        m_ready = sem("m_ready")
        turned_ready = sem("turned_ready")
        turned_out = sem("turned_out")
        mrow_loaded = [sem(f"mrow_loaded{i}") for i in range(heads)]
        s2_ready = sem("s2_ready")
        exp_done = sem("exp_done")
        summed = sem("summed")
        pv_done = sem("pv_done")
        fin_done = sem("fin_done")
        out_ready = sem("out_ready")
        rden_done = sem("rden_done")
        out_free = sem("out_free")
        block = ctx.enter_context(nc.Block())

        def run(emit):
            for n in range(RC):
                emit("rotate", n, -1)
            for what, n, _ in PREP:
                emit(what, n, 0)
            emit("qk", 0, 0)
            emit("qk", 1, 0)
            for h in range(heads):
                for what, n, d in head_order(STEPS, PER, HALVES, PREP, h == 0, h == heads - 1):
                    emit(what, n, h + d)

        last_of = lambda qb: max(i for i, s in enumerate(STEPS) if s[0] == qb)

        @block.sync
        def _(sp):
            sp.dma_start(w[:], w_dram).then_inc(w_loaded, 16)
            sp.dma_start(table[:], table_dram).then_inc(table_loaded, 16)
            sp.dma_start(wv[:], wv_dram).then_inc(wv_loaded, 16)
            sp.dma_start(wo[:], wo_dram).then_inc(wo_loaded, 16)
            for h in range(heads):
                sp.wait_ge(turned_out, h + 1)
                sp.dma_start(max_row[h][:].bitcast(F32), turned_max[h][:].bitcast(F32))\
                  .then_inc(mrow_loaded[h], 16)

        @block.gpsimd
        def _(pool):
            pool.memset(minus_one[:].bitcast(F32), -1.0).then_inc(consts, 1)
            pool.memset(one[:], 1.0).then_inc(consts, 1)
            pool.memset(part_max[:], LOWEST).then_inc(consts, 1)

            def emit(what, n, h):
                if what == "rotate":
                    use = RC * (h + 1) + n
                    ns = slice(n * RW, (n + 1) * RW)
                    pool.wait_ge(hi_ready, use + 1)
                    pool.tensor_tensor(lo[:, h + 1, ns], rotated[n % 2][:], hi[:, h + 1, ns].bitcast(F32),
                                       ALU.subtract).then_inc(lo_ready, 1)
                if what == "pv":
                    qb, k, r = STEPS[n]
                    block_no = BLOCKS * h + qb
                    pool.wait_ge(exp_done, NS * h + n + 1)
                    total = prob_sum[qb % 2]
                    if k == 0:
                        if block_no >= 2:
                            pool.wait_ge(out_ready, HALVES * (block_no - 1))
                        pool.tensor_copy(total[:], probs[n % AHEAD][:]).then_inc(summed, 1)
                    else:
                        pool.wait_ge(summed, NS * h + n)
                        pool.tensor_tensor(total[:, P * r:], total[:, P * r:], probs[n % AHEAD][:, 0:BANK - P * r],
                                           ALU.add).then_inc(summed, 1)

            run(emit)

        @block.scalar
        def _(act):
            norm_scalar(act, norm)
            turn_scalar(act, ut, s1, T, ut_psum, ut_ready)
            for g in range(BLOCKS):
                act.wait_ge(v_psum, g + 1)
                act.activation(v[:, PER * g:PER * g + PER, :].rearrange("p t d -> p (t d)"), s2[g % 2][:],
                               ACT.Copy).then_inc(v_ready, 1)

            def emit(what, n, h):
                if what == "rotate":
                    use = RC * (h + 1) + n
                    act.wait_ge(rotated_done, use + 1)
                    act.activation(hi[:, h + 1, n * RW:(n + 1) * RW], rotated[n % 2][:], ACT.Copy)\
                       .then_inc(hi_ready, 1)
                if what == "qk":
                    width = BANK - P * STEPS[n][2]
                    use = NS * h + n
                    act.wait_ge(s2_ready, use + 1)
                    if use >= AHEAD:
                        act.wait_ge(pv_done, use - AHEAD + 1)
                        act.wait_ge(summed, use - AHEAD + 1)
                    act.activation(probs[n % AHEAD][:, 0:width], s2[n % 2][:, 0:width], ACT.Exp,
                                   scale=SCALE).then_inc(exp_done, 1)
                if what == "fin":
                    block_no = BLOCKS * h + n
                    act.wait_ge(pv_done, NS * h + last_of(n) + 1)
                    if block_no >= 2:
                        act.wait_ge(out_ready, HALVES * (block_no - 1))
                    act.activation(block_out[n % 2][:], o[n % 2][:], ACT.Copy).then_inc(fin_done, 1)

            run(emit)

        @block.tensor
        def _(pe):
            turn_tensor(pe, sh, u, s1, T, u_ready, ut_psum, ut_ready)
            pe.wait_ge(ut_ready, T // PER)
            pe.wait_ge(wv_loaded, 16)
            for g in range(BLOCKS):
                if g >= 2:
                    pe.wait_ge(v_ready, g - 1)
                for j in range(PER):
                    t = PER * g + j
                    mm = pe.matmul(s2[g % 2][:, j * P:(j + 1) * P], ut[:, t * P:(t + 1) * P], wv[:],
                                   start=True, stop=True)
                mm.then_inc(v_psum, 1)
            pe.wait_ge(v_ready, BLOCKS)
            pe.wait_ge(w_loaded, 16)
            pe.wait_ge(consts, 3)

            def emit(what, n, h):
                if what == "rotate":
                    use = RC * (h + 1) + n
                    if use >= 1:
                        pe.wait_ge(product_done, use)
                    for s in range(2):
                        mm = pe.matmul(pj[:, s, :], w[:, h + 1, s, :], ut[:, n * RW:(n + 1) * RW],
                                       start=True, stop=True)
                    mm.then_inc(pair_ready, 1)
                if what == "max":
                    t, c = CHUNKS[n]
                    width = min(BANK, (t + 1) * P - c * BANK)
                    diag = c == t // PER
                    if t % PER == 0 and c == 0:
                        pe.wait_ge(hi_ready, RC * (h + 1) + RB * (t // PER + 1))
                    if NC * h + n >= 2:
                        pe.wait_ge(max_done, NC * h + n - 1)
                    mm = pe.matmul(s1[n % 2][:, 0:width], hi[:, h + 1, t * P:(t + 1) * P],
                                   hi[:, 0, c * BANK:c * BANK + width], start=True, stop=not diag)
                    if diag:
                        mm = pe.matmul(s1[n % 2][:, width - P:width], sh.identb[:], sh.mask_qk[:],
                                       start=False, stop=True)
                    mm.then_inc(s1_ready, 1)
                if what == "mrow":
                    pe.wait_ge(m_ready, h + 1)
                    pe.wait_ge(product_done, RC * (h + 2))
                    pe.transpose(pj[0:T, 0, 0:P], row_max[:], sh.ident[:]).then_inc(turned_ready, 1)
                if what == "qk":
                    qb, k, r = STEPS[n]
                    qs = slice((PER * qb + r) * P, (qb + 1) * BANK)
                    ks = slice(k * P, (k + 1) * P)
                    width = BANK - P * r
                    diag = k >= PER * qb
                    use = NS * h + n
                    if n == 0:
                        pe.wait_ge(mrow_loaded[h], 16)
                        pe.wait_ge(lo_ready, RC * (h + 2))
                    if use >= 2:
                        pe.wait_ge(exp_done, use - 1)
                    dst = s2[n % 2]
                    pe.matmul(dst[:, 0:width], hi[:, 0, ks], hi[:, h + 1, qs], start=True, stop=False)
                    pe.matmul(dst[:, 0:width], hi[:, 0, ks], lo[:, h + 1, qs], start=False, stop=False)
                    pe.matmul(dst[:, 0:width], lo[:, 0, ks], hi[:, h + 1, qs], start=False, stop=False)
                    mm = pe.matmul(dst[:, 0:width], minus_one[:], max_row[h][:, qs], start=False, stop=not diag)
                    if diag:
                        mm = pe.matmul(dst[:, 0:P], sh.identb[:], sh.mask_kq[:], start=False, stop=True)
                    mm.then_inc(s2_ready, 1)
                if what == "pv":
                    qb, k, r = STEPS[n]
                    pe.wait_ge(exp_done, NS * h + n + 1)
                    if k == 0 and BLOCKS * h + qb >= 2:
                        pe.wait_ge(fin_done, BLOCKS * h + qb - 1)
                    pe.matmul(o[qb % 2][:, P * r:BANK], v[:, k, :], probs[n % AHEAD][:, 0:BANK - P * r],
                              start=(k == 0), stop=(k == PER * qb + PER - 1)).then_inc(pv_done, 1)
                if what == "out":
                    qb = n // HALVES
                    use = BLOCKS * HALVES * h + n
                    if use == 0:
                        pe.wait_ge(wo_loaded, 16)
                    pe.wait_ge(fin_done, BLOCKS * h + qb + 1)
                    pe.wait_ge(summed, NS * h + last_of(qb) + 1)
                    if use >= 1:
                        pe.wait_ge(out_free, use)
                    for j in range(HT):
                        q = (n % HALVES) * HT + j
                        pe.matmul(ob[:, j, 0:P], block_out[qb % 2][:, q * P:(q + 1) * P], wo[:, h, :],
                                  start=True, stop=True)
                        mm = pe.matmul(ob[:, j, P:P + 1], prob_sum[qb % 2][:, q * P:(q + 1) * P], one[:],
                                       start=True, stop=True)
                    mm.then_inc(out_ready, 1)

            run(emit)

        @block.vector
        def _(dve):
            norm_vector(dve, norm, sh.x)
            standardize(dve, norm, u, sh.x, u_ready)
            dve.wait_ge(consts, 3)
            dve.wait_ge(table_loaded, 16)

            def emit(what, n, h):
                if what == "rotate":
                    use = RC * (h + 1) + n
                    dve.wait_ge(pair_ready, use + 1)
                    dve.tensor_tensor(product[n % 2][:], pj[:], table[:, n], ALU.mult).then_inc(product_done, 1)
                    if use >= 2:
                        dve.wait_ge(lo_ready, use - 1)
                    dve.wait_ge(product_done, use + 1)
                    dve.tensor_tensor(rotated[n % 2][:], product[n % 2][:, 0, :], product[n % 2][:, 1, :],
                                      ALU.add).then_inc(rotated_done, 1)
                if what == "max":
                    t, c = CHUNKS[n]
                    width = min(BANK, (t + 1) * P - c * BANK)
                    dve.wait_ge(s1_ready, NC * h + n + 1)
                    dve.reduce_max(part_max[:, t, c:c + 1], s1[n % 2][:, 0:width], AX.X).then_inc(max_done, 1)
                if what == "rowmax":
                    dve.wait_ge(max_done, NC * (h + 1))
                    dve.tensor_reduce(row_max[:], part_max[:], AX.X, ALU.max).then_inc(m_ready, 1)
                if what == "mrow":
                    dve.wait_ge(turned_ready, h + 1)
                    dve.tensor_copy(turned_max[h][:], pj[0:T, 0, 0:P]).then_inc(turned_out, 1)
                if what == "out":
                    use = BLOCKS * HALVES * h + n
                    dve.wait_ge(out_ready, use + 1)
                    dve.reciprocal(rden[:], ob[:, :, P]).then_inc(rden_done, 1)
                    dve.wait_ge(rden_done, use + 1)
                    for j in range(HT):
                        t = n * HT + j
                        mm = dve.scalar_tensor_tensor(out=sh.x[:, t, :], in0=ob[:, j, 0:P], scalar=rden[:, j:j + 1],
                                                      in1=sh.x[:, t, :], op0=ALU.mult, op1=ALU.add)
                    mm.then_inc(out_free, 1)

            run(emit)


def first_choice_stage(nc, sh, tag, router_dram, rbias_dram, we_dram, be_dram, experts):
    T = sh.tiles
    N = T * P
    E = experts
    PER = BANK // P
    BANKS = E * P // BANK
    with nc.cleanup_on_exit(), ExitStack() as ctx:
        sb = lambda name, shape, dt=F32: ctx.enter_context(nc.sbuf_tensor(f"{tag}_{name}", shape, dt))
        psum = lambda name, shape: ctx.enter_context(nc.psum_tensor(f"{tag}_{name}", shape, F32))
        sem = lambda name: nc.alloc_semaphore(f"{tag}_{name}")
        norm = Norm(nc, ctx, tag + "n", T)
        u = sb("u", [P, T, P])
        ut = sb("ut", [P, N])
        router = sb("router", [P, E])
        rbias = sb("rbias", [P, E])
        we = sb("we", [P, E * P])
        be = sb("be", [P, T, P])
        logits = sb("logits", [P, T, E])
        top = sb("top", [P, T])
        prob = sb("prob", [P, T, E])
        total = sb("total", [P, T])
        weight = sb("weight", [P, T])
        order = sb("order", [P, T, E])
        rank = sb("rank", [P, T, E])
        choice = sb("choice", [P, T, E])
        choice_t = sb("choice_t", [P, P])
        turn = [psum(f"turn{i}", [P, BANK]) for i in range(2)]
        y = [psum(f"y{i}", [P, E, P]) for i in range(2)]
        small = psum("small", [P, T, E])
        bias = psum("bias", [P, PER, P])

        loaded = sem("loaded")
        u_ready = sem("u_ready")
        ut_psum = sem("ut_psum")
        ut_ready = sem("ut_ready")
        consts = sem("consts")
        be_loaded = sem("be_loaded")
        logits_psum = sem("logits_psum")
        step = sem("step")
        shifted = sem("shifted")
        exp_done = sem("exp_done")
        choice_ready = sem("choice_ready")
        turned = sem("turned")
        turned_out = sem("turned_out")
        y_ready = sem("y_ready")
        y_used = sem("y_used")
        bias_ready = sem("bias_ready")
        bias_used = sem("bias_used")
        block = ctx.enter_context(nc.Block())

        @block.sync
        def _(sp):
            sp.dma_start(router[:], router_dram).then_inc(loaded, 16)
            sp.dma_start(rbias[:], rbias_dram.partition_broadcast(P)).then_inc(loaded, 16)
            sp.dma_start(we[:], we_dram).then_inc(loaded, 16)
            sp.wait_ge(consts, 1)
            for t in range(T):
                sp.dma_start(be[t * E:(t + 1) * E, t, :], be_dram).then_inc(be_loaded, 16)

        @block.gpsimd
        def _(pool):
            pool.memset(be[:], 0.0).then_inc(consts, 1)
            for e in range(E):
                pool.memset(order[:, :, e:e + 1], float(E - e)).then_inc(consts, 1)

        @block.scalar
        def _(act):
            norm_scalar(act, norm)
            turn_scalar(act, ut, turn, T, ut_psum, ut_ready)
            act.wait_ge(shifted, 1)
            act.activation(prob[:], logits[:], ACT.Exp).then_inc(exp_done, 1)

        @block.tensor
        def _(pe):
            turn_tensor(pe, sh, u, turn, T, u_ready, ut_psum, ut_ready)
            pe.wait_ge(ut_ready, T // PER)
            pe.wait_ge(loaded, 48)
            for t in range(T):
                mm = pe.matmul(small[:, t, :], ut[:, t * P:(t + 1) * P], router[:], start=True, stop=True)
            mm.then_inc(logits_psum, 1)

            def tile(t):
                if t >= 2:
                    pe.wait_ge(y_used, t - 1)
                for b in range(BANKS):
                    mm = pe.matmul(y[t % 2][:, b * PER:(b + 1) * PER, :].rearrange("p e o -> p (e o)"),
                                   ut[:, t * P:(t + 1) * P], we[:, b * BANK:(b + 1) * BANK], start=True, stop=True)
                mm.then_inc(y_ready, 1)

            tile(0)
            tile(1)
            pe.wait_ge(choice_ready, 1)
            pe.transpose(turn[0][:, 0:P], choice[:].rearrange("p t e -> p (t e)"), sh.ident[:]).then_inc(turned, 1)
            pe.wait_ge(turned_out, 1)
            pe.wait_ge(be_loaded, 16 * T)
            for g in range(T // PER):
                if g:
                    pe.wait_ge(bias_used, g)
                for j in range(PER):
                    mm = pe.matmul(bias[:, j, :], choice_t[:], be[:, PER * g + j, :], start=True, stop=True)
                mm.then_inc(bias_ready, 1)
                for t in range(PER * g, PER * g + PER):
                    if t >= 2:
                        tile(t)

        @block.vector
        def _(dve):
            norm_vector(dve, norm, sh.x)
            standardize(dve, norm, u, sh.x, u_ready)
            wide = lambda a: a[:].unsqueeze(2).broadcast_to([P, T, E])
            count = 0

            def then(instruction):
                nonlocal count
                instruction.then_inc(step, 1)
                count += 1
                dve.wait_ge(step, count)

            dve.wait_ge(loaded, 48)
            dve.wait_ge(logits_psum, 1)
            then(dve.tensor_tensor(logits[:], small[:], rbias[:].unsqueeze(1).broadcast_to([P, T, E]), ALU.add))
            then(dve.tensor_reduce(top[:], logits[:], AX.X, ALU.max))
            dve.tensor_tensor(logits[:], logits[:], wide(top), ALU.subtract).then_inc(shifted, 1)
            dve.wait_ge(exp_done, 1)
            dve.wait_ge(consts, 1 + E)
            then(dve.tensor_reduce(top[:], prob[:], AX.X, ALU.max))
            then(dve.tensor_reduce(total[:], prob[:], AX.X, ALU.add))
            then(dve.reciprocal(total[:], total[:]))
            then(dve.tensor_tensor(rank[:], prob[:], wide(top), ALU.is_equal))
            then(dve.tensor_tensor(rank[:], rank[:], order[:], ALU.mult))
            then(dve.scalar_tensor_tensor(out=weight[:], in0=top[:], scalar=0.5, in1=total[:], op0=ALU.mult,
                                          op1=ALU.mult))
            then(dve.tensor_reduce(top[:], rank[:], AX.X, ALU.max))
            then(dve.tensor_tensor(rank[:], rank[:], wide(top), ALU.is_equal))
            dve.tensor_tensor(choice[:], rank[:], wide(weight), ALU.mult).then_inc(choice_ready, 1)
            dve.wait_ge(turned, 1)
            dve.tensor_copy(choice_t[:], turn[0][:, 0:P]).then_inc(turned_out, 1)
            dve.wait_ge(choice_ready, 1)
            for t in range(T):
                if t % PER == 0:
                    g = t // PER
                    xs = sh.x[:, t:t + PER, :]
                    dve.wait_ge(bias_ready, g + 1)
                    dve.tensor_tensor(xs, bias[:], xs, ALU.add).then_inc(bias_used, 1)
                    dve.wait_ge(bias_used, g + 1)
                dve.wait_ge(y_ready, t + 1)
                for e in range(E):
                    add = dve.scalar_tensor_tensor(out=sh.x[:, t, :], in0=y[t % 2][:, e, :], scalar=choice[:, t, e:e + 1],
                                                   in1=sh.x[:, t, :], op0=ALU.mult, op1=ALU.add)
                    if e < E - 1:
                        then(add)
                add.then_inc(y_used, 1)


def balanced_stage(nc, sh, tag, cent_dram, g_dram, b_dram, w1_dram, b1_dram, w2_dram, b2_dram, experts, hidden):
    T = sh.tiles
    N = T * P
    E = experts
    C = N // E
    CT = C // P
    F = hidden // P
    RADIX = 16
    G = P // RADIX
    GT = N // G
    HALF = 1 << 16
    STEPS = [HALF // RADIX ** (i + 1) for i in range(4)]
    ROUNDS = 2 * len(STEPS)
    TAKEN = -1e5
    CHAIN = 3 * ROUNDS + 12
    with nc.cleanup_on_exit(), ExitStack() as ctx:
        sb = lambda name, shape, dt=F32: ctx.enter_context(nc.sbuf_tensor(f"{tag}_{name}", shape, dt))
        psum = lambda name, shape: ctx.enter_context(nc.psum_tensor(f"{tag}_{name}", shape, F32))
        sem = lambda name: nc.alloc_semaphore(f"{tag}_{name}")
        dram = lambda name, shape: nc.dram_tensor(f"{tag}_{name}", shape, F32, kind="Internal").ap()
        norm = Norm(nc, ctx, tag + "n", T)
        norm2 = Norm(nc, ctx, tag + "m", T)
        u = sb("u", [P, T, P])
        nrm = sb("nrm", [P, T, P])
        gain = sb("gain", [P, P])
        shift = sb("shift", [P, P])
        cent = sb("cent", [P, E])
        nt = sb("nt", [P, N])
        score = sb("score", [P, E, T])
        flip = sb("flip", [P, E * T], I32)
        key = sb("key", [P, E * T], I32)
        part = sb("part", [P, 2, E * T], I32)
        half = sb("half", [P, 2, E * T])
        half_t = sb("half_t", [P, 2, P])
        keys = sb("keys", [P, 2, E, GT])
        taken = sb("taken", [P, GT])
        high = sb("high", [P, GT])
        both = sb("both", [P, GT])
        junk = sb("junk", [P, GT])
        cnt = [sb(f"cnt{i}", [P, 1], BF16) for i in range(2)]
        reach = sb("reach", [P, RADIX])
        reached = sb("reached", [P, 1])
        cand = sb("cand", [P, 2])
        cand0 = sb("cand0", [P, 2])
        move = sb("move", [P, ROUNDS])
        rest = sb("rest", [P, 1])
        lane = sb("lane", [P, 1], I32)
        lane_f = sb("lane_f", [P, 1])
        group_i = sb("group_i", [P, 1], I32)
        group = sb("group", [P, 1])
        iota_i = sb("iota_i", [P, P], I32)
        iota_f = sb("iota_f", [P, P])
        pick = sb("pick", [P, RADIX], BF16)
        before = sb("before", [P, P], BF16)
        every = sb("every", [P, P], BF16)
        first_slot = sb("first_slot", [P, E])
        above = sb("above", [P, GT])
        equal = sb("equal", [P, GT])
        tied = sb("tied", [P, 2], BF16)
        equal_sum = sb("equal_sum", [P, GT])
        ones = sb("ones", [P, GT])
        ranks = sb("ranks", [P, 4])
        free = sb("free", [P, 1])
        room = sb("room", [P, 1])
        chosen = sb("chosen", [P, GT])
        chosen_sum = sb("chosen_sum", [P, GT])
        base = sb("base", [P, 1])
        slot_part = sb("slot_part", [P, GT])
        slots = sb("slots", [P, GT])
        slot = sb("slot", [P, T], U32)
        routed = sb("routed", [P, T, P])
        w1 = [sb(f"w1_{i}", [P, hidden]) for i in range(2)]
        w2 = [sb(f"w2_{i}", [P, F, P]) for i in range(2)]
        b1 = sb("b1", [P, E, F])
        b2 = sb("b2", [P, E, P])
        hid = [sb(f"hid{i}", [P, F, C]) for i in range(2)]
        y = sb("y", [P, T, P])
        back = sb("back", [P, T, P])
        turn = [psum(f"turn{i}", [P, BANK]) for i in range(2)]
        counts = psum("counts", [P, BANK])
        hp = [psum(f"hp{i}", [P, C]) for i in range(2)]
        yp = psum("yp", [P, CT, P])
        keys_dram = dram("keys_dram", (2, E * T, P))
        routed_dram = dram("routed_dram", (N, P))
        y_dram = dram("y_dram", (N, P))

        loaded = sem("loaded")
        biases = sem("biases")
        u_ready = sem("u_ready")
        std2 = sem("std2")
        gained = sem("gained")
        nrm_ready = sem("nrm_ready")
        nt_psum = sem("nt_psum")
        nt_ready = sem("nt_ready")
        scored = sem("scored")
        prep = sem("prep")
        key_ready = sem("key_ready")
        key_psum = sem("key_psum")
        key_out = sem("key_out")
        key_stored = sem("key_stored")
        key_loaded = sem("key_loaded")
        consts = sem("consts")
        shapes = sem("shapes")
        chain = sem("chain")
        cnt_ready = sem("cnt_ready")
        counts_ready = sem("counts_ready")
        tied_ready = sem("tied_ready")
        ranks_ready = sem("ranks_ready")
        chosen_ready = sem("chosen_ready")
        slot_step = sem("slot_step")
        slot_psum = sem("slot_psum")
        slot_ready = sem("slot_ready")
        scattered = sem("scattered")
        routed_loaded = sem("routed_loaded")
        rt_psum = sem("rt_psum")
        rt_ready = sem("rt_ready")
        w_loaded = [sem(f"w_loaded{i}") for i in range(2)]
        h_psum = sem("h_psum")
        h_ready = sem("h_ready")
        y_psum = sem("y_psum")
        y_ready = sem("y_ready")
        y_stored = sem("y_stored")
        gathered = sem("gathered")
        half_added = sem("half_added")
        block = ctx.enter_context(nc.Block())

        @block.sync
        def _(sp):
            sp.dma_start(gain[:], g_dram.partition_broadcast(P)).then_inc(loaded, 16)
            sp.dma_start(shift[:], b_dram.partition_broadcast(P)).then_inc(loaded, 16)
            sp.dma_start(cent[:], cent_dram).then_inc(loaded, 16)
            sp.dma_start(b1[:], b1_dram).then_inc(biases, 16)
            sp.dma_start(b2[:].rearrange("p e d -> p (e d)"), b2_dram.partition_broadcast(P)).then_inc(biases, 16)

            def weights(e, par):
                sp.dma_start(w1[par][:], w1_dram[bass.ds(e, 1)].rearrange("a p f -> (a p) f"))\
                  .then_inc(w_loaded[par], 16)
                sp.dma_start(w2[par][:], w2_dram[bass.ds(e, 1)].rearrange("a (c p) d -> (a p) c d", p=P))\
                  .then_inc(w_loaded[par], 16)

            weights(0, 0)
            weights(1, 1)
            sp.wait_ge(key_out, 1)
            sp.dma_start(keys_dram.rearrange("h r p -> r h p"), half_t[:]).then_inc(key_stored, 16)
            sp.wait_ge(key_stored, 16)
            for g in range(G):
                src = keys_dram.rearrange("h (e t) p -> h e (t p)", e=E)[:, :, g * GT:(g + 1) * GT]
                sp.dma_start(keys[g * RADIX:(g + 1) * RADIX], src.partition_broadcast(RADIX)).then_inc(key_loaded, 16)
            sp.wait_ge(scattered, 16 * T)
            sp.dma_start(routed[:], routed_dram.rearrange("(t p) d -> p t d", p=P)).then_inc(routed_loaded, 16)
            with sp.Fori(0, E // 2 - 1) as i:
                for par in range(2):
                    e = 2 * i + par
                    sp.wait_ge(y_psum, e + 1)
                    weights(e + 2, par)
            for c in range(2):
                ts = slice(c * T // 2, (c + 1) * T // 2)
                sp.wait_ge(y_ready, (c + 1) * E // 2)
                sp.dma_start(y_dram.rearrange("(t p) d -> p t d", p=P)[:, ts], y[:, ts]).then_inc(y_stored, 16)

        @block.gpsimd
        def _(pool):
            pool.iota(lane[:], pattern=[[0, 1]], base=0, channel_multiplier=1).then_inc(consts, 1)
            pool.iota(iota_i[:], pattern=[[1, P]], base=0, channel_multiplier=0).then_inc(consts, 1)
            pool.memset(every[:], 1.0 / RADIX).then_inc(consts, 1)
            pool.memset(before[:], 1.0 / RADIX).then_inc(consts, 1)
            for e in range(E):
                pool.memset(first_slot[:, e:e + 1], float(e * C - 1)).then_inc(consts, 1)
            pool.memset(ones[:], 1.0).then_inc(consts, 1)
            pool.memset(taken[:], 0.0).then_inc(consts, 1)
            pool.memset(slots[:], 0.0).then_inc(slot_step, 1)
            pool.wait_ge(consts, 6 + E)
            blocks = before[:].rearrange("p (b r) -> p b r", r=RADIX)
            pool.affine_select(out=blocks, in_=blocks, compare_op=ALU.is_gt, fill=0.0, base=0,
                               pattern=[[RADIX, G], [0, RADIX]], channel_multiplier=-1).then_inc(consts, 1)

            pool.wait_ge(slot_step, 1)
            with pool.Fori(0, E) as e:
                pool.wait_ge(chosen_ready, e + 1)
                pool.tensor_tensor(slot_part[:], chosen_sum[:], base[:].broadcast_to([P, GT]), ALU.add).then_inc(slot_step, 1)
                pool.wait_ge(slot_step, 3 * e + 2)
                pool.tensor_tensor(slot_part[:], slot_part[:], chosen[:], ALU.mult).then_inc(slot_step, 1)
                pool.wait_ge(slot_step, 3 * e + 3)
                pool.tensor_tensor(slots[:], slots[:], slot_part[:], ALU.add).then_inc(slot_step, 1)
                pool.wait_ge(slot_step, 3 * e + 4)
            pool.wait_ge(slot_ready, 1)
            for t in range(T):
                pool.indirect_dma_start(out=routed_dram, out_offset=bass.IndirectOffsetOnAxis(ap=slot[:, t:t + 1], axis=0),
                                        in_=nrm[:, t, :], in_offset=None).then_inc(scattered, 16)
            pool.wait_ge(scattered, 16 * T)
            pool.wait_ge(y_stored, 32)
            for t in range(T):
                pool.indirect_dma_start(out=back[:, t, :], out_offset=None, in_=y_dram,
                                        in_offset=bass.IndirectOffsetOnAxis(ap=slot[:, t:t + 1], axis=0)).then_inc(gathered, 16)

        @block.scalar
        def _(act):
            norm_scalar(act, norm)
            norm_scalar(act, norm2)
            turn_scalar(act, nt, turn, T, nt_psum, nt_ready)
            act.wait_ge(key_psum, 1)
            act.activation(half_t[:].rearrange("p h q -> p (h q)"), turn[0][:, 0:2 * P], ACT.Copy).then_inc(key_out, 1)
            act.wait_ge(scored, 1)
            turn_scalar(act, nt, turn, T, rt_psum, rt_ready)
            act.wait_ge(biases, 32)

            def expert(e, par):
                for c in range(F):
                    act.wait_ge(h_psum, F * e + c + 1)
                    if not (known(e) and e < 2) and c == 0:
                        act.wait_ge(y_psum, e - 1)
                    act.activation(hid[par][:, c, :], hp[c % 2][:], ACT.Gelu_apprx_tanh,
                                   bias=b1[:, bass.ds(e, 1), c:c + 1].rearrange("p a b -> p (a b)")).then_inc(h_ready, 1)

            expert(0, 0)
            expert(1, 1)
            with act.Fori(1, E // 2) as i:
                expert(2 * i, 0)
                expert(2 * i + 1, 1)

        @block.tensor
        def _(pe):
            turn_tensor(pe, sh, nrm, turn, T, nrm_ready, nt_psum, nt_ready)
            pe.wait_ge(nt_ready, T * P // BANK)
            pe.wait_ge(loaded, 48)
            for t in range(T):
                mm = pe.matmul(counts[:, t * E:(t + 1) * E], nt[:, t * P:(t + 1) * P], cent[:], start=True, stop=True)
            mm.then_inc(scored, 1)
            pe.wait_ge(key_ready, 1)
            for h in range(2):
                mm = pe.transpose(turn[0][:, h * P:(h + 1) * P], half[:, h, :], sh.ident[:])
            mm.then_inc(key_psum, 1)
            with pe.Fori(0, E) as e:
                for r in range(ROUNDS):
                    pe.wait_ge(cnt_ready, ROUNDS * e + r + 1)
                    pe.matmul(counts[:, 0:RADIX], cnt[r % 2][:].broadcast_to([P, P]), pick[:], start=True, stop=True)\
                      .then_inc(counts_ready, 1)
                pe.wait_ge(tied_ready, e + 1)
                pe.matmul(counts[:, 0:2], before[:], tied[:], start=True, stop=True)
                pe.matmul(counts[:, 2:4], every[:], tied[:], start=True, stop=True).then_inc(ranks_ready, 1)
            pe.wait_ge(slot_step, 3 * E + 1)
            for h in range(2):
                mm = pe.transpose(turn[0][:, h * P:(h + 1) * P], slots[:, h * P:(h + 1) * P], sh.ident[:])
            mm.then_inc(slot_psum, 1)
            pe.wait_ge(slot_ready, 1)
            pe.wait_ge(routed_loaded, 16)
            for g in range(N // BANK):
                if g >= 2:
                    pe.wait_ge(rt_ready, g - 1)
                for j in range(BANK // P):
                    mm = pe.transpose(turn[g % 2][:, j * P:(j + 1) * P], routed[:, BANK // P * g + j, :], sh.ident[:])
                mm.then_inc(rt_psum, 1)
            pe.wait_ge(rt_ready, N // BANK)

            def expert(e, par):
                pe.wait_ge(w_loaded[par], 16 * (e - par) + 32)
                for c in range(F):
                    if not (known(e) and e == 0 and c < 2):
                        pe.wait_ge(h_ready, F * e + c - 1)
                    pe.matmul(hp[c % 2][:], w1[par][:, c * P:(c + 1) * P], nt[:, bass.ds(e * C, C)], start=True,
                              stop=True).then_inc(h_psum, 1)
                if not (known(e) and e == 0):
                    pe.wait_ge(y_ready, e)
                pe.wait_ge(h_ready, F * e + F)
                for s in range(CT):
                    for c in range(F):
                        mm = pe.matmul(yp[:, s, :], hid[par][:, c, s * P:(s + 1) * P], w2[par][:, c, :],
                                       start=(c == 0), stop=(c == F - 1))
                mm.then_inc(y_psum, 1)

            expert(0, 0)
            expert(1, 1)
            with pe.Fori(1, E // 2) as i:
                expert(2 * i, 0)
                expert(2 * i + 1, 1)

        @block.vector
        def _(dve):
            wide = lambda a: a[:].unsqueeze(1).broadcast_to([P, T, P])
            norm_vector(dve, norm, sh.x)
            standardize(dve, norm, u, sh.x, u_ready)
            dve.wait_ge(u_ready, T)
            norm_vector(dve, norm2, u)
            standardize(dve, norm2, nrm, u, std2)
            dve.wait_ge(loaded, 48)
            PER = BANK // P
            for g in range(T // PER):
                ts = slice(PER * g, PER * g + PER)
                dve.wait_ge(std2, PER * (g + 1))
                dve.tensor_tensor(nrm[:, ts], nrm[:, ts], gain[:].unsqueeze(1).broadcast_to([P, PER, P]), ALU.mult)\
                   .then_inc(gained, 1)
                dve.wait_ge(gained, g + 1)
                dve.tensor_tensor(nrm[:, ts], nrm[:, ts], shift[:].unsqueeze(1).broadcast_to([P, PER, P]), ALU.add)\
                   .then_inc(nrm_ready, PER)
            dve.scalar_tensor_tensor(out=sh.x[:], in0=u[:], scalar=0.5, in1=sh.x[:], op0=ALU.mult, op1=ALU.add)\
               .then_inc(half_added, 1)

            count = 0

            def made(instruction):
                nonlocal count
                instruction.then_inc(shapes, 1)
                count += 1
                dve.wait_ge(shapes, count)

            dve.wait_ge(consts, 7 + E)
            made(dve.tensor_single_scalar(group_i[:], lane[:], 4, ALU.arith_shift_right))
            made(dve.tensor_copy(group[:], group_i[:]))
            made(dve.tensor_single_scalar(group_i[:], lane[:], RADIX - 1, ALU.bitwise_and))
            made(dve.tensor_copy(lane_f[:], group_i[:]))
            made(dve.tensor_copy(iota_f[:], iota_i[:]))
            made(dve.tensor_scalar(pick[:], iota_f[:, 0:RADIX], lane_f[:, 0:1], None, ALU.is_equal))
            for i in range(2):
                scale = 1.0 / HALF if i else 1.0
                made(dve.tensor_scalar(cand0[:, i:i + 1], lane_f[:], STEPS[0] * scale, 0.0 if i else -HALF / 2,
                                       ALU.mult, ALU.add))
                for s, step in enumerate(STEPS):
                    following = STEPS[s + 1] if s + 1 < len(STEPS) else 0
                    made(dve.tensor_scalar(move[:, 4 * i + s:4 * i + s + 1], lane_f[:], (following - step) * scale,
                                           -step * scale, ALU.mult, ALU.add))

            count = 0

            def then(instruction):
                nonlocal count
                instruction.then_inc(prep, 1)
                count += 1
                dve.wait_ge(prep, count)

            dve.wait_ge(scored, 1)
            then(dve.tensor_copy(score[:].rearrange("p e t -> p t e"),
                                 counts[:, 0:T * E].rearrange("p (t e) -> p t e", e=E)))
            bits = score[:].rearrange("p e t -> p (e t)").bitcast(I32)
            then(dve.tensor_scalar(flip[:], bits, 31, 0x7FFFFFFF, ALU.arith_shift_right, ALU.bitwise_and))
            then(dve.tensor_tensor(key[:], bits, flip[:], ALU.bitwise_xor))
            then(dve.tensor_single_scalar(part[:, 0, :], key[:], 16, ALU.arith_shift_right))
            then(dve.tensor_single_scalar(part[:, 1, :], key[:], HALF - 1, ALU.bitwise_and))
            then(dve.tensor_copy(half[:, 0, :], part[:, 0, :]))
            then(dve.tensor_copy(half[:, 1, :], part[:, 1, :]))
            dve.tensor_scalar(half[:, 1, :], half[:, 1, :], 1.0 / HALF, None, ALU.mult).then_inc(key_ready, 1)
            dve.wait_ge(key_loaded, 16 * G)

            with dve.Fori(0, E) as e:
                done = 0

                def then(instruction):
                    nonlocal done
                    instruction.then_inc(chain, 1)
                    done += 1
                    dve.wait_ge(chain, CHAIN * e + done)

                key_of = lambda h: keys[:, h, bass.ds(e, 1), :].rearrange("p a t -> p (a t)")
                then(dve.tensor_tensor(high[:], key_of(0), taken[:], ALU.add))
                for i in range(2):
                    if i:
                        then(dve.scalar_tensor_tensor(out=both[:], in0=high[:], scalar=cand[:, 0:1], in1=key_of(1),
                                                      op0=ALU.subtract, op1=ALU.add))
                    for s, step in enumerate(STEPS):
                        r = len(STEPS) * i + s
                        now = cand0[:, i:i + 1] if s == 0 else cand[:, i:i + 1]
                        dve.tensor_scalar(junk[:], (both if i else high)[:], now, 0.0, ALU.is_ge, ALU.add,
                                          accum_out=cnt[r % 2][:]).then_inc(cnt_ready, 1)
                        then(dve.tensor_tensor(rest[:], now, move[:, r:r + 1], ALU.add))
                        dve.wait_ge(counts_ready, ROUNDS * e + r + 1)
                        then(dve.tensor_scalar(reach[:], counts[:, 0:RADIX], float(C), 0.0, ALU.is_ge, ALU.add,
                                               accum_out=reached[:]))
                        then(dve.scalar_tensor_tensor(out=cand[:, i:i + 1], in0=reached[:],
                                                      scalar=step / HALF if i else float(step), in1=rest[:],
                                                      op0=ALU.mult, op1=ALU.add))
                then(dve.tensor_scalar(above[:], both[:], cand[:, 1:2], 0.0, ALU.is_gt, ALU.add,
                                       accum_out=tied[:, 0:1]))
                dve.tensor_scalar(equal[:], both[:], cand[:, 1:2], 0.0, ALU.is_equal, ALU.add,
                                  accum_out=tied[:, 1:2]).then_inc(tied_ready, 1)
                dve.wait_ge(tied_ready, e + 1)
                then(dve.tensor_tensor_scan(equal_sum[:], ones[:], equal[:], 0.0, ALU.mult, ALU.add))
                dve.wait_ge(ranks_ready, e + 1)
                then(dve.tensor_copy(ranks[:], counts[:, 0:4]))
                then(dve.tensor_scalar(room[:], ranks[:, 2:3], -1.0, float(C), ALU.mult, ALU.add))
                then(dve.tensor_tensor(free[:], room[:], ranks[:, 1:2], ALU.subtract))
                then(dve.scalar_tensor_tensor(out=equal[:], in0=equal_sum[:], scalar=free[:, 0:1], in1=equal[:],
                                              op0=ALU.is_le, op1=ALU.mult))
                dve.wait_ge(slot_step, 3 * e + 1)
                then(dve.tensor_tensor(chosen[:], above[:], equal[:], ALU.add))
                then(dve.scalar_tensor_tensor(out=taken[:], in0=chosen[:], scalar=TAKEN, in1=taken[:],
                                              op0=ALU.mult, op1=ALU.add))
                then(dve.tensor_tensor_scan(chosen_sum[:], ones[:], chosen[:], 0.0, ALU.mult, ALU.add))
                then(dve.scalar_tensor_tensor(out=base[:], in0=ranks[:, 1:2], scalar=room[:, 0:1], in1=ranks[:, 0:1],
                                              op0=ALU.min, op1=ALU.add))
                dve.tensor_tensor(base[:], base[:], first_slot[:, bass.ds(e, 1)], ALU.add).then_inc(chosen_ready, 1)
                dve.wait_ge(chosen_ready, e + 1)
                assert done == CHAIN

            dve.wait_ge(slot_psum, 1)
            dve.tensor_copy(slot[:].rearrange("p (g h) -> p h g", h=GT // P),
                            turn[0][:, 0:GT].rearrange("p (h g j) -> p h g j", h=GT // P, j=RADIX)[:, :, :, 0])\
               .then_inc(slot_ready, 1)

            dve.wait_ge(biases, 32)
            with dve.Fori(0, E) as e:
                dve.wait_ge(y_psum, e + 1)
                dve.tensor_tensor(y[:, bass.ds(e * CT, CT), :], yp[:], b2[:, bass.ds(e, 1), :].broadcast_to([P, CT, P]),
                                  ALU.add).then_inc(y_ready, 1)
            dve.wait_ge(half_added, 1)
            dve.wait_ge(gathered, 16 * T)
            dve.scalar_tensor_tensor(out=sh.x[:], in0=back[:], scalar=0.5, in1=sh.x[:], op0=ALU.mult, op1=ALU.add)\
               .then_inc(half_added, 1)

def rotary_table(tokens, width, chunk):
    import numpy as np
    positions = np.arange(0, width, 2, dtype=np.float64)
    theta = np.power(10000.0, -2.0 * positions / width).astype(np.float32)
    angles = (np.arange(tokens, dtype=np.float32)[:, None] * theta[None, :]).astype(np.float32)
    cos = np.repeat(np.cos(angles).astype(np.float32).T, 2, axis=0)
    sin = np.repeat(np.sin(angles).astype(np.float32).T, 2, axis=0)
    sin[0::2] = -sin[0::2]
    both = np.stack([cos.reshape(width, -1, chunk), sin.reshape(width, -1, chunk)], axis=2)
    return np.ascontiguousarray(both)


def build(nc, x, cent, ln_g, ln_b, w1, b1, w2, b2, rot_w, rot_wv, rot_wo, rot_table, wqk, wv, wo, router, rbias, we, be,
          out):
    tokens, width = x.shape[1], x.shape[2]
    experts, _, hidden = w1.shape
    with ExitStack() as ctx:
        sh = Shared(nc, ctx, tokens, width)
        load_stage(nc, sh, x)
        balanced_stage(nc, sh, "f0a", cent, ln_g, ln_b, w1, b1, w2, b2, experts, hidden)
        rotary_stage(nc, sh, rot_w, rot_wv, rot_wo, rot_table, rot_wo.shape[1])
        balanced_stage(nc, sh, "f0b", cent, ln_g, ln_b, w1, b1, w2, b2, experts, hidden)
        first_choice_stage(nc, sh, "f1a", router, rbias, we, be, router.shape[1])
        heads_stage(nc, sh, wqk, wv, wo, wqk.shape[0])
        first_choice_stage(nc, sh, "f1b", router, rbias, we, be, router.shape[1])
        store_stage(nc, sh, out)

def kernel(L0_attn_x, L0_attn_Wq, L0_attn_Wk, L0_attn_Wv, L0_attn_Wo, L0_ffn_centroids, L0_ffn_ln_g, L0_ffn_ln_b,
           L0_ffn_w1, L0_ffn_b1, L0_ffn_w2, L0_ffn_b2, L1_attn_w_q, L1_attn_w_k, L1_attn_w_v, L1_attn_w_o,
           L1_ffn_router_w, L1_ffn_router_b, L1_ffn_expert_w, L1_ffn_expert_b):
    import numpy as np
    import concourse.bacc as _bacc
    from concourse.bass_utils import run_bass_kernel_spmd as _run

    x = np.asarray(L0_attn_x)
    _, tokens, width = x.shape
    experts, _, hidden = L0_ffn_w1.shape
    heads, dh, _ = L1_attn_w_q.shape
    rot_heads = L0_attn_Wq.shape[0]
    plain = np.concatenate([np.asarray(L0_attn_Wk)[None], np.asarray(L0_attn_Wq)])
    swapped = plain.reshape(-1, width // 2, 2, width)[:, :, ::-1].reshape(plain.shape)
    arrays = {
        "x": x,
        "cent": np.asarray(L0_ffn_centroids).T,
        "ln_g": np.asarray(L0_ffn_ln_g),
        "ln_b": np.asarray(L0_ffn_ln_b),
        "w1": np.asarray(L0_ffn_w1),
        "b1": np.asarray(L0_ffn_b1).reshape(experts, hidden // P, P).transpose(2, 0, 1),
        "w2": np.asarray(L0_ffn_w2),
        "b2": np.asarray(L0_ffn_b2).reshape(-1),
        "rot_w": np.stack([plain, swapped], axis=1).transpose(3, 0, 1, 2),
        "rot_wv": np.asarray(L0_attn_Wv).T,
        "rot_wo": np.asarray(L0_attn_Wo).reshape(width, rot_heads, width).transpose(2, 1, 0),
        "rot_table": rotary_table(tokens, width, 256),
        "wqk": np.concatenate([np.asarray(L1_attn_w_q), np.asarray(L1_attn_w_k)], axis=1).transpose(0, 2, 1),
        "wv": np.asarray(L1_attn_w_v).reshape(heads * dh, width).T,
        "wo": np.asarray(L1_attn_w_o).T.reshape(heads, dh, width),
        "router": np.asarray(L1_ffn_router_w).T,
        "rbias": np.asarray(L1_ffn_router_b),
        "we": np.asarray(L1_ffn_expert_w).transpose(2, 0, 1).reshape(width, -1),
        "be": np.asarray(L1_ffn_expert_b),
    }
    nc = _bacc.Bacc("TRN2", target_bir_lowering=False, num_devices=1)
    arrays = {name: np.ascontiguousarray(a) for name, a in arrays.items()}
    args = [nc.dram_tensor(name, a.shape, mybir.dt.from_np(a.dtype), kind="ExternalInput").ap()
            for name, a in arrays.items()]
    out = nc.dram_tensor("out", x.shape, F32, kind="ExternalOutput").ap()
    build(nc, *args, out)
    result = _run(nc, [arrays], core_ids=[0])
    return result.results[0]["out"]
```

```python
from contextlib import ExitStack

import concourse.bass as bass
from concourse import mybir

F32 = mybir.dt.float32
F32R = mybir.dt.float32r
BF16 = mybir.dt.bfloat16
U32 = mybir.dt.uint32
I32 = mybir.dt.int32
ALU = mybir.AluOpType
ACT = mybir.ActivationFunctionType
AX = mybir.AxisListType

P = 128
BANK = 512
EPS = 1e-5
MASKED = -1e30
LOWEST = -3e38

class Shared:

    def __init__(self, nc, ctx, tokens, width):
        self.tiles = tokens // P
        self.width = width
        self.x = ctx.enter_context(nc.sbuf_tensor("residual", [P, self.tiles, width], F32))
        self.ident = ctx.enter_context(nc.sbuf_tensor("ident", [P, P], F32))
        self.identb = ctx.enter_context(nc.sbuf_tensor("identb", [P, P], BF16))
        self.mask_qk = ctx.enter_context(nc.sbuf_tensor("mask_qk", [P, P], BF16))
        self.mask_kq = ctx.enter_context(nc.sbuf_tensor("mask_kq", [P, P], BF16))

def load_stage(nc, sh, x_dram):
    with nc.cleanup_on_exit(), ExitStack() as ctx:
        x_loaded = nc.alloc_semaphore("x_loaded")
        zeroed = nc.alloc_semaphore("zeroed")
        made = nc.alloc_semaphore("made")
        block = ctx.enter_context(nc.Block())

        @block.sync
        def _(sp):
            sp.dma_start(sh.x[:], x_dram.rearrange("b (t p) d -> p (b t) d", p=P)).then_inc(x_loaded, 16)
            sp.wait_ge(x_loaded, 16)

        @block.gpsimd
        def _(pool):
            for m in (sh.ident, sh.identb, sh.mask_qk, sh.mask_kq):
                pool.memset(m[:], 0.0).then_inc(zeroed, 1)
            pool.wait_ge(zeroed, 4)
            for m in (sh.ident, sh.identb):
                pool.affine_select(out=m[:], in_=m[:], compare_op=ALU.not_equal, fill=1.0, base=0,
                                   pattern=[[-1, P]], channel_multiplier=1).then_inc(made, 1)
            pool.affine_select(out=sh.mask_qk[:], in_=sh.mask_qk[:], compare_op=ALU.is_ge, fill=MASKED, base=0,
                               pattern=[[-1, P]], channel_multiplier=1).then_inc(made, 1)
            pool.affine_select(out=sh.mask_kq[:], in_=sh.mask_kq[:], compare_op=ALU.is_ge, fill=MASKED, base=0,
                               pattern=[[1, P]], channel_multiplier=-1).then_inc(made, 1)
            pool.wait_ge(made, 4)

def store_stage(nc, sh, out_dram):
    with nc.cleanup_on_exit(), ExitStack() as ctx:
        stored = nc.alloc_semaphore("out_stored")
        block = ctx.enter_context(nc.Block())

        @block.sync
        def _(sp):
            sp.dma_start(out_dram.rearrange("b (t p) d -> p (b t) d", p=P), sh.x[:]).then_inc(stored, 16)
            sp.wait_ge(stored, 16)

class Norm:

    def __init__(self, nc, ctx, tag, tiles):
        self.tiles = tiles
        self.stats = ctx.enter_context(nc.sbuf_tensor(f"{tag}_stats", [P, tiles, 6], F32))
        self.moments = ctx.enter_context(nc.sbuf_tensor(f"{tag}_moments", [P, tiles, 2], F32))
        self.var = ctx.enter_context(nc.sbuf_tensor(f"{tag}_var", [P, tiles], F32))
        self.std = ctx.enter_context(nc.sbuf_tensor(f"{tag}_std", [P, tiles], F32))
        self.rstd = ctx.enter_context(nc.sbuf_tensor(f"{tag}_rstd", [P, tiles], F32))
        self.stats_done = nc.alloc_semaphore(f"{tag}_stats_done")
        self.var_ready = nc.alloc_semaphore(f"{tag}_var_ready")
        self.std_ready = nc.alloc_semaphore(f"{tag}_std_ready")
        self.rstd_ready = nc.alloc_semaphore(f"{tag}_rstd_ready")

def norm_vector(dve, n, src):
    for t in range(n.tiles):
        dve.bn_stats(n.stats[:, t, :], src[:, t, :]).then_inc(n.stats_done, 1)
    for t in range(n.tiles):
        dve.wait_ge(n.stats_done, t + 1)
        dve.bn_aggr(n.moments[:, t, :], n.stats[:, t, :]).then_inc(n.stats_done, 1)
    dve.wait_ge(n.stats_done, 2 * n.tiles)
    dve.tensor_scalar(n.var[:], n.moments[:, :, 1], EPS, None, ALU.add).then_inc(n.var_ready, 1)
    dve.wait_ge(n.std_ready, 1)
    dve.reciprocal(n.rstd[:], n.std[:]).then_inc(n.rstd_ready, 1)
    dve.wait_ge(n.rstd_ready, 1)

def norm_scalar(act, n):
    act.wait_ge(n.var_ready, 1)
    act.activation(n.std[:], n.var[:], ACT.Sqrt).then_inc(n.std_ready, 1)

def standardize(dve, n, dst, src, ready):
    for t in range(n.tiles):
        dve.tensor_scalar(dst[:, t, :], src[:, t, :], n.moments[:, t, 0:1], n.rstd[:, t:t + 1],
                          ALU.subtract, ALU.mult).then_inc(ready, 1)

def turn_tensor(pe, sh, u, banks, tiles, u_ready, ut_psum, ut_ready):
    per = BANK // P
    for g in range(tiles // per):
        pe.wait_ge(u_ready, per * (g + 1))
        if g >= 2:
            pe.wait_ge(ut_ready, g - 1)
        for j in range(per):
            mm = pe.transpose(banks[g % 2][:, j * P:(j + 1) * P], u[:, per * g + j, :], sh.ident[:])
        mm.then_inc(ut_psum, 1)

def turn_scalar(act, ut, banks, tiles, ut_psum, ut_ready):
    for g in range(tiles * P // BANK):
        act.wait_ge(ut_psum, g + 1)
        act.activation(ut[:, g * BANK:(g + 1) * BANK], banks[g % 2][:], ACT.Copy).then_inc(ut_ready, 1)


def causal_steps(tiles, per):
    return [(qb, k, max(0, k - per * qb)) for qb in range(tiles // per) for k in range(per * qb + per)]

def head_order(steps, per, halves, prep, first, last, lag=0):
    n = len(steps)
    blocks = steps[-1][0] + 1
    at = {}
    for qb in range(blocks):
        end = max(i for i, s in enumerate(steps) if s[0] == qb)
        carried = end + 1 == n
        if carried and first:
            continue
        begin = (0 if carried else end + 1) + lag
        at.setdefault(begin + 1 - (lag > 0), []).append(("fin", qb, -1 if carried else 0))
        for half in range(halves):
            at.setdefault(begin + 3 + half - (lag > 0), []).append(("out", halves * qb + half, -1 if carried else 0))
    order, used, done, spent = [], 0, 0.0, 0.0
    widths = [per - s[2] for s in steps]
    for i in range(n):
        done += widths[i] / sum(widths[:n - 5])
        while used < len(prep) and not last and spent <= done * sum(p[2] for p in prep):
            order.append((prep[used][0], prep[used][1], 1))
            spent += prep[used][2]
            used += 1
        order.append(("pv", i, 0))
        if lag and i >= lag:
            order.append(("lo", i - lag, 0))
        elif lag and not first:
            order.append(("lo", n + i - lag, -1))
        if i + 2 < n:
            order.append(("qk", i + 2, 0))
        elif not last:
            order.append(("qk", i + 2 - n, 1))
        order += at.get(i, [])
    if last:
        order += [("lo", i, 0) for i in range(n - lag, n)] if lag else []
        order.append(("fin", blocks - 1, 0))
        order += [("out", halves * (blocks - 1) + half, 0) for half in range(halves)]
    return order
def known(h):
    return isinstance(h, int)


def heads_stage(nc, sh, w_dram, wo_dram, heads):
    T = sh.tiles
    DH = 64
    PER = BANK // P
    N = T * P
    STEPS = causal_steps(T, PER)
    NS = len(STEPS)
    BLOCKS = T // PER
    HALVES = 2
    HT = PER // HALVES
    CHUNKS = [(t, c) for t in range(T) for c in range(t // PER + 1)]
    NC = len(CHUNKS)
    VT = BANK // DH
    VS = T // VT
    USES = BLOCKS + VS + 1
    SCALE = float(DH) ** -0.5
    CONSTS = 13
    AHEAD = 5
    LAG = 3
    OWNER = [int(n % 5 in (0, 2, 4)) for n in range(NS)]
    PREP = [("proj", 0, 0.5), ("high", 0, 0.9), ("low", 0, 2.2), ("proj", 1, 0.5), ("high", 1, 0.9), ("low", 1, 1.2)]
    later = [(("proj", n), ("high", n), ("low", n)) for n in range(2, BLOCKS)] + \
            [(("value", n), ("value_high", n), ("value_low", n)) for n in range(VS)]
    for m in range(NC):
        PREP.append(("max", m, 0.6))
        if m % 2 and m >= 3 and (m - 3) // 2 < 3 * len(later):
            part = (m - 3) // 2 % 3
            PREP.append(later[(m - 3) // 6][part] + (1.0 if part == 2 else 0.2,))
    PREP += [("rowmax", 0, 1.5), ("mrow", 0, 1.0)]
    with nc.cleanup_on_exit(), ExitStack() as ctx:
        sb = lambda name, shape, dt=F32: ctx.enter_context(nc.sbuf_tensor("a1_" + name, shape, dt))
        psum = lambda name, shape: ctx.enter_context(nc.psum_tensor("a1_" + name, shape, F32))
        sem = lambda name: nc.alloc_semaphore("a1_" + name)
        norm = Norm(nc, ctx, "a1n", T)
        u = sb("u", [P, T, P])
        ut = sb("ut", [P, N])
        w = [sb(f"w{i}", [P, 3 * DH]) for i in range(2)]
        wo = [sb(f"wo{i}", [DH + 1, P + 1]) for i in range(2)]
        q_hh = [sb(f"q_hh{i}", [P, N], F32R) for i in range(2)]
        q_lm = [sb(f"q_lm{i}", [P, N], F32R) for i in range(2)]
        k_lh = [sb(f"k_lh{i}", [P, N], F32R) for i in range(2)]
        k_h1 = [sb(f"k_h1{i}", [P, N], F32R) for i in range(2)]
        vh = [sb(f"vh{i}", [P, T, DH + 1], F32R) for i in range(2)]
        vl = [sb(f"vl{i}", [P, T, DH], F32R) for i in range(2)]
        part_max = sb("part_max", [P, T, T // PER])
        row_max = sb("row_max", [P, T])
        max_row = [sb(f"max_row{i}", [T, P], F32R) for i in range(2)]
        probs = [sb(f"probs{i}", [P, BANK]) for i in range(AHEAD)]
        ph = [sb(f"ph{i}", [P, BANK], F32R) for i in range(AHEAD)]
        pl = [sb(f"pl{i}", [P, BANK], F32R) for i in range(AHEAD)]
        block_out = [sb(f"block_out{i}", [DH + 1, BANK]) for i in range(2)]
        rden = sb("rden", [P, HT])
        s1 = [psum(f"s1_{i}", [P, BANK]) for i in range(2)]
        s2 = [psum(f"s2_{i}", [P, BANK]) for i in range(2)]
        o = [psum(f"o{i}", [P, BANK]) for i in range(2)]
        pj = psum("pj", [P, BANK])
        ob = psum("ob", [P, HT, BANK // HT])

        u_ready = sem("u_ready")
        ut_psum = sem("ut_psum")
        ut_ready = sem("ut_ready")
        consts = sem("consts")
        w_loaded = [sem(f"w_loaded{i}") for i in range(2)]
        wo_loaded = [sem(f"wo_loaded{i}") for i in range(2)]
        proj_ready = sem("proj_ready")
        proj_free = sem("proj_free")
        split_hi = sem("split_hi")
        kh_copied = [sem(f"kh_copied{c}") for c in range(BLOCKS)]
        qh_copied = [sem(f"qh_copied{c}") for c in range(BLOCKS)]
        vh_ready = sem("vh_ready")
        s1_ready = sem("s1_ready")
        max_done = sem("max_done")
        m_ready = sem("m_ready")
        mrow_loaded = [sem(f"mrow_loaded{i}") for i in range(2)]
        s2_ready = sem("s2_ready")
        ph_ready = sem("ph_ready")
        exp_done = sem("exp_done")
        pl_ready = [sem(f"pl_ready{i}") for i in range(2)]
        pv_done = sem("pv_done")
        lo_done = sem("lo_done")
        fin_done = sem("fin_done")
        out_ready = sem("out_ready")
        rden_done = sem("rden_done")
        out_free = sem("out_free")
        block = ctx.enter_context(nc.Block())

        def run(emit):
            for what, n, _ in PREP:
                emit(what, n, 0, 0)
            emit("qk", 0, 0, 0)
            emit("qk", 1, 0, 0)

            def head(h, par):
                for what, n, d in head_order(STEPS, PER, HALVES, PREP, known(h) and h == 0,
                                                 known(h) and h == heads - 1, LAG):
                    emit(what, n, h + d, (par + d) % 2)

            return head

        def low_part(engine, owner, n, h):
            if OWNER[n] == owner:
                width = BANK - P * STEPS[n][2]
                engine.wait_ge(exp_done, NS * h + n + 1)
                engine.wait_ge(ph_ready, NS * h + n + 1)
                own = [m for m in range(NS) if OWNER[m] == owner]
                since = own[own.index(n) - 1] if n != own[0] else (-1 if known(h) and h == 0 else own[-1] - NS)
                if n >= AHEAD or not (known(h) and h == 0):
                    engine.wait_ge(lo_done, NS * h + n - AHEAD + 1)
                engine.tensor_tensor(pl[n % AHEAD][:, 0:width], probs[n % AHEAD][:, 0:width],
                                     ph[n % AHEAD][:, 0:width].bitcast(F32), ALU.subtract)\
                      .then_inc(pl_ready[owner], n - since)

        def loads(h, par):
            return 8 * (h - par) + 16

        @block.sync
        def _(sp):
            def weights(h, par):
                if not known(h) or h >= 2:
                    sp.wait_ge(proj_ready, USES * (h - 2) + BLOCKS + VS)
                sp.dma_start(w[par][:], w_dram[bass.ds(h, 1)].rearrange("a p n -> (a p) n"))\
                  .then_inc(w_loaded[par], 16)

            def out_weights(h, par):
                if not known(h) or h >= 2:
                    sp.wait_ge(out_ready, BLOCKS * HALVES * (h - 1))
                sp.dma_start(wo[par][0:DH, 0:P], wo_dram[bass.ds(h, 1)].rearrange("a p n -> (a p) n"))\
                  .then_inc(wo_loaded[par], 16)

            def maxima(h, par):
                sp.wait_ge(proj_free, USES * (h + 1))
                sp.dma_start(q_lm[par][DH:DH + 1, :].bitcast(F32), max_row[par][:, :].bitcast(F32))\
                  .then_inc(mrow_loaded[par], 16)

            def copies(h, par):
                for c in range(BLOCKS):
                    cs = slice(c * BANK, (c + 1) * BANK)
                    sp.wait_ge(split_hi, BLOCKS * h + c + 1)
                    sp.dma_start(k_h1[par][0:DH, cs].bitcast(F32), k_lh[par][DH:P, cs].bitcast(F32))\
                      .then_inc(kh_copied[c], 16)
                    sp.dma_start(q_hh[par][DH:P, cs].bitcast(F32), q_hh[par][0:DH, cs].bitcast(F32))\
                      .then_inc(qh_copied[c], 16)

            def head(h, par):
                if not known(h) or h + 2 < heads:
                    weights(h + 2, par)
                if not known(h) or h + 1 < heads:
                    copies(h + 1, 1 - par)
                    out_weights(h + 1, 1 - par)
                    maxima(h + 1, 1 - par)

            sp.wait_ge(consts, CONSTS)
            weights(0, 0)
            weights(1, 1)
            out_weights(0, 0)
            copies(0, 0)
            maxima(0, 0)
            head(0, 0)
            with sp.Fori(0, heads // 2 - 2) as i:
                head(2 * i + 1, 1)
                head(2 * i + 2, 0)
            for h in range(heads - 3, heads):
                head(h, h % 2)

        @block.gpsimd
        def _(pool):
            count = 0
            for i in range(2):
                for part, value in ((q_lm[i][DH:P, :].bitcast(F32), 0.0), (k_h1[i][DH:P, :].bitcast(F32), 0.0),
                                    (k_h1[i][DH:DH + 1, :].bitcast(F32), -1.0), (vh[i][:, :, DH:DH + 1].bitcast(F32), 1.0),
                                    (wo[i][:], 0.0), (wo[i][DH:DH + 1, P:P + 1], 1.0)):
                    pool.memset(part, value).then_inc(consts, 1)
                    count += 1
                    pool.wait_ge(consts, count)
            pool.memset(part_max[:], LOWEST).then_inc(consts, 1)

            def emit(what, n, h, par):
                if what == "pv":
                    low_part(pool, 1, n, h)

            head = run(emit)
            head(0, 0)
            with pool.Fori(0, heads // 2 - 1) as i:
                head(2 * i + 1, 1)
                head(2 * i + 2, 0)
            head(heads - 1, 1)

        @block.scalar
        def _(act):
            norm_scalar(act, norm)
            turn_scalar(act, ut, s1, T, ut_psum, ut_ready)
            def emit(what, n, h, par):
                if what == "high":
                    cs = slice(n * BANK, (n + 1) * BANK)
                    if n == 0 and not (known(h) and h < 2):
                        act.wait_ge(pv_done, NS * (h - 1))
                    act.wait_ge(proj_ready, USES * h + n + 1)
                    act.activation(q_hh[par][0:DH, cs], pj[0:DH, :], ACT.Copy)
                    act.activation(k_lh[par][DH:P, cs], pj[DH:P, :], ACT.Copy).then_inc(split_hi, 1)
                if what == "value_high":
                    if n == 0 and not (known(h) and h < 2):
                        act.wait_ge(lo_done, NS * (h - 1))
                    act.wait_ge(proj_ready, USES * h + BLOCKS + n + 1)
                    act.activation(vh[par][:, n * VT:(n + 1) * VT, 0:DH], pj[:].rearrange("p (t v) -> p t v", v=DH),
                                   ACT.Copy).then_inc(vh_ready, 1)
                if what == "qk":
                    width = BANK - P * STEPS[n][2]
                    act.wait_ge(s2_ready, NS * h + n + 1)
                    if n >= AHEAD or not (known(h) and h == 0):
                        act.wait_ge(pv_done, NS * h + n - AHEAD + 1)
                    act.activation(ph[n % AHEAD][:, 0:width], s2[n % 2][:, 0:width], ACT.Exp,
                                   scale=SCALE).then_inc(ph_ready, 1)
                    if n >= AHEAD or not (known(h) and h == 0):
                        before = (n - AHEAD) % NS
                        act.wait_ge(pl_ready[OWNER[before]], NS * h + n - AHEAD + 1)
                    act.activation(probs[n % AHEAD][:, 0:width], s2[n % 2][:, 0:width], ACT.Exp,
                                   scale=SCALE).then_inc(exp_done, 1)
                if what == "fin":
                    last = max(i for i, s in enumerate(STEPS) if s[0] == n)
                    act.wait_ge(lo_done, NS * h + last + 1)
                    if n >= 2 or not (known(h) and h == 0):
                        act.wait_ge(out_ready, HALVES * (BLOCKS * h + n - 1))
                    act.activation(block_out[n % 2][:], o[n % 2][0:DH + 1, :], ACT.Copy).then_inc(fin_done, 1)

            head = run(emit)
            head(0, 0)
            with act.Fori(0, heads // 2 - 1) as i:
                head(2 * i + 1, 1)
                head(2 * i + 2, 0)
            head(heads - 1, 1)

        @block.tensor
        def _(pe):
            turn_tensor(pe, sh, u, s1, T, u_ready, ut_psum, ut_ready)
            pe.wait_ge(ut_ready, T // PER)
            pe.wait_ge(consts, CONSTS)

            def emit(what, n, h, par):
                if what == "proj":
                    if n == 0:
                        pe.wait_ge(w_loaded[par], loads(h, par))
                    pe.wait_ge(proj_free, USES * h + n)
                    pe.matmul(pj[:], w[par][:, 0:2 * DH], ut[:, n * BANK:(n + 1) * BANK],
                              start=True, stop=True).then_inc(proj_ready, 1)
                if what == "value":
                    pe.wait_ge(proj_free, USES * h + BLOCKS + n)
                    for j in range(VT):
                        t = n * VT + j
                        mm = pe.matmul(pj[:, j * DH:(j + 1) * DH], ut[:, t * P:(t + 1) * P], w[par][:, 2 * DH:3 * DH],
                                       start=True, stop=True)
                    mm.then_inc(proj_ready, 1)
                if what == "max":
                    t, c = CHUNKS[n]
                    width = min(BANK, (t + 1) * P - c * BANK)
                    diag = c == t // PER
                    if t % PER == 0 and c == 0:
                        pe.wait_ge(kh_copied[t // PER], 16 * h + 16)
                    if n >= 2:
                        pe.wait_ge(max_done, NC * h + n - 1)
                    mm = pe.matmul(s1[n % 2][:, 0:width], q_hh[par][0:DH, t * P:(t + 1) * P],
                                   k_h1[par][0:DH, c * BANK:c * BANK + width], start=True, stop=not diag)
                    if diag:
                        mm = pe.matmul(s1[n % 2][:, width - P:width], sh.identb[:], sh.mask_qk[:],
                                       start=False, stop=True)
                    mm.then_inc(s1_ready, 1)
                if what == "mrow":
                    pe.wait_ge(m_ready, h + 1)
                    pe.wait_ge(proj_free, USES * h + USES - 1)
                    pe.transpose(pj[0:T, 0:P], row_max[:], sh.ident[:]).then_inc(proj_ready, 1)
                if what == "qk":
                    qb, k, r = STEPS[n]
                    qs = slice((PER * qb + r) * P, (qb + 1) * BANK)
                    ks = slice(k * P, (k + 1) * P)
                    width = BANK - P * r
                    diag = k >= PER * qb
                    if k == 0:
                        pe.wait_ge(qh_copied[qb], 16 * h + 16)
                    if n == 0:
                        pe.wait_ge(mrow_loaded[par], loads(h, par))
                    if n >= 2 or not (known(h) and h == 0):
                        pe.wait_ge(exp_done, NS * h + n - 1)
                    dst = s2[n % 2]
                    pe.matmul(dst[:, 0:width], k_lh[par][:, ks], q_hh[par][:, qs], start=True, stop=False)
                    mm = pe.matmul(dst[:, 0:width], k_h1[par][:, ks], q_lm[par][:, qs], start=False, stop=not diag)
                    if diag:
                        mm = pe.matmul(dst[:, 0:P], sh.identb[:], sh.mask_kq[:], start=False, stop=True)
                    mm.then_inc(s2_ready, 1)
                if what == "pv":
                    qb, k, r = STEPS[n]
                    if n == 0:
                        pe.wait_ge(vh_ready, VS * h + VS)
                        pe.wait_ge(proj_free, USES * h + BLOCKS + VS)
                    pe.wait_ge(ph_ready, NS * h + n + 1)
                    if k == 0 and (qb >= 2 or not (known(h) and h == 0)):
                        pe.wait_ge(fin_done, BLOCKS * h + qb - 1)
                    pe.matmul(o[qb % 2][0:DH + 1, P * r:BANK], vh[par][:, k, :], ph[n % AHEAD][:, 0:BANK - P * r],
                              start=(k == 0), stop=False)
                    pe.matmul(o[qb % 2][0:DH, P * r:BANK], vl[par][:, k, :], ph[n % AHEAD][:, 0:BANK - P * r],
                              start=False, stop=False).then_inc(pv_done, 1)
                if what == "lo":
                    qb, k, r = STEPS[n]
                    pe.wait_ge(pl_ready[OWNER[n]], NS * h + n + 1)
                    pe.matmul(o[qb % 2][0:DH + 1, P * r:BANK], vh[par][:, k, :], pl[n % AHEAD][:, 0:BANK - P * r],
                              start=False, stop=(k == PER * qb + PER - 1)).then_inc(lo_done, 1)
                if what == "out":
                    qb = n // HALVES
                    if n == 0:
                        pe.wait_ge(wo_loaded[par], loads(h, par))
                    pe.wait_ge(fin_done, BLOCKS * h + qb + 1)
                    pe.wait_ge(out_free, BLOCKS * HALVES * h + n)
                    for j in range(HT):
                        q = (n % HALVES) * HT + j
                        mm = pe.matmul(ob[:, j, 0:P + 1], block_out[qb % 2][:, q * P:(q + 1) * P], wo[par][:],
                                       start=True, stop=True)
                    mm.then_inc(out_ready, 1)

            head = run(emit)
            head(0, 0)
            with pe.Fori(0, heads // 2 - 1) as i:
                head(2 * i + 1, 1)
                head(2 * i + 2, 0)
            head(heads - 1, 1)

        @block.vector
        def _(dve):
            norm_vector(dve, norm, sh.x)
            standardize(dve, norm, u, sh.x, u_ready)
            dve.wait_ge(consts, CONSTS)

            def emit(what, n, h, par):
                if what == "low":
                    cs = slice(n * BANK, (n + 1) * BANK)
                    dve.wait_ge(split_hi, BLOCKS * h + n + 1)
                    dve.tensor_tensor(q_lm[par][0:DH, cs], pj[0:DH, :], q_hh[par][0:DH, cs].bitcast(F32),
                                      ALU.subtract)
                    dve.tensor_tensor(k_lh[par][0:DH, cs], pj[DH:P, :], k_lh[par][DH:P, cs].bitcast(F32),
                                      ALU.subtract).then_inc(proj_free, 1)
                if what == "value_low":
                    half = slice(n * VT, (n + 1) * VT)
                    dve.wait_ge(vh_ready, VS * h + n + 1)
                    dve.tensor_tensor(vl[par][:, half, :], pj[:].rearrange("p (t v) -> p t v", v=DH),
                                      vh[par][:, half, 0:DH].bitcast(F32), ALU.subtract).then_inc(proj_free, 1)
                if what == "max":
                    t, c = CHUNKS[n]
                    width = min(BANK, (t + 1) * P - c * BANK)
                    dve.wait_ge(s1_ready, NC * h + n + 1)
                    dve.reduce_max(part_max[:, t, c:c + 1], s1[n % 2][:, 0:width], AX.X).then_inc(max_done, 1)
                if what == "pv":
                    low_part(dve, 0, n, h)
                if what == "rowmax":
                    dve.wait_ge(max_done, NC * (h + 1))
                    dve.tensor_reduce(row_max[:], part_max[:], AX.X, ALU.max).then_inc(m_ready, 1)
                if what == "mrow":
                    dve.wait_ge(proj_ready, USES * (h + 1))
                    dve.tensor_copy(max_row[par][:], pj[0:T, 0:P]).then_inc(proj_free, 1)
                if what == "out":
                    use = BLOCKS * HALVES * h + n
                    dve.wait_ge(out_ready, use + 1)
                    dve.reciprocal(rden[:], ob[:, :, P]).then_inc(rden_done, 1)
                    dve.wait_ge(rden_done, use + 1)
                    for j in range(HT):
                        t = n * HT + j
                        mm = dve.scalar_tensor_tensor(out=sh.x[:, t, :], in0=ob[:, j, 0:P], scalar=rden[:, j:j + 1],
                                                      in1=sh.x[:, t, :], op0=ALU.mult, op1=ALU.add)
                    mm.then_inc(out_free, 1)

            head = run(emit)
            head(0, 0)
            with dve.Fori(0, heads // 2 - 1) as i:
                head(2 * i + 1, 1)
                head(2 * i + 2, 0)
            head(heads - 1, 1)

def rotary_stage(nc, sh, w_dram, wv_dram, wo_dram, table_dram, heads):
    T = sh.tiles
    D = P
    PER = BANK // P
    N = T * P
    STEPS = causal_steps(T, PER)
    NS = len(STEPS)
    BLOCKS = T // PER
    HALVES = 2
    HT = PER // HALVES
    CHUNKS = [(t, c) for t in range(T) for c in range(t // PER + 1)]
    NC = len(CHUNKS)
    RW = BANK // 2
    RC = N // RW
    RB = BANK // RW
    SCALE = float(D) ** -0.5
    AHEAD = 4
    PREP = [("rotate", 0, 1.5), ("rotate", 1, 1.5)]
    for b in range(BLOCKS):
        PREP += [("rotate", RB * (b + 1) + r, 1.5) for r in range(RB)] if b + 1 < BLOCKS else []
        PREP += [("max", m, 0.6) for m, (t, c) in enumerate(CHUNKS) if t // PER == b]
    PREP += [("rowmax", 0, 1.0), ("mrow", 0, 1.0)]
    with nc.cleanup_on_exit(), ExitStack() as ctx:
        sb = lambda name, shape, dt=F32: ctx.enter_context(nc.sbuf_tensor("a0_" + name, shape, dt))
        psum = lambda name, shape: ctx.enter_context(nc.psum_tensor("a0_" + name, shape, F32))
        sem = lambda name: nc.alloc_semaphore("a0_" + name)
        norm = Norm(nc, ctx, "a0n", T)
        u = sb("u", [P, T, P])
        ut = sb("ut", [P, N])
        w = sb("w", [P, heads + 1, 2, D])
        wv = sb("wv", [P, D])
        wo = sb("wo", [P, heads, P])
        table = sb("table", [P, RC, 2, RW])
        hi = sb("hi", [P, heads + 1, N], F32R)
        lo = sb("lo", [P, heads + 1, N], F32R)
        product = [sb(f"product{i}", [P, 2, RW]) for i in range(2)]
        rotated = [sb(f"rotated{i}", [P, RW]) for i in range(2)]
        v = sb("v", [P, T, D])
        part_max = sb("part_max", [P, T, T // PER])
        row_max = sb("row_max", [P, T])
        turned_max = [sb(f"turned_max{i}", [T, P], F32R) for i in range(heads)]
        max_row = [sb(f"max_row{i}", [1, N], F32R) for i in range(heads)]
        minus_one = sb("minus_one", [1, P], F32R)
        one = sb("one", [P, 1])
        probs = [sb(f"probs{i}", [P, BANK]) for i in range(AHEAD)]
        prob_sum = [sb(f"prob_sum{i}", [P, BANK]) for i in range(2)]
        block_out = [sb(f"block_out{i}", [P, BANK]) for i in range(2)]
        rden = sb("rden", [P, HT])
        s1 = [psum(f"s1_{i}", [P, BANK]) for i in range(2)]
        s2 = [psum(f"s2_{i}", [P, BANK]) for i in range(2)]
        o = [psum(f"o{i}", [P, BANK]) for i in range(2)]
        pj = psum("pj", [P, 2, RW])
        ob = psum("ob", [P, HT, BANK // HT])

        u_ready = sem("u_ready")
        ut_psum = sem("ut_psum")
        ut_ready = sem("ut_ready")
        consts = sem("consts")
        w_loaded = sem("w_loaded")
        wv_loaded = sem("wv_loaded")
        wo_loaded = sem("wo_loaded")
        table_loaded = sem("table_loaded")
        v_psum = sem("v_psum")
        v_ready = sem("v_ready")
        pair_ready = sem("pair_ready")
        product_done = sem("product_done")
        rotated_done = sem("rotated_done")
        hi_ready = sem("hi_ready")
        lo_ready = sem("lo_ready")
        s1_ready = sem("s1_ready")
        max_done = sem("max_done")
        m_ready = sem("m_ready")
        turned_ready = sem("turned_ready")
        turned_out = sem("turned_out")
        mrow_loaded = [sem(f"mrow_loaded{i}") for i in range(heads)]
        s2_ready = sem("s2_ready")
        exp_done = sem("exp_done")
        summed = sem("summed")
        pv_done = sem("pv_done")
        fin_done = sem("fin_done")
        out_ready = sem("out_ready")
        rden_done = sem("rden_done")
        out_free = sem("out_free")
        block = ctx.enter_context(nc.Block())

        def run(emit):
            for n in range(RC):
                emit("rotate", n, -1)
            for what, n, _ in PREP:
                emit(what, n, 0)
            emit("qk", 0, 0)
            emit("qk", 1, 0)
            for h in range(heads):
                for what, n, d in head_order(STEPS, PER, HALVES, PREP, h == 0, h == heads - 1):
                    emit(what, n, h + d)

        last_of = lambda qb: max(i for i, s in enumerate(STEPS) if s[0] == qb)

        @block.sync
        def _(sp):
            sp.dma_start(w[:], w_dram).then_inc(w_loaded, 16)
            sp.dma_start(table[:], table_dram).then_inc(table_loaded, 16)
            sp.dma_start(wv[:], wv_dram).then_inc(wv_loaded, 16)
            sp.dma_start(wo[:], wo_dram).then_inc(wo_loaded, 16)
            for h in range(heads):
                sp.wait_ge(turned_out, h + 1)
                sp.dma_start(max_row[h][:].bitcast(F32), turned_max[h][:].bitcast(F32))\
                  .then_inc(mrow_loaded[h], 16)

        @block.gpsimd
        def _(pool):
            pool.memset(minus_one[:].bitcast(F32), -1.0).then_inc(consts, 1)
            pool.memset(one[:], 1.0).then_inc(consts, 1)
            pool.memset(part_max[:], LOWEST).then_inc(consts, 1)

            def emit(what, n, h):
                if what == "rotate":
                    use = RC * (h + 1) + n
                    ns = slice(n * RW, (n + 1) * RW)
                    pool.wait_ge(hi_ready, use + 1)
                    pool.tensor_tensor(lo[:, h + 1, ns], rotated[n % 2][:], hi[:, h + 1, ns].bitcast(F32),
                                       ALU.subtract).then_inc(lo_ready, 1)
                if what == "pv":
                    qb, k, r = STEPS[n]
                    block_no = BLOCKS * h + qb
                    pool.wait_ge(exp_done, NS * h + n + 1)
                    total = prob_sum[qb % 2]
                    if k == 0:
                        if block_no >= 2:
                            pool.wait_ge(out_ready, HALVES * (block_no - 1))
                        pool.tensor_copy(total[:], probs[n % AHEAD][:]).then_inc(summed, 1)
                    else:
                        pool.wait_ge(summed, NS * h + n)
                        pool.tensor_tensor(total[:, P * r:], total[:, P * r:], probs[n % AHEAD][:, 0:BANK - P * r],
                                           ALU.add).then_inc(summed, 1)

            run(emit)

        @block.scalar
        def _(act):
            norm_scalar(act, norm)
            turn_scalar(act, ut, s1, T, ut_psum, ut_ready)
            for g in range(BLOCKS):
                act.wait_ge(v_psum, g + 1)
                act.activation(v[:, PER * g:PER * g + PER, :].rearrange("p t d -> p (t d)"), s2[g % 2][:],
                               ACT.Copy).then_inc(v_ready, 1)

            def emit(what, n, h):
                if what == "rotate":
                    use = RC * (h + 1) + n
                    act.wait_ge(rotated_done, use + 1)
                    act.activation(hi[:, h + 1, n * RW:(n + 1) * RW], rotated[n % 2][:], ACT.Copy)\
                       .then_inc(hi_ready, 1)
                if what == "qk":
                    width = BANK - P * STEPS[n][2]
                    use = NS * h + n
                    act.wait_ge(s2_ready, use + 1)
                    if use >= AHEAD:
                        act.wait_ge(pv_done, use - AHEAD + 1)
                        act.wait_ge(summed, use - AHEAD + 1)
                    act.activation(probs[n % AHEAD][:, 0:width], s2[n % 2][:, 0:width], ACT.Exp,
                                   scale=SCALE).then_inc(exp_done, 1)
                if what == "fin":
                    block_no = BLOCKS * h + n
                    act.wait_ge(pv_done, NS * h + last_of(n) + 1)
                    if block_no >= 2:
                        act.wait_ge(out_ready, HALVES * (block_no - 1))
                    act.activation(block_out[n % 2][:], o[n % 2][:], ACT.Copy).then_inc(fin_done, 1)

            run(emit)

        @block.tensor
        def _(pe):
            turn_tensor(pe, sh, u, s1, T, u_ready, ut_psum, ut_ready)
            pe.wait_ge(ut_ready, T // PER)
            pe.wait_ge(wv_loaded, 16)
            for g in range(BLOCKS):
                if g >= 2:
                    pe.wait_ge(v_ready, g - 1)
                for j in range(PER):
                    t = PER * g + j
                    mm = pe.matmul(s2[g % 2][:, j * P:(j + 1) * P], ut[:, t * P:(t + 1) * P], wv[:],
                                   start=True, stop=True)
                mm.then_inc(v_psum, 1)
            pe.wait_ge(v_ready, BLOCKS)
            pe.wait_ge(w_loaded, 16)
            pe.wait_ge(consts, 3)

            def emit(what, n, h):
                if what == "rotate":
                    use = RC * (h + 1) + n
                    if use >= 1:
                        pe.wait_ge(product_done, use)
                    for s in range(2):
                        mm = pe.matmul(pj[:, s, :], w[:, h + 1, s, :], ut[:, n * RW:(n + 1) * RW],
                                       start=True, stop=True)
                    mm.then_inc(pair_ready, 1)
                if what == "max":
                    t, c = CHUNKS[n]
                    width = min(BANK, (t + 1) * P - c * BANK)
                    diag = c == t // PER
                    if t % PER == 0 and c == 0:
                        pe.wait_ge(hi_ready, RC * (h + 1) + RB * (t // PER + 1))
                    if NC * h + n >= 2:
                        pe.wait_ge(max_done, NC * h + n - 1)
                    mm = pe.matmul(s1[n % 2][:, 0:width], hi[:, h + 1, t * P:(t + 1) * P],
                                   hi[:, 0, c * BANK:c * BANK + width], start=True, stop=not diag)
                    if diag:
                        mm = pe.matmul(s1[n % 2][:, width - P:width], sh.identb[:], sh.mask_qk[:],
                                       start=False, stop=True)
                    mm.then_inc(s1_ready, 1)
                if what == "mrow":
                    pe.wait_ge(m_ready, h + 1)
                    pe.wait_ge(product_done, RC * (h + 2))
                    pe.transpose(pj[0:T, 0, 0:P], row_max[:], sh.ident[:]).then_inc(turned_ready, 1)
                if what == "qk":
                    qb, k, r = STEPS[n]
                    qs = slice((PER * qb + r) * P, (qb + 1) * BANK)
                    ks = slice(k * P, (k + 1) * P)
                    width = BANK - P * r
                    diag = k >= PER * qb
                    use = NS * h + n
                    if n == 0:
                        pe.wait_ge(mrow_loaded[h], 16)
                        pe.wait_ge(lo_ready, RC * (h + 2))
                    if use >= 2:
                        pe.wait_ge(exp_done, use - 1)
                    dst = s2[n % 2]
                    pe.matmul(dst[:, 0:width], hi[:, 0, ks], hi[:, h + 1, qs], start=True, stop=False)
                    pe.matmul(dst[:, 0:width], hi[:, 0, ks], lo[:, h + 1, qs], start=False, stop=False)
                    pe.matmul(dst[:, 0:width], lo[:, 0, ks], hi[:, h + 1, qs], start=False, stop=False)
                    mm = pe.matmul(dst[:, 0:width], minus_one[:], max_row[h][:, qs], start=False, stop=not diag)
                    if diag:
                        mm = pe.matmul(dst[:, 0:P], sh.identb[:], sh.mask_kq[:], start=False, stop=True)
                    mm.then_inc(s2_ready, 1)
                if what == "pv":
                    qb, k, r = STEPS[n]
                    pe.wait_ge(exp_done, NS * h + n + 1)
                    if k == 0 and BLOCKS * h + qb >= 2:
                        pe.wait_ge(fin_done, BLOCKS * h + qb - 1)
                    pe.matmul(o[qb % 2][:, P * r:BANK], v[:, k, :], probs[n % AHEAD][:, 0:BANK - P * r],
                              start=(k == 0), stop=(k == PER * qb + PER - 1)).then_inc(pv_done, 1)
                if what == "out":
                    qb = n // HALVES
                    use = BLOCKS * HALVES * h + n
                    if use == 0:
                        pe.wait_ge(wo_loaded, 16)
                    pe.wait_ge(fin_done, BLOCKS * h + qb + 1)
                    pe.wait_ge(summed, NS * h + last_of(qb) + 1)
                    if use >= 1:
                        pe.wait_ge(out_free, use)
                    for j in range(HT):
                        q = (n % HALVES) * HT + j
                        pe.matmul(ob[:, j, 0:P], block_out[qb % 2][:, q * P:(q + 1) * P], wo[:, h, :],
                                  start=True, stop=True)
                        mm = pe.matmul(ob[:, j, P:P + 1], prob_sum[qb % 2][:, q * P:(q + 1) * P], one[:],
                                       start=True, stop=True)
                    mm.then_inc(out_ready, 1)

            run(emit)

        @block.vector
        def _(dve):
            norm_vector(dve, norm, sh.x)
            standardize(dve, norm, u, sh.x, u_ready)
            dve.wait_ge(consts, 3)
            dve.wait_ge(table_loaded, 16)

            def emit(what, n, h):
                if what == "rotate":
                    use = RC * (h + 1) + n
                    dve.wait_ge(pair_ready, use + 1)
                    dve.tensor_tensor(product[n % 2][:], pj[:], table[:, n], ALU.mult).then_inc(product_done, 1)
                    if use >= 2:
                        dve.wait_ge(lo_ready, use - 1)
                    dve.wait_ge(product_done, use + 1)
                    dve.tensor_tensor(rotated[n % 2][:], product[n % 2][:, 0, :], product[n % 2][:, 1, :],
                                      ALU.add).then_inc(rotated_done, 1)
                if what == "max":
                    t, c = CHUNKS[n]
                    width = min(BANK, (t + 1) * P - c * BANK)
                    dve.wait_ge(s1_ready, NC * h + n + 1)
                    dve.reduce_max(part_max[:, t, c:c + 1], s1[n % 2][:, 0:width], AX.X).then_inc(max_done, 1)
                if what == "rowmax":
                    dve.wait_ge(max_done, NC * (h + 1))
                    dve.tensor_reduce(row_max[:], part_max[:], AX.X, ALU.max).then_inc(m_ready, 1)
                if what == "mrow":
                    dve.wait_ge(turned_ready, h + 1)
                    dve.tensor_copy(turned_max[h][:], pj[0:T, 0, 0:P]).then_inc(turned_out, 1)
                if what == "out":
                    use = BLOCKS * HALVES * h + n
                    dve.wait_ge(out_ready, use + 1)
                    dve.reciprocal(rden[:], ob[:, :, P]).then_inc(rden_done, 1)
                    dve.wait_ge(rden_done, use + 1)
                    for j in range(HT):
                        t = n * HT + j
                        mm = dve.scalar_tensor_tensor(out=sh.x[:, t, :], in0=ob[:, j, 0:P], scalar=rden[:, j:j + 1],
                                                      in1=sh.x[:, t, :], op0=ALU.mult, op1=ALU.add)
                    mm.then_inc(out_free, 1)

            run(emit)


def first_choice_stage(nc, sh, tag, router_dram, rbias_dram, we_dram, be_dram, experts):
    T = sh.tiles
    N = T * P
    E = experts
    PER = BANK // P
    BANKS = E * P // BANK
    with nc.cleanup_on_exit(), ExitStack() as ctx:
        sb = lambda name, shape, dt=F32: ctx.enter_context(nc.sbuf_tensor(f"{tag}_{name}", shape, dt))
        psum = lambda name, shape: ctx.enter_context(nc.psum_tensor(f"{tag}_{name}", shape, F32))
        sem = lambda name: nc.alloc_semaphore(f"{tag}_{name}")
        norm = Norm(nc, ctx, tag + "n", T)
        u = sb("u", [P, T, P])
        ut = sb("ut", [P, N])
        router = sb("router", [P, E])
        rbias = sb("rbias", [P, E])
        we = sb("we", [P, E * P])
        be = sb("be", [P, T, P])
        logits = sb("logits", [P, T, E])
        top = sb("top", [P, T])
        prob = sb("prob", [P, T, E])
        total = sb("total", [P, T])
        weight = sb("weight", [P, T])
        order = sb("order", [P, T, E])
        rank = sb("rank", [P, T, E])
        choice = sb("choice", [P, T, E])
        choice_t = sb("choice_t", [P, P])
        turn = [psum(f"turn{i}", [P, BANK]) for i in range(2)]
        y = [psum(f"y{i}", [P, E, P]) for i in range(2)]
        small = psum("small", [P, T, E])
        bias = psum("bias", [P, PER, P])

        loaded = sem("loaded")
        u_ready = sem("u_ready")
        ut_psum = sem("ut_psum")
        ut_ready = sem("ut_ready")
        consts = sem("consts")
        be_loaded = sem("be_loaded")
        logits_psum = sem("logits_psum")
        step = sem("step")
        shifted = sem("shifted")
        exp_done = sem("exp_done")
        choice_ready = sem("choice_ready")
        turned = sem("turned")
        turned_out = sem("turned_out")
        y_ready = sem("y_ready")
        y_used = sem("y_used")
        bias_ready = sem("bias_ready")
        bias_used = sem("bias_used")
        block = ctx.enter_context(nc.Block())

        @block.sync
        def _(sp):
            sp.dma_start(router[:], router_dram).then_inc(loaded, 16)
            sp.dma_start(rbias[:], rbias_dram.partition_broadcast(P)).then_inc(loaded, 16)
            sp.dma_start(we[:], we_dram).then_inc(loaded, 16)
            sp.wait_ge(consts, 1)
            for t in range(T):
                sp.dma_start(be[t * E:(t + 1) * E, t, :], be_dram).then_inc(be_loaded, 16)

        @block.gpsimd
        def _(pool):
            pool.memset(be[:], 0.0).then_inc(consts, 1)
            for e in range(E):
                pool.memset(order[:, :, e:e + 1], float(E - e)).then_inc(consts, 1)

        @block.scalar
        def _(act):
            norm_scalar(act, norm)
            turn_scalar(act, ut, turn, T, ut_psum, ut_ready)
            act.wait_ge(shifted, 1)
            act.activation(prob[:], logits[:], ACT.Exp).then_inc(exp_done, 1)

        @block.tensor
        def _(pe):
            turn_tensor(pe, sh, u, turn, T, u_ready, ut_psum, ut_ready)
            pe.wait_ge(ut_ready, T // PER)
            pe.wait_ge(loaded, 48)
            for t in range(T):
                mm = pe.matmul(small[:, t, :], ut[:, t * P:(t + 1) * P], router[:], start=True, stop=True)
            mm.then_inc(logits_psum, 1)

            def tile(t):
                if t >= 2:
                    pe.wait_ge(y_used, t - 1)
                for b in range(BANKS):
                    mm = pe.matmul(y[t % 2][:, b * PER:(b + 1) * PER, :].rearrange("p e o -> p (e o)"),
                                   ut[:, t * P:(t + 1) * P], we[:, b * BANK:(b + 1) * BANK], start=True, stop=True)
                mm.then_inc(y_ready, 1)

            tile(0)
            tile(1)
            pe.wait_ge(choice_ready, 1)
            pe.transpose(turn[0][:, 0:P], choice[:].rearrange("p t e -> p (t e)"), sh.ident[:]).then_inc(turned, 1)
            pe.wait_ge(turned_out, 1)
            pe.wait_ge(be_loaded, 16 * T)
            for g in range(T // PER):
                if g:
                    pe.wait_ge(bias_used, g)
                for j in range(PER):
                    mm = pe.matmul(bias[:, j, :], choice_t[:], be[:, PER * g + j, :], start=True, stop=True)
                mm.then_inc(bias_ready, 1)
                for t in range(PER * g, PER * g + PER):
                    if t >= 2:
                        tile(t)

        @block.vector
        def _(dve):
            norm_vector(dve, norm, sh.x)
            standardize(dve, norm, u, sh.x, u_ready)
            wide = lambda a: a[:].unsqueeze(2).broadcast_to([P, T, E])
            count = 0

            def then(instruction):
                nonlocal count
                instruction.then_inc(step, 1)
                count += 1
                dve.wait_ge(step, count)

            dve.wait_ge(loaded, 48)
            dve.wait_ge(logits_psum, 1)
            then(dve.tensor_tensor(logits[:], small[:], rbias[:].unsqueeze(1).broadcast_to([P, T, E]), ALU.add))
            then(dve.tensor_reduce(top[:], logits[:], AX.X, ALU.max))
            dve.tensor_tensor(logits[:], logits[:], wide(top), ALU.subtract).then_inc(shifted, 1)
            dve.wait_ge(exp_done, 1)
            dve.wait_ge(consts, 1 + E)
            then(dve.tensor_reduce(top[:], prob[:], AX.X, ALU.max))
            then(dve.tensor_reduce(total[:], prob[:], AX.X, ALU.add))
            then(dve.reciprocal(total[:], total[:]))
            then(dve.tensor_tensor(rank[:], prob[:], wide(top), ALU.is_equal))
            then(dve.tensor_tensor(rank[:], rank[:], order[:], ALU.mult))
            then(dve.scalar_tensor_tensor(out=weight[:], in0=top[:], scalar=0.5, in1=total[:], op0=ALU.mult,
                                          op1=ALU.mult))
            then(dve.tensor_reduce(top[:], rank[:], AX.X, ALU.max))
            then(dve.tensor_tensor(rank[:], rank[:], wide(top), ALU.is_equal))
            dve.tensor_tensor(choice[:], rank[:], wide(weight), ALU.mult).then_inc(choice_ready, 1)
            dve.wait_ge(turned, 1)
            dve.tensor_copy(choice_t[:], turn[0][:, 0:P]).then_inc(turned_out, 1)
            dve.wait_ge(choice_ready, 1)
            for t in range(T):
                if t % PER == 0:
                    g = t // PER
                    xs = sh.x[:, t:t + PER, :]
                    dve.wait_ge(bias_ready, g + 1)
                    dve.tensor_tensor(xs, bias[:], xs, ALU.add).then_inc(bias_used, 1)
                    dve.wait_ge(bias_used, g + 1)
                dve.wait_ge(y_ready, t + 1)
                for e in range(E):
                    add = dve.scalar_tensor_tensor(out=sh.x[:, t, :], in0=y[t % 2][:, e, :], scalar=choice[:, t, e:e + 1],
                                                   in1=sh.x[:, t, :], op0=ALU.mult, op1=ALU.add)
                    if e < E - 1:
                        then(add)
                add.then_inc(y_used, 1)


def balanced_stage(nc, sh, tag, cent_dram, g_dram, b_dram, w1_dram, b1_dram, w2_dram, b2_dram, experts, hidden):
    T = sh.tiles
    N = T * P
    E = experts
    C = N // E
    CT = C // P
    F = hidden // P
    RADIX = 16
    G = P // RADIX
    GT = N // G
    HALF = 1 << 16
    STEPS = [HALF // RADIX ** (i + 1) for i in range(4)]
    ROUNDS = 2 * len(STEPS)
    TAKEN = -1e5
    CHAIN = 3 * ROUNDS + 12
    with nc.cleanup_on_exit(), ExitStack() as ctx:
        sb = lambda name, shape, dt=F32: ctx.enter_context(nc.sbuf_tensor(f"{tag}_{name}", shape, dt))
        psum = lambda name, shape: ctx.enter_context(nc.psum_tensor(f"{tag}_{name}", shape, F32))
        sem = lambda name: nc.alloc_semaphore(f"{tag}_{name}")
        dram = lambda name, shape: nc.dram_tensor(f"{tag}_{name}", shape, F32, kind="Internal").ap()
        norm = Norm(nc, ctx, tag + "n", T)
        norm2 = Norm(nc, ctx, tag + "m", T)
        u = sb("u", [P, T, P])
        nrm = sb("nrm", [P, T, P])
        gain = sb("gain", [P, P])
        shift = sb("shift", [P, P])
        cent = sb("cent", [P, E])
        nt = sb("nt", [P, N])
        score = sb("score", [P, E, T])
        flip = sb("flip", [P, E * T], I32)
        key = sb("key", [P, E * T], I32)
        part = sb("part", [P, 2, E * T], I32)
        half = sb("half", [P, 2, E * T])
        half_t = sb("half_t", [P, 2, P])
        keys = sb("keys", [P, 2, E, GT])
        taken = sb("taken", [P, GT])
        high = sb("high", [P, GT])
        both = sb("both", [P, GT])
        junk = sb("junk", [P, GT])
        cnt = [sb(f"cnt{i}", [P, 1], BF16) for i in range(2)]
        reach = sb("reach", [P, RADIX])
        reached = sb("reached", [P, 1])
        cand = sb("cand", [P, 2])
        cand0 = sb("cand0", [P, 2])
        move = sb("move", [P, ROUNDS])
        rest = sb("rest", [P, 1])
        lane = sb("lane", [P, 1], I32)
        lane_f = sb("lane_f", [P, 1])
        group_i = sb("group_i", [P, 1], I32)
        lane_all = sb("lane_all", [P, 1])
        iota_i = sb("iota_i", [P, P], I32)
        iota_f = sb("iota_f", [P, P])
        pick = sb("pick", [P, RADIX], BF16)
        before = sb("before", [P, P], BF16)
        every = sb("every", [P, P], BF16)
        pick_group = sb("pick_group", [P, G, P], BF16)
        place = sb("place", [P, CT])
        above = sb("above", [P, GT])
        equal = sb("equal", [P, GT])
        tied = sb("tied", [P, 2], BF16)
        equal_sum = sb("equal_sum", [P, GT])
        ones = sb("ones", [P, GT])
        ranks = sb("ranks", [P, 4])
        free = sb("free", [P, 1])
        room = sb("room", [P, 1])
        chosen = sb("chosen", [P, GT])
        chosen_sum = sb("chosen_sum", [P, GT])
        base = sb("base", [P, 1])
        chosen_upto = sb("chosen_upto", [P, GT], BF16)
        sign = [sb(f"sign{i}", [P, N], BF16) for i in range(CT)]
        balance = sb("balance", [P, CT])
        token = sb("token", [P, E, CT], U32)
        routed = [sb(f"routed{i}", [P, CT, P]) for i in range(2)]
        routed_t = [sb(f"routed_t{i}", [P, C]) for i in range(2)]
        w1 = [sb(f"w1_{i}", [P, hidden]) for i in range(2)]
        w2 = [sb(f"w2_{i}", [P, F, P]) for i in range(2)]
        b1 = sb("b1", [P, E, F])
        b2 = sb("b2", [P, E, P])
        hid = [sb(f"hid{i}", [P, F, C]) for i in range(2)]
        y = sb("y", [P, T, P])
        back = sb("back", [P, T, P])
        turn = [psum(f"turn{i}", [P, BANK]) for i in range(2)]
        counts = psum("counts", [P, BANK])
        upto = psum("upto", [P, N])
        hp = [turn[0], psum("hp", [P, BANK])]
        yp = turn[1][:, 0:C].rearrange("p (s d) -> p s d", d=P)
        keys_dram = dram("keys_dram", (2, E * T, P))
        nrm_dram = dram("nrm_dram", (N, P))
        y_dram = dram("y_dram", (N, P))

        loaded = sem("loaded")
        biases = sem("biases")
        u_ready = sem("u_ready")
        std2 = sem("std2")
        gained = sem("gained")
        nrm_ready = sem("nrm_ready")
        nt_psum = sem("nt_psum")
        nt_ready = sem("nt_ready")
        scored = sem("scored")
        prep = sem("prep")
        key_ready = sem("key_ready")
        key_psum = sem("key_psum")
        key_out = sem("key_out")
        key_stored = sem("key_stored")
        key_loaded = sem("key_loaded")
        consts = sem("consts")
        shapes = sem("shapes")
        chain = sem("chain")
        cnt_ready = sem("cnt_ready")
        counts_ready = sem("counts_ready")
        tied_ready = sem("tied_ready")
        ranks_ready = sem("ranks_ready")
        chosen_ready = sem("chosen_ready")
        upto_ready = sem("upto_ready")
        sign_done = sem("sign_done")
        token_ready = sem("token_ready")
        nrm_stored = sem("nrm_stored")
        routed_loaded = [sem(f"routed_loaded{i}") for i in range(2)]
        rt_psum = sem("rt_psum")
        rt_ready = sem("rt_ready")
        w_loaded = [sem(f"w_loaded{i}") for i in range(2)]
        h_psum = sem("h_psum")
        h_ready = sem("h_ready")
        y_psum = sem("y_psum")
        y_ready = sem("y_ready")
        y_stored = sem("y_stored")
        y_back = sem("y_back")
        half_added = sem("half_added")
        SHAPES = 5 + 2 * (1 + len(STEPS)) + CT

        def stages(engine, body):
            for e in range(4):
                body(e, e % 2)
            with engine.Fori(2, E // 2) as i:
                body(2 * i, 0)
                body(2 * i + 1, 1)
            for e in range(E, E + 3):
                body(e, e % 2)

        block = ctx.enter_context(nc.Block())

        @block.sync
        def _(sp):
            sp.dma_start(gain[:], g_dram.partition_broadcast(P)).then_inc(loaded, 16)
            sp.dma_start(shift[:], b_dram.partition_broadcast(P)).then_inc(loaded, 16)
            sp.dma_start(cent[:], cent_dram).then_inc(loaded, 16)
            sp.dma_start(b1[:], b1_dram).then_inc(biases, 16)
            sp.dma_start(b2[:].rearrange("p e d -> p (e d)"), b2_dram.partition_broadcast(P)).then_inc(biases, 16)

            def weights(e, par):
                sp.dma_start(w1[par][:], w1_dram[bass.ds(e, 1)].rearrange("a p f -> (a p) f"))\
                  .then_inc(w_loaded[par], 16)
                sp.dma_start(w2[par][:], w2_dram[bass.ds(e, 1)].rearrange("a (c p) d -> (a p) c d", p=P))\
                  .then_inc(w_loaded[par], 16)

            weights(0, 0)
            weights(1, 1)
            sp.wait_ge(nrm_ready, T)
            sp.dma_start(nrm_dram.rearrange("(t p) d -> p t d", p=P), nrm[:]).then_inc(nrm_stored, 16)
            sp.wait_ge(key_out, 1)
            sp.dma_start(keys_dram.rearrange("h r p -> r h p"), half_t[:]).then_inc(key_stored, 16)
            sp.wait_ge(key_stored, 16)
            for g in range(G):
                src = keys_dram.rearrange("h (e t) p -> h e (t p)", e=E)[:, :, g * GT:(g + 1) * GT]
                sp.dma_start(keys[g * RADIX:(g + 1) * RADIX], src.partition_broadcast(RADIX)).then_inc(key_loaded, 16)
            with sp.Fori(0, E // 2 - 1) as i:
                for par in range(2):
                    e = 2 * i + par
                    sp.wait_ge(y_psum, e + 1)
                    weights(e + 2, par)
            sp.wait_ge(y_stored, 16 * E * CT)
            sp.dma_start(back[:], y_dram.rearrange("(t p) d -> p t d", p=P)).then_inc(y_back, 16)

        @block.gpsimd
        def _(pool):
            pool.iota(lane[:], pattern=[[0, 1]], base=0, channel_multiplier=1).then_inc(consts, 1)
            pool.iota(iota_i[:], pattern=[[1, P]], base=0, channel_multiplier=0).then_inc(consts, 1)
            pool.memset(every[:], 1.0 / RADIX).then_inc(consts, 1)
            pool.memset(before[:], 1.0 / RADIX).then_inc(consts, 1)
            pool.memset(pick_group[:], 0.0).then_inc(consts, 1)
            pool.memset(ones[:], 1.0).then_inc(consts, 1)
            pool.memset(taken[:], 0.0).then_inc(consts, 1)
            pool.wait_ge(consts, 7)
            blocks = before[:].rearrange("p (b r) -> p b r", r=RADIX)
            pool.affine_select(out=blocks, in_=blocks, compare_op=ALU.is_gt, fill=0.0, base=0,
                               pattern=[[RADIX, G], [0, RADIX]], channel_multiplier=-1).then_inc(consts, 1)
            pool.affine_select(out=pick_group[:], in_=pick_group[:], compare_op=ALU.not_equal, fill=1.0, base=0,
                               pattern=[[-RADIX, G], [0, P]], channel_multiplier=1).then_inc(consts, 1)

            def fetch(e):
                pool.wait_ge(token_ready, e + 1)
                if e >= 2:
                    pool.wait_ge(rt_psum, e - 1)
                for s in range(CT):
                    pool.indirect_dma_start(out=routed[e % 2][:, s, :], out_offset=None, in_=nrm_dram,
                                            in_offset=bass.IndirectOffsetOnAxis(ap=token[:, e, s:s + 1], axis=0))\
                        .then_inc(routed_loaded[e % 2], 16)

            def store(e):
                pool.wait_ge(y_ready, e + 1)
                for s in range(CT):
                    pool.indirect_dma_start(out=y_dram, out_offset=bass.IndirectOffsetOnAxis(ap=token[:, e, s:s + 1], axis=0),
                                            in_=y[:, e * CT + s, :], in_offset=None).then_inc(y_stored, 16)

            pool.wait_ge(nrm_stored, 16)
            for e in range(E + 2):
                if e < E:
                    fetch(e)
                if e >= 2:
                    store(e - 2)

        @block.scalar
        def _(act):
            norm_scalar(act, norm)
            norm_scalar(act, norm2)
            turn_scalar(act, nt, turn, T, nt_psum, nt_ready)
            act.wait_ge(key_psum, 1)
            act.activation(half_t[:].rearrange("p h q -> p (h q)"), turn[0][:, 0:2 * P], ACT.Copy).then_inc(key_out, 1)
            act.wait_ge(biases, 32)
            act.wait_ge(shapes, SHAPES)

            def find(e):
                if not (known(e) and e == 0):
                    act.wait_ge(token_ready, e)
                act.wait_ge(upto_ready, e + 1)
                for s in range(CT):
                    act.activation(sign[s][:], upto[:], ACT.Sign, bias=place[:, s:s + 1], accum_out=balance[:, s:s + 1])\
                       .then_inc(sign_done, 1)

            def found(e):
                act.wait_ge(sign_done, CT * e + CT)
                act.activation(token[:, bass.ds(e, 1), :].rearrange("p a s -> p (a s)"), balance[:], ACT.Copy,
                               scale=-0.5, bias=N / 2.0).then_inc(token_ready, 1)

            def turned(e, par):
                act.wait_ge(rt_psum, e + 1)
                act.activation(routed_t[par][:], turn[0][:, 0:C], ACT.Copy).then_inc(rt_ready, 1)

            def first_layer(e, par):
                for c in range(F):
                    act.wait_ge(h_psum, F * e + c + 1)
                    if not (known(e) and e < 2) and c == 0:
                        act.wait_ge(y_psum, e - 1)
                    act.activation(hid[par][:, c, :], hp[c % 2][:, 0:C], ACT.Gelu_apprx_tanh,
                                   bias=b1[:, bass.ds(e, 1), c:c + 1].rearrange("p a b -> p (a b)")).then_inc(h_ready, 1)

            def body(e, par):
                if not known(e) or 1 <= e <= E:
                    find(e - 1)
                    found(e - 1)
                if not known(e) or 2 <= e <= E + 1:
                    turned(e - 2, par)
                    first_layer(e - 2, par)

            stages(act, body)

        @block.tensor
        def _(pe):
            turn_tensor(pe, sh, nrm, turn, T, nrm_ready, nt_psum, nt_ready)
            pe.wait_ge(nt_ready, T * P // BANK)
            pe.wait_ge(loaded, 48)
            for t in range(T):
                mm = pe.matmul(counts[:, t * E:(t + 1) * E], nt[:, t * P:(t + 1) * P], cent[:], start=True, stop=True)
            mm.then_inc(scored, 1)
            pe.wait_ge(key_ready, 1)
            for h in range(2):
                mm = pe.transpose(turn[0][:, h * P:(h + 1) * P], half[:, h, :], sh.ident[:])
            mm.then_inc(key_psum, 1)

            def count(e, r):
                if not known(e) or e < E:
                    pe.wait_ge(cnt_ready, ROUNDS * e + r + 1)
                    pe.matmul(counts[:, 0:RADIX], cnt[r % 2][:].broadcast_to([P, P]), pick[:], start=True, stop=True)\
                      .then_inc(counts_ready, 1)

            def spread(e, gs):
                if not known(e) or 0 <= e < E:
                    if gs[0] == 0:
                        pe.wait_ge(chosen_ready, e + 1)
                        if not (known(e) and e == 0):
                            pe.wait_ge(sign_done, CT * e)
                    for g in gs:
                        mm = pe.matmul(upto[:, g * GT:(g + 1) * GT], pick_group[:, g, :], chosen_upto[:],
                                       start=True, stop=True)
                    if gs[-1] == G - 1:
                        mm.then_inc(upto_ready, 1)

            def turn_routed(e, par):
                if not known(e) or 0 <= e < E:
                    pe.wait_ge(routed_loaded[par], 16 * (e - par) + 32)
                    if not (known(e) and e == 0):
                        pe.wait_ge(rt_ready, e)
                        pe.wait_ge(h_ready, F * e - 1)
                    for s in range(CT):
                        mm = pe.transpose(turn[0][:, s * P:(s + 1) * P], routed[par][:, s, :], sh.ident[:])
                    mm.then_inc(rt_psum, 1)

            def up(e, par, c):
                if not known(e) or 0 <= e < E:
                    if c == 0:
                        pe.wait_ge(w_loaded[par], 16 * (e - par) + 32)
                        pe.wait_ge(rt_ready, e + 1)
                    if not (known(e) and e == 0 and c < 2):
                        pe.wait_ge(h_ready, F * e + c - 1)
                    pe.matmul(hp[c % 2][:, 0:C], w1[par][:, c * P:(c + 1) * P], routed_t[par][:], start=True,
                              stop=True).then_inc(h_psum, 1)

            def down(e, par, s):
                if not known(e) or 0 <= e < E:
                    if s == 0:
                        if not (known(e) and e == 0):
                            pe.wait_ge(y_ready, e)
                        pe.wait_ge(h_ready, F * e + F)
                    for c in range(F):
                        mm = pe.matmul(yp[:, s, :], hid[par][:, c, s * P:(s + 1) * P], w2[par][:, c, :],
                                       start=(c == 0), stop=(c == F - 1))
                    if s == CT - 1:
                        mm.then_inc(y_psum, 1)

            def body(e, par):
                count(e, 0)
                spread(e - 1, range(0, G // 2))
                count(e, 1)
                spread(e - 1, range(G // 2, G))
                for s in range(CT):
                    count(e, 2 + s)
                    down(e - 3, 1 - par, s)
                count(e, 4)
                turn_routed(e - 2, par)
                for r in range(5, ROUNDS):
                    count(e, r)
                    if r > 5:
                        up(e - 2, par, r - 6)
                if not known(e) or e < E:
                    pe.wait_ge(tied_ready, e + 1)
                    pe.matmul(counts[:, 0:2], before[:], tied[:], start=True, stop=True)
                    pe.matmul(counts[:, 2:4], every[:], tied[:], start=True, stop=True).then_inc(ranks_ready, 1)
                for c in range(ROUNDS - 6, F):
                    up(e - 2, par, c)

            pe.wait_ge(consts, 9)
            pe.wait_ge(key_out, 1)
            stages(pe, body)

        @block.vector
        def _(dve):
            wide = lambda a: a[:].unsqueeze(1).broadcast_to([P, T, P])
            norm_vector(dve, norm, sh.x)
            standardize(dve, norm, u, sh.x, u_ready)
            dve.wait_ge(u_ready, T)
            norm_vector(dve, norm2, u)
            standardize(dve, norm2, nrm, u, std2)
            dve.wait_ge(loaded, 48)
            PER = BANK // P
            for g in range(T // PER):
                ts = slice(PER * g, PER * g + PER)
                dve.wait_ge(std2, PER * (g + 1))
                dve.tensor_tensor(nrm[:, ts], nrm[:, ts], gain[:].unsqueeze(1).broadcast_to([P, PER, P]), ALU.mult)\
                   .then_inc(gained, 1)
                dve.wait_ge(gained, g + 1)
                dve.tensor_tensor(nrm[:, ts], nrm[:, ts], shift[:].unsqueeze(1).broadcast_to([P, PER, P]), ALU.add)\
                   .then_inc(nrm_ready, PER)
            dve.scalar_tensor_tensor(out=sh.x[:], in0=u[:], scalar=0.5, in1=sh.x[:], op0=ALU.mult, op1=ALU.add)\
               .then_inc(half_added, 1)

            count = 0

            def made(instruction):
                nonlocal count
                instruction.then_inc(shapes, 1)
                count += 1
                dve.wait_ge(shapes, count)

            dve.wait_ge(consts, 9)
            made(dve.tensor_copy(lane_all[:], lane[:]))
            made(dve.tensor_single_scalar(group_i[:], lane[:], RADIX - 1, ALU.bitwise_and))
            made(dve.tensor_copy(lane_f[:], group_i[:]))
            made(dve.tensor_copy(iota_f[:], iota_i[:]))
            made(dve.tensor_scalar(pick[:], iota_f[:, 0:RADIX], lane_f[:, 0:1], None, ALU.is_equal))
            for i in range(2):
                scale = 1.0 / HALF if i else 1.0
                made(dve.tensor_scalar(cand0[:, i:i + 1], lane_f[:], STEPS[0] * scale, 0.0 if i else -HALF / 2,
                                       ALU.mult, ALU.add))
                for s, step in enumerate(STEPS):
                    following = STEPS[s + 1] if s + 1 < len(STEPS) else 0
                    made(dve.tensor_scalar(move[:, 4 * i + s:4 * i + s + 1], lane_f[:], (following - step) * scale,
                                           -step * scale, ALU.mult, ALU.add))

            for s in range(CT):
                made(dve.tensor_scalar(place[:, s:s + 1], lane_all[:], -1.0, -(s * P + 0.5), ALU.mult, ALU.add))
            assert count == SHAPES

            count = 0

            def then(instruction):
                nonlocal count
                instruction.then_inc(prep, 1)
                count += 1
                dve.wait_ge(prep, count)

            dve.wait_ge(scored, 1)
            then(dve.tensor_copy(score[:].rearrange("p e t -> p t e"),
                                 counts[:, 0:T * E].rearrange("p (t e) -> p t e", e=E)))
            bits = score[:].rearrange("p e t -> p (e t)").bitcast(I32)
            then(dve.tensor_scalar(flip[:], bits, 31, 0x7FFFFFFF, ALU.arith_shift_right, ALU.bitwise_and))
            then(dve.tensor_tensor(key[:], bits, flip[:], ALU.bitwise_xor))
            then(dve.tensor_single_scalar(part[:, 0, :], key[:], 16, ALU.arith_shift_right))
            then(dve.tensor_single_scalar(part[:, 1, :], key[:], HALF - 1, ALU.bitwise_and))
            then(dve.tensor_copy(half[:, 0, :], part[:, 0, :]))
            then(dve.tensor_copy(half[:, 1, :], part[:, 1, :]))
            dve.tensor_scalar(half[:, 1, :], half[:, 1, :], 1.0 / HALF, None, ALU.mult).then_inc(key_ready, 1)
            dve.wait_ge(key_loaded, 16 * G)

            def body(e):
                done = 0

                def then(instruction):
                    nonlocal done
                    instruction.then_inc(chain, 1)
                    done += 1
                    dve.wait_ge(chain, CHAIN * e + done)

                key_of = lambda h: keys[:, h, bass.ds(e, 1), :].rearrange("p a t -> p (a t)")
                then(dve.tensor_tensor(high[:], key_of(0), taken[:], ALU.add))
                for i in range(2):
                    if i:
                        then(dve.scalar_tensor_tensor(out=both[:], in0=high[:], scalar=cand[:, 0:1], in1=key_of(1),
                                                      op0=ALU.subtract, op1=ALU.add))
                    for s, step in enumerate(STEPS):
                        r = len(STEPS) * i + s
                        now = cand0[:, i:i + 1] if s == 0 else cand[:, i:i + 1]
                        dve.tensor_scalar(junk[:], (both if i else high)[:], now, 0.0, ALU.is_ge, ALU.add,
                                          accum_out=cnt[r % 2][:]).then_inc(cnt_ready, 1)
                        then(dve.tensor_tensor(rest[:], now, move[:, r:r + 1], ALU.add))
                        if r == 5 and (not known(e) or e >= 3):
                            add_bias(e - 3)
                        dve.wait_ge(counts_ready, ROUNDS * e + r + 1)
                        then(dve.tensor_scalar(reach[:], counts[:, 0:RADIX], float(C), 0.0, ALU.is_ge, ALU.add,
                                               accum_out=reached[:]))
                        then(dve.scalar_tensor_tensor(out=cand[:, i:i + 1], in0=reached[:],
                                                      scalar=step / HALF if i else float(step), in1=rest[:],
                                                      op0=ALU.mult, op1=ALU.add))
                then(dve.tensor_scalar(above[:], both[:], cand[:, 1:2], 0.0, ALU.is_gt, ALU.add,
                                       accum_out=tied[:, 0:1]))
                dve.tensor_scalar(equal[:], both[:], cand[:, 1:2], 0.0, ALU.is_equal, ALU.add,
                                  accum_out=tied[:, 1:2]).then_inc(tied_ready, 1)
                dve.wait_ge(tied_ready, e + 1)
                then(dve.tensor_tensor_scan(equal_sum[:], ones[:], equal[:], 0.0, ALU.mult, ALU.add))
                dve.wait_ge(ranks_ready, e + 1)
                then(dve.tensor_copy(ranks[:], counts[:, 0:4]))
                then(dve.tensor_scalar(room[:], ranks[:, 2:3], -1.0, float(C), ALU.mult, ALU.add))
                then(dve.tensor_tensor(free[:], room[:], ranks[:, 1:2], ALU.subtract))
                then(dve.scalar_tensor_tensor(out=equal[:], in0=equal_sum[:], scalar=free[:, 0:1], in1=equal[:],
                                              op0=ALU.is_le, op1=ALU.mult))
                then(dve.tensor_tensor(chosen[:], above[:], equal[:], ALU.add))
                then(dve.scalar_tensor_tensor(out=taken[:], in0=chosen[:], scalar=TAKEN, in1=taken[:],
                                              op0=ALU.mult, op1=ALU.add))
                then(dve.tensor_tensor_scan(chosen_sum[:], ones[:], chosen[:], 0.0, ALU.mult, ALU.add))
                then(dve.scalar_tensor_tensor(out=base[:], in0=ranks[:, 1:2], scalar=room[:, 0:1], in1=ranks[:, 0:1],
                                              op0=ALU.min, op1=ALU.add))
                if not (known(e) and e == 0):
                    dve.wait_ge(upto_ready, e)
                dve.tensor_tensor(chosen_upto[:], chosen_sum[:], base[:].broadcast_to([P, GT]), ALU.add)\
                   .then_inc(chosen_ready, 1)
                dve.wait_ge(chosen_ready, e + 1)
                assert done == CHAIN

            def add_bias(e):
                dve.wait_ge(y_psum, e + 1)
                dve.tensor_tensor(y[:, bass.ds(e * CT, CT), :], yp, b2[:, bass.ds(e, 1), :].broadcast_to([P, CT, P]),
                                  ALU.add).then_inc(y_ready, 1)

            dve.wait_ge(biases, 32)
            for e in range(3):
                body(e)
            with dve.Fori(3, E) as e:
                body(e)
            for e in range(E - 3, E):
                add_bias(e)
            dve.wait_ge(half_added, 1)
            dve.wait_ge(y_back, 16)
            dve.scalar_tensor_tensor(out=sh.x[:], in0=back[:], scalar=0.5, in1=sh.x[:], op0=ALU.mult, op1=ALU.add)\
               .then_inc(half_added, 1)

def rotary_table(tokens, width, chunk):
    import numpy as np
    positions = np.arange(0, width, 2, dtype=np.float64)
    theta = np.power(10000.0, -2.0 * positions / width).astype(np.float32)
    angles = (np.arange(tokens, dtype=np.float32)[:, None] * theta[None, :]).astype(np.float32)
    cos = np.repeat(np.cos(angles).astype(np.float32).T, 2, axis=0)
    sin = np.repeat(np.sin(angles).astype(np.float32).T, 2, axis=0)
    sin[0::2] = -sin[0::2]
    both = np.stack([cos.reshape(width, -1, chunk), sin.reshape(width, -1, chunk)], axis=2)
    return np.ascontiguousarray(both)


def build(nc, x, cent, ln_g, ln_b, w1, b1, w2, b2, rot_w, rot_wv, rot_wo, rot_table, heads_w, wo, router, rbias, we, be,
          out):
    tokens, width = x.shape[1], x.shape[2]
    experts, _, hidden = w1.shape
    with ExitStack() as ctx:
        sh = Shared(nc, ctx, tokens, width)
        load_stage(nc, sh, x)
        balanced_stage(nc, sh, "f0a", cent, ln_g, ln_b, w1, b1, w2, b2, experts, hidden)
        rotary_stage(nc, sh, rot_w, rot_wv, rot_wo, rot_table, rot_wo.shape[1])
        balanced_stage(nc, sh, "f0b", cent, ln_g, ln_b, w1, b1, w2, b2, experts, hidden)
        first_choice_stage(nc, sh, "f1a", router, rbias, we, be, router.shape[1])
        heads_stage(nc, sh, heads_w, wo, wo.shape[0])
        first_choice_stage(nc, sh, "f1b", router, rbias, we, be, router.shape[1])
        store_stage(nc, sh, out)

def kernel(L0_attn_x, L0_attn_Wq, L0_attn_Wk, L0_attn_Wv, L0_attn_Wo, L0_ffn_centroids, L0_ffn_ln_g, L0_ffn_ln_b,
           L0_ffn_w1, L0_ffn_b1, L0_ffn_w2, L0_ffn_b2, L1_attn_w_q, L1_attn_w_k, L1_attn_w_v, L1_attn_w_o,
           L1_ffn_router_w, L1_ffn_router_b, L1_ffn_expert_w, L1_ffn_expert_b):
    import numpy as np
    import concourse.bacc as _bacc
    from concourse.bass_utils import run_bass_kernel_spmd as _run

    x = np.asarray(L0_attn_x)
    _, tokens, width = x.shape
    experts, _, hidden = L0_ffn_w1.shape
    heads, dh, _ = L1_attn_w_q.shape
    rot_heads = L0_attn_Wq.shape[0]
    plain = np.concatenate([np.asarray(L0_attn_Wk)[None], np.asarray(L0_attn_Wq)])
    swapped = plain.reshape(-1, width // 2, 2, width)[:, :, ::-1].reshape(plain.shape)
    arrays = {
        "x": x,
        "cent": np.asarray(L0_ffn_centroids).T,
        "ln_g": np.asarray(L0_ffn_ln_g),
        "ln_b": np.asarray(L0_ffn_ln_b),
        "w1": np.asarray(L0_ffn_w1),
        "b1": np.asarray(L0_ffn_b1).reshape(experts, hidden // P, P).transpose(2, 0, 1),
        "w2": np.asarray(L0_ffn_w2),
        "b2": np.asarray(L0_ffn_b2).reshape(-1),
        "rot_w": np.stack([plain, swapped], axis=1).transpose(3, 0, 1, 2),
        "rot_wv": np.asarray(L0_attn_Wv).T,
        "rot_wo": np.asarray(L0_attn_Wo).reshape(width, rot_heads, width).transpose(2, 1, 0),
        "rot_table": rotary_table(tokens, width, 256),
        "heads_w": np.concatenate([np.asarray(w) for w in (L1_attn_w_q, L1_attn_w_k, L1_attn_w_v)],
                                  axis=1).transpose(0, 2, 1),
        "wo": np.asarray(L1_attn_w_o).T.reshape(heads, dh, width),
        "router": np.asarray(L1_ffn_router_w).T,
        "rbias": np.asarray(L1_ffn_router_b),
        "we": np.asarray(L1_ffn_expert_w).transpose(2, 0, 1).reshape(width, -1),
        "be": np.asarray(L1_ffn_expert_b),
    }
    nc = _bacc.Bacc("TRN2", target_bir_lowering=False, num_devices=1)
    arrays = {name: np.ascontiguousarray(a) for name, a in arrays.items()}
    args = [nc.dram_tensor(name, a.shape, mybir.dt.from_np(a.dtype), kind="ExternalInput").ap()
            for name, a in arrays.items()]
    out = nc.dram_tensor("out", x.shape, F32, kind="ExternalOutput").ap()
    build(nc, *args, out)
    result = _run(nc, [arrays], core_ids=[0])
    return result.results[0]["out"]
```

```python
from contextlib import ExitStack

import concourse.bass as bass
from concourse import mybir

F32 = mybir.dt.float32
F32R = mybir.dt.float32r
BF16 = mybir.dt.bfloat16
U32 = mybir.dt.uint32
I32 = mybir.dt.int32
ALU = mybir.AluOpType
ACT = mybir.ActivationFunctionType
AX = mybir.AxisListType

P = 128
BANK = 512
EPS = 1e-5
MASKED = -1e30
LOWEST = -3e38

class Shared:

    def __init__(self, nc, ctx, tokens, width):
        self.tiles = tokens // P
        self.width = width
        self.x = ctx.enter_context(nc.sbuf_tensor("residual", [P, self.tiles, width], F32))
        self.ident = ctx.enter_context(nc.sbuf_tensor("ident", [P, P], F32))
        self.identb = ctx.enter_context(nc.sbuf_tensor("identb", [P, P], BF16))
        self.mask_qk = ctx.enter_context(nc.sbuf_tensor("mask_qk", [P, P], BF16))
        self.mask_kq = ctx.enter_context(nc.sbuf_tensor("mask_kq", [P, P], BF16))

def load_stage(nc, sh, x_dram):
    with nc.cleanup_on_exit(), ExitStack() as ctx:
        x_loaded = nc.alloc_semaphore("x_loaded")
        zeroed = nc.alloc_semaphore("zeroed")
        made = nc.alloc_semaphore("made")
        block = ctx.enter_context(nc.Block())

        @block.sync
        def _(sp):
            sp.dma_start(sh.x[:], x_dram.rearrange("b (t p) d -> p (b t) d", p=P)).then_inc(x_loaded, 16)
            sp.wait_ge(x_loaded, 16)

        @block.gpsimd
        def _(pool):
            for m in (sh.ident, sh.identb, sh.mask_qk, sh.mask_kq):
                pool.memset(m[:], 0.0).then_inc(zeroed, 1)
            pool.wait_ge(zeroed, 4)
            for m in (sh.ident, sh.identb):
                pool.affine_select(out=m[:], in_=m[:], compare_op=ALU.not_equal, fill=1.0, base=0,
                                   pattern=[[-1, P]], channel_multiplier=1).then_inc(made, 1)
            pool.affine_select(out=sh.mask_qk[:], in_=sh.mask_qk[:], compare_op=ALU.is_ge, fill=MASKED, base=0,
                               pattern=[[-1, P]], channel_multiplier=1).then_inc(made, 1)
            pool.affine_select(out=sh.mask_kq[:], in_=sh.mask_kq[:], compare_op=ALU.is_ge, fill=MASKED, base=0,
                               pattern=[[1, P]], channel_multiplier=-1).then_inc(made, 1)
            pool.wait_ge(made, 4)

def store_stage(nc, sh, out_dram):
    with nc.cleanup_on_exit(), ExitStack() as ctx:
        stored = nc.alloc_semaphore("out_stored")
        block = ctx.enter_context(nc.Block())

        @block.sync
        def _(sp):
            sp.dma_start(out_dram.rearrange("b (t p) d -> p (b t) d", p=P), sh.x[:]).then_inc(stored, 16)
            sp.wait_ge(stored, 16)

class Norm:

    def __init__(self, nc, ctx, tag, tiles):
        self.tiles = tiles
        self.stats = ctx.enter_context(nc.sbuf_tensor(f"{tag}_stats", [P, tiles, 6], F32))
        self.moments = ctx.enter_context(nc.sbuf_tensor(f"{tag}_moments", [P, tiles, 2], F32))
        self.var = ctx.enter_context(nc.sbuf_tensor(f"{tag}_var", [P, tiles], F32))
        self.std = ctx.enter_context(nc.sbuf_tensor(f"{tag}_std", [P, tiles], F32))
        self.rstd = ctx.enter_context(nc.sbuf_tensor(f"{tag}_rstd", [P, tiles], F32))
        self.stats_done = nc.alloc_semaphore(f"{tag}_stats_done")
        self.var_ready = nc.alloc_semaphore(f"{tag}_var_ready")
        self.std_ready = nc.alloc_semaphore(f"{tag}_std_ready")
        self.rstd_ready = nc.alloc_semaphore(f"{tag}_rstd_ready")

def norm_vector(dve, n, src):
    for t in range(n.tiles):
        dve.bn_stats(n.stats[:, t, :], src[:, t, :]).then_inc(n.stats_done, 1)
    for t in range(n.tiles):
        dve.wait_ge(n.stats_done, t + 1)
        dve.bn_aggr(n.moments[:, t, :], n.stats[:, t, :]).then_inc(n.stats_done, 1)
    dve.wait_ge(n.stats_done, 2 * n.tiles)
    dve.tensor_scalar(n.var[:], n.moments[:, :, 1], EPS, None, ALU.add).then_inc(n.var_ready, 1)
    dve.wait_ge(n.std_ready, 1)
    dve.reciprocal(n.rstd[:], n.std[:]).then_inc(n.rstd_ready, 1)
    dve.wait_ge(n.rstd_ready, 1)

def norm_scalar(act, n):
    act.wait_ge(n.var_ready, 1)
    act.activation(n.std[:], n.var[:], ACT.Sqrt).then_inc(n.std_ready, 1)

def standardize(dve, n, dst, src, ready):
    for t in range(n.tiles):
        dve.tensor_scalar(dst[:, t, :], src[:, t, :], n.moments[:, t, 0:1], n.rstd[:, t:t + 1],
                          ALU.subtract, ALU.mult).then_inc(ready, 1)

def turn_tensor(pe, sh, u, banks, tiles, u_ready, ut_psum, ut_ready):
    per = BANK // P
    for g in range(tiles // per):
        pe.wait_ge(u_ready, per * (g + 1))
        if g >= 2:
            pe.wait_ge(ut_ready, g - 1)
        for j in range(per):
            mm = pe.transpose(banks[g % 2][:, j * P:(j + 1) * P], u[:, per * g + j, :], sh.ident[:])
        mm.then_inc(ut_psum, 1)

def turn_scalar(act, ut, banks, tiles, ut_psum, ut_ready):
    for g in range(tiles * P // BANK):
        act.wait_ge(ut_psum, g + 1)
        act.activation(ut[:, g * BANK:(g + 1) * BANK], banks[g % 2][:], ACT.Copy).then_inc(ut_ready, 1)


def causal_steps(tiles, per):
    return [(qb, k, max(0, k - per * qb)) for qb in range(tiles // per) for k in range(per * qb + per)]

def head_order(steps, per, halves, prep, first, last, lag=0):
    n = len(steps)
    blocks = steps[-1][0] + 1
    at = {}
    for qb in range(blocks):
        end = max(i for i, s in enumerate(steps) if s[0] == qb)
        carried = end + 1 == n
        if carried and first:
            continue
        begin = (0 if carried else end + 1) + lag
        at.setdefault(begin + 1 - (lag > 0), []).append(("fin", qb, -1 if carried else 0))
        for half in range(halves):
            at.setdefault(begin + 3 + half - (lag > 0), []).append(("out", halves * qb + half, -1 if carried else 0))
    order, used, done, spent = [], 0, 0.0, 0.0
    widths = [per - s[2] for s in steps]
    for i in range(n):
        done += widths[i] / sum(widths[:n - 5])
        while used < len(prep) and not last and spent <= done * sum(p[2] for p in prep):
            order.append((prep[used][0], prep[used][1], 1))
            spent += prep[used][2]
            used += 1
        order.append(("pv", i, 0))
        if lag and i >= lag:
            order.append(("lo", i - lag, 0))
        elif lag and not first:
            order.append(("lo", n + i - lag, -1))
        if i + 2 < n:
            order.append(("qk", i + 2, 0))
        elif not last:
            order.append(("qk", i + 2 - n, 1))
        order += at.get(i, [])
    if last:
        order += [("lo", i, 0) for i in range(n - lag, n)] if lag else []
        order.append(("fin", blocks - 1, 0))
        order += [("out", halves * (blocks - 1) + half, 0) for half in range(halves)]
    return order
def known(h):
    return isinstance(h, int)


def heads_stage(nc, sh, w_dram, wv_dram, wo_dram, heads):
    T = sh.tiles
    DH = 64
    PER = BANK // P
    N = T * P
    STEPS = causal_steps(T, PER)
    NS = len(STEPS)
    BLOCKS = T // PER
    HALVES = 2
    HT = PER // HALVES
    CHUNKS = [(t, c) for t in range(T) for c in range(t // PER + 1)]
    NC = len(CHUNKS)
    VP = BANK // (2 * DH)
    VS = T // VP
    USES = BLOCKS + VS + 1
    VH = 2
    SCALE = float(DH) ** -0.5
    CONSTS = 13
    AHEAD = 4
    LAG = 2
    OWNER = [int(n % 5 in (0, 2, 4)) for n in range(NS)]
    def preparation(par):
        prep = [("proj", 0, 0.5), ("high", 0, 0.9), ("low", 0, 2.2), ("proj", 1, 0.5), ("high", 1, 0.9), ("low", 1, 1.8)]
        between = [part for n in range(2, BLOCKS) for part in (("proj", n, 0.2), ("high", n, 0.2), ("low", n, 1.0))]
        for n in range(VH if par else VS):
            between += [("kept_high", n, 0.2), ("kept_low", n, 0.5)] if par else \
                [("value", n, 0.2), ("value_high", n, 0.2), ("value_low", n, 0.5)]
        for m in range(NC):
            prep.append(("max", m, 0.6))
            if m % 2 and m >= 3 and between:
                prep.append(between.pop(0))
        return prep + [("rowmax", 0, 1.5), ("mrow", 0, 1.0)]

    PREP = [preparation(par) for par in range(2)]
    with nc.cleanup_on_exit(), ExitStack() as ctx:
        sb = lambda name, shape, dt=F32: ctx.enter_context(nc.sbuf_tensor("a1_" + name, shape, dt))
        psum = lambda name, shape: ctx.enter_context(nc.psum_tensor("a1_" + name, shape, F32))
        sem = lambda name: nc.alloc_semaphore("a1_" + name)
        norm = Norm(nc, ctx, "a1n", T)
        u = sb("u", [P, T, P])
        ut = sb("ut", [P, N])
        w = [sb(f"w{i}", [P, 2 * DH]) for i in range(2)]
        wv = sb("wv", [P, 2 * DH])
        v_kept = sb("v_kept", [P, T, DH])
        wo = [sb(f"wo{i}", [DH + 1, P + 1]) for i in range(2)]
        q_hh = [sb(f"q_hh{i}", [P, N], F32R) for i in range(2)]
        q_lm = [sb(f"q_lm{i}", [P, N], F32R) for i in range(2)]
        k_lh = [sb(f"k_lh{i}", [P, N], F32R) for i in range(2)]
        k_h1 = [sb(f"k_h1{i}", [P, N], F32R) for i in range(2)]
        vh = [sb(f"vh{i}", [P, T, DH + 1], F32R) for i in range(2)]
        vl = [sb(f"vl{i}", [P, T, DH], F32R) for i in range(2)]
        part_max = sb("part_max", [P, T, T // PER])
        row_max = sb("row_max", [P, T])
        max_row = [sb(f"max_row{i}", [T, P], F32R) for i in range(2)]
        probs = [sb(f"probs{i}", [P, BANK]) for i in range(AHEAD)]
        ph = [sb(f"ph{i}", [P, BANK], F32R) for i in range(AHEAD)]
        pl = [sb(f"pl{i}", [P, BANK], F32R) for i in range(AHEAD)]
        block_out = [sb(f"block_out{i}", [DH + 1, BANK]) for i in range(2)]
        rden = sb("rden", [P, HT])
        s1 = [psum(f"s1_{i}", [P, BANK]) for i in range(2)]
        s2 = [psum(f"s2_{i}", [P, BANK]) for i in range(2)]
        o = [psum(f"o{i}", [P, BANK]) for i in range(2)]
        pj = psum("pj", [P, BANK])
        ob = psum("ob", [P, HT, BANK // HT])

        def max_banks(h):
            return [s1[0], s1[1], s2[0], s2[1], o[0], o[1]] if known(h) and h == 0 else s1

        def proj_bank(h, use):
            return ob[:].rearrange("p a b -> p (a b)") if known(h) and h == 0 and use % 2 else pj[:]

        u_ready = sem("u_ready")
        ut_psum = sem("ut_psum")
        ut_ready = sem("ut_ready")
        consts = sem("consts")
        w_loaded = [sem(f"w_loaded{i}") for i in range(2)]
        wo_loaded = [sem(f"wo_loaded{i}") for i in range(2)]
        proj_ready = sem("proj_ready")
        proj_free = sem("proj_free")
        split_hi = sem("split_hi")
        kh_copied = [sem(f"kh_copied{c}") for c in range(BLOCKS)]
        qh_copied = [sem(f"qh_copied{c}") for c in range(BLOCKS)]
        wv_loaded = sem("wv_loaded")
        vh_ready = sem("vh_ready")
        vl_ready = sem("vl_ready")
        s1_ready = sem("s1_ready")
        max_done = sem("max_done")
        m_ready = sem("m_ready")
        mrow_loaded = [sem(f"mrow_loaded{i}") for i in range(2)]
        s2_ready = sem("s2_ready")
        ph_ready = sem("ph_ready")
        exp_done = sem("exp_done")
        pl_ready = [sem(f"pl_ready{i}") for i in range(2)]
        pv_done = sem("pv_done")
        lo_done = sem("lo_done")
        fin_done = sem("fin_done")
        out_ready = sem("out_ready")
        rden_done = sem("rden_done")
        out_free = sem("out_free")
        block = ctx.enter_context(nc.Block())

        def run(emit):
            for what, n, _ in PREP[0]:
                emit(what, n, 0, 0)
            emit("qk", 0, 0, 0)
            emit("qk", 1, 0, 0)

            def head(h, par):
                for what, n, d in head_order(STEPS, PER, HALVES, PREP[1 - par], known(h) and h == 0,
                                                 known(h) and h == heads - 1, LAG):
                    emit(what, n, h + d, (par + d) % 2)

            return head

        def low_part(engine, owner, n, h):
            if OWNER[n] == owner:
                width = BANK - P * STEPS[n][2]
                engine.wait_ge(exp_done, NS * h + n + 1)
                engine.wait_ge(ph_ready, NS * h + n + 1)
                own = [m for m in range(NS) if OWNER[m] == owner]
                since = own[own.index(n) - 1] if n != own[0] else (-1 if known(h) and h == 0 else own[-1] - NS)
                if n >= AHEAD or not (known(h) and h == 0):
                    engine.wait_ge(lo_done, NS * h + n - AHEAD + 1)
                engine.tensor_tensor(pl[n % AHEAD][:, 0:width], probs[n % AHEAD][:, 0:width],
                                     ph[n % AHEAD][:, 0:width].bitcast(F32), ALU.subtract)\
                      .then_inc(pl_ready[owner], n - since)

        def loads(h, par):
            return 8 * (h - par) + 16

        @block.sync
        def _(sp):
            def weights(h, par):
                if not known(h) or h >= 2:
                    sp.wait_ge(proj_ready, USES * (h - 2) + BLOCKS + (0 if par else VS))
                sp.dma_start(w[par][:], w_dram[bass.ds(h, 1)].rearrange("a p n -> (a p) n"))\
                  .then_inc(w_loaded[par], 16)
                if par == 0:
                    sp.dma_start(wv[:], wv_dram[bass.ds(h // 2, 1)].rearrange("a p n -> (a p) n"))\
                      .then_inc(wv_loaded, 16)

            def out_weights(h, par):
                if not known(h) or h >= 2:
                    sp.wait_ge(out_ready, BLOCKS * HALVES * (h - 1))
                sp.dma_start(wo[par][0:DH, 0:P], wo_dram[bass.ds(h, 1)].rearrange("a p n -> (a p) n"))\
                  .then_inc(wo_loaded[par], 16)

            def maxima(h, par):
                sp.wait_ge(proj_free, USES * (h + 1))
                sp.dma_start(q_lm[par][DH:DH + 1, :].bitcast(F32), max_row[par][:, :].bitcast(F32))\
                  .then_inc(mrow_loaded[par], 16)

            def copies(h, par):
                for c in range(BLOCKS):
                    cs = slice(c * BANK, (c + 1) * BANK)
                    sp.wait_ge(split_hi, BLOCKS * h + c + 1)
                    sp.dma_start(k_h1[par][0:DH, cs].bitcast(F32), k_lh[par][DH:P, cs].bitcast(F32))\
                      .then_inc(kh_copied[c], 16)
                    sp.dma_start(q_hh[par][DH:P, cs].bitcast(F32), q_hh[par][0:DH, cs].bitcast(F32))\
                      .then_inc(qh_copied[c], 16)

            def head(h, par):
                if not known(h) or h + 2 < heads:
                    weights(h + 2, par)
                if not known(h) or h + 1 < heads:
                    copies(h + 1, 1 - par)
                    out_weights(h + 1, 1 - par)
                    maxima(h + 1, 1 - par)

            sp.wait_ge(consts, CONSTS)
            weights(0, 0)
            weights(1, 1)
            out_weights(0, 0)
            copies(0, 0)
            maxima(0, 0)
            head(0, 0)
            with sp.Fori(0, heads // 2 - 2) as i:
                head(2 * i + 1, 1)
                head(2 * i + 2, 0)
            for h in range(heads - 3, heads):
                head(h, h % 2)

        @block.gpsimd
        def _(pool):
            count = 0
            for i in range(2):
                for part, value in ((q_lm[i][DH:P, :].bitcast(F32), 0.0), (k_h1[i][DH:P, :].bitcast(F32), 0.0),
                                    (k_h1[i][DH:DH + 1, :].bitcast(F32), -1.0), (vh[i][:, :, DH:DH + 1].bitcast(F32), 1.0),
                                    (wo[i][:], 0.0), (wo[i][DH:DH + 1, P:P + 1], 1.0)):
                    pool.memset(part, value).then_inc(consts, 1)
                    count += 1
                    pool.wait_ge(consts, count)
            pool.memset(part_max[:], LOWEST).then_inc(consts, 1)

            def emit(what, n, h, par):
                if what == "pv":
                    low_part(pool, 1, n, h)

            head = run(emit)
            head(0, 0)
            with pool.Fori(0, heads // 2 - 1) as i:
                head(2 * i + 1, 1)
                head(2 * i + 2, 0)
            head(heads - 1, 1)

        @block.scalar
        def _(act):
            norm_scalar(act, norm)
            turn_scalar(act, ut, s1, T, ut_psum, ut_ready)
            def emit(what, n, h, par):
                if what == "high":
                    cs = slice(n * BANK, (n + 1) * BANK)
                    if n == 0 and not (known(h) and h < 2):
                        act.wait_ge(pv_done, NS * (h - 1))
                    act.wait_ge(proj_ready, USES * h + n + 1)
                    bank = proj_bank(h, n)
                    act.activation(q_hh[par][0:DH, cs], bank[0:DH, :], ACT.Copy)
                    act.activation(k_lh[par][DH:P, cs], bank[DH:P, :], ACT.Copy).then_inc(split_hi, 1)
                if what == "value_high":
                    if n == 0 and not (known(h) and h < 2):
                        act.wait_ge(lo_done, NS * (h - 1))
                        act.wait_ge(vl_ready, VH // 2 * h)
                    act.wait_ge(proj_ready, USES * h + BLOCKS + n + 1)
                    ts = slice(n * VP, (n + 1) * VP)
                    both = proj_bank(h, BLOCKS + n).rearrange("p (t v) -> p t v", v=2 * DH)
                    act.activation(v_kept[:, ts, :], both[:, :, DH:], ACT.Copy)
                    act.activation(vh[par][:, ts, 0:DH], both[:, :, 0:DH], ACT.Copy).then_inc(vh_ready, 1)
                if what == "kept_high":
                    if n == 0 and not (known(h) and h < 2):
                        act.wait_ge(lo_done, NS * (h - 1))
                    ts = slice(n * T // VH, (n + 1) * T // VH)
                    act.wait_ge(vh_ready, VS * h)
                    act.activation(vh[par][:, ts, 0:DH], v_kept[:, ts, :], ACT.Copy).then_inc(vh_ready, VS // VH)
                if what == "qk":
                    width = BANK - P * STEPS[n][2]
                    act.wait_ge(s2_ready, NS * h + n + 1)
                    if n >= AHEAD or not (known(h) and h == 0):
                        act.wait_ge(pv_done, NS * h + n - AHEAD + 1)
                    act.activation(ph[n % AHEAD][:, 0:width], s2[n % 2][:, 0:width], ACT.Exp,
                                   scale=SCALE).then_inc(ph_ready, 1)
                    if n >= AHEAD or not (known(h) and h == 0):
                        before = (n - AHEAD) % NS
                        act.wait_ge(pl_ready[OWNER[before]], NS * h + n - AHEAD + 1)
                    act.activation(probs[n % AHEAD][:, 0:width], s2[n % 2][:, 0:width], ACT.Exp,
                                   scale=SCALE).then_inc(exp_done, 1)
                if what == "fin":
                    last = max(i for i, s in enumerate(STEPS) if s[0] == n)
                    act.wait_ge(lo_done, NS * h + last + 1)
                    if n >= 2 or not (known(h) and h == 0):
                        act.wait_ge(out_ready, HALVES * (BLOCKS * h + n - 1))
                    act.activation(block_out[n % 2][:], o[n % 2][0:DH + 1, :], ACT.Copy).then_inc(fin_done, 1)

            head = run(emit)
            head(0, 0)
            with act.Fori(0, heads // 2 - 1) as i:
                head(2 * i + 1, 1)
                head(2 * i + 2, 0)
            head(heads - 1, 1)

        @block.tensor
        def _(pe):
            turn_tensor(pe, sh, u, s1, T, u_ready, ut_psum, ut_ready)
            pe.wait_ge(ut_ready, T // PER)
            pe.wait_ge(consts, CONSTS)

            def emit(what, n, h, par):
                if what == "proj":
                    if n == 0:
                        pe.wait_ge(w_loaded[par], loads(h, par))
                    if not (known(h) and h == 0):
                        pe.wait_ge(proj_free, USES * h + n)
                    elif n >= 2:
                        pe.wait_ge(proj_free, n - 1)
                    pe.matmul(proj_bank(h, n), w[par][:, 0:2 * DH], ut[:, n * BANK:(n + 1) * BANK],
                              start=True, stop=True).then_inc(proj_ready, 1)
                if what == "value":
                    if n == 0:
                        pe.wait_ge(wv_loaded, loads(h, 0))
                    others = int(known(h) and h == 0)
                    pe.wait_ge(proj_free, USES * h + BLOCKS + n - others)
                    bank = proj_bank(h, BLOCKS + n)
                    for j in range(VP):
                        t = n * VP + j
                        mm = pe.matmul(bank[:, j * 2 * DH:(j + 1) * 2 * DH], ut[:, t * P:(t + 1) * P], wv[:],
                                       start=True, stop=True)
                    mm.then_inc(proj_ready, 1)
                if what == "max":
                    t, c = CHUNKS[n]
                    width = min(BANK, (t + 1) * P - c * BANK)
                    diag = c == t // PER
                    if t % PER == 0 and c == 0:
                        pe.wait_ge(kh_copied[t // PER], 16 * h + 16)
                    banks = max_banks(h)
                    if n >= len(banks):
                        pe.wait_ge(max_done, NC * h + n + 1 - len(banks))
                    dst = banks[n % len(banks)]
                    mm = pe.matmul(dst[:, 0:width], q_hh[par][0:DH, t * P:(t + 1) * P],
                                   k_h1[par][0:DH, c * BANK:c * BANK + width], start=True, stop=not diag)
                    if diag:
                        mm = pe.matmul(dst[:, width - P:width], sh.identb[:], sh.mask_qk[:],
                                       start=False, stop=True)
                    mm.then_inc(s1_ready, 1)
                if what == "mrow":
                    pe.wait_ge(m_ready, h + 1)
                    pe.wait_ge(proj_free, USES * h + BLOCKS + (0 if par else VS))
                    pe.transpose(pj[0:T, 0:P], row_max[:], sh.ident[:]).then_inc(proj_ready, 1 + VS * par)
                if what == "qk":
                    qb, k, r = STEPS[n]
                    qs = slice((PER * qb + r) * P, (qb + 1) * BANK)
                    ks = slice(k * P, (k + 1) * P)
                    width = BANK - P * r
                    diag = k >= PER * qb
                    if k == 0:
                        pe.wait_ge(qh_copied[qb], 16 * h + 16)
                    if n == 0:
                        pe.wait_ge(mrow_loaded[par], loads(h, par))
                    if n >= 2 or not (known(h) and h == 0):
                        pe.wait_ge(exp_done, NS * h + n - 1)
                    dst = s2[n % 2]
                    pe.matmul(dst[:, 0:width], k_lh[par][:, ks], q_hh[par][:, qs], start=True, stop=False)
                    mm = pe.matmul(dst[:, 0:width], k_h1[par][:, ks], q_lm[par][:, qs], start=False, stop=not diag)
                    if diag:
                        mm = pe.matmul(dst[:, 0:P], sh.identb[:], sh.mask_kq[:], start=False, stop=True)
                    mm.then_inc(s2_ready, 1)
                if what == "pv":
                    qb, k, r = STEPS[n]
                    if n == 0:
                        pe.wait_ge(vh_ready, VS * h + VS)
                        if par:
                            pe.wait_ge(vl_ready, VH // 2 * (h + 1))
                        else:
                            pe.wait_ge(proj_free, USES * h + BLOCKS + VS)
                    pe.wait_ge(ph_ready, NS * h + n + 1)
                    if k == 0 and (qb >= 2 or not (known(h) and h == 0)):
                        pe.wait_ge(fin_done, BLOCKS * h + qb - 1)
                    pe.matmul(o[qb % 2][0:DH + 1, P * r:BANK], vh[par][:, k, :], ph[n % AHEAD][:, 0:BANK - P * r],
                              start=(k == 0), stop=False)
                    pe.matmul(o[qb % 2][0:DH, P * r:BANK], vl[par][:, k, :], ph[n % AHEAD][:, 0:BANK - P * r],
                              start=False, stop=False).then_inc(pv_done, 1)
                if what == "lo":
                    qb, k, r = STEPS[n]
                    pe.wait_ge(pl_ready[OWNER[n]], NS * h + n + 1)
                    pe.matmul(o[qb % 2][0:DH + 1, P * r:BANK], vh[par][:, k, :], pl[n % AHEAD][:, 0:BANK - P * r],
                              start=False, stop=(k == PER * qb + PER - 1)).then_inc(lo_done, 1)
                if what == "out":
                    qb = n // HALVES
                    if n == 0:
                        pe.wait_ge(wo_loaded[par], loads(h, par))
                    pe.wait_ge(fin_done, BLOCKS * h + qb + 1)
                    pe.wait_ge(out_free, BLOCKS * HALVES * h + n)
                    for j in range(HT):
                        q = (n % HALVES) * HT + j
                        mm = pe.matmul(ob[:, j, 0:P + 1], block_out[qb % 2][:, q * P:(q + 1) * P], wo[par][:],
                                       start=True, stop=True)
                    mm.then_inc(out_ready, 1)

            head = run(emit)
            head(0, 0)
            with pe.Fori(0, heads // 2 - 1) as i:
                head(2 * i + 1, 1)
                head(2 * i + 2, 0)
            head(heads - 1, 1)

        @block.vector
        def _(dve):
            norm_vector(dve, norm, sh.x)
            standardize(dve, norm, u, sh.x, u_ready)
            dve.wait_ge(consts, CONSTS)

            def emit(what, n, h, par):
                if what == "low":
                    cs = slice(n * BANK, (n + 1) * BANK)
                    dve.wait_ge(split_hi, BLOCKS * h + n + 1)
                    bank = proj_bank(h, n)
                    dve.tensor_tensor(q_lm[par][0:DH, cs], bank[0:DH, :], q_hh[par][0:DH, cs].bitcast(F32),
                                      ALU.subtract)
                    dve.tensor_tensor(k_lh[par][0:DH, cs], bank[DH:P, :], k_lh[par][DH:P, cs].bitcast(F32),
                                      ALU.subtract).then_inc(proj_free, 1)
                if what == "value_low":
                    ts = slice(n * VP, (n + 1) * VP)
                    dve.wait_ge(vh_ready, VS * h + n + 1)
                    both = proj_bank(h, BLOCKS + n).rearrange("p (t v) -> p t v", v=2 * DH)
                    dve.tensor_tensor(vl[par][:, ts, :], both[:, :, 0:DH],
                                      vh[par][:, ts, 0:DH].bitcast(F32), ALU.subtract).then_inc(proj_free, 1)
                if what == "kept_low":
                    ts = slice(n * T // VH, (n + 1) * T // VH)
                    dve.wait_ge(vh_ready, VS * h + (n + 1) * VS // VH)
                    dve.tensor_tensor(vl[par][:, ts, :], v_kept[:, ts, :], vh[par][:, ts, 0:DH].bitcast(F32),
                                      ALU.subtract).then_inc(vl_ready, 1)
                if what == "max":
                    t, c = CHUNKS[n]
                    width = min(BANK, (t + 1) * P - c * BANK)
                    dve.wait_ge(s1_ready, NC * h + n + 1)
                    bank = max_banks(h)[n % len(max_banks(h))]
                    dve.reduce_max(part_max[:, t, c:c + 1], bank[:, 0:width], AX.X).then_inc(max_done, 1)
                if what == "pv":
                    low_part(dve, 0, n, h)
                if what == "rowmax":
                    dve.wait_ge(max_done, NC * (h + 1))
                    dve.tensor_reduce(row_max[:], part_max[:], AX.X, ALU.max).then_inc(m_ready, 1)
                if what == "mrow":
                    dve.wait_ge(proj_ready, USES * (h + 1))
                    dve.tensor_copy(max_row[par][:], pj[0:T, 0:P]).then_inc(proj_free, 1 + VS * par)
                if what == "out":
                    use = BLOCKS * HALVES * h + n
                    dve.wait_ge(out_ready, use + 1)
                    dve.reciprocal(rden[:], ob[:, :, P]).then_inc(rden_done, 1)
                    dve.wait_ge(rden_done, use + 1)
                    for j in range(HT):
                        t = n * HT + j
                        mm = dve.scalar_tensor_tensor(out=sh.x[:, t, :], in0=ob[:, j, 0:P], scalar=rden[:, j:j + 1],
                                                      in1=sh.x[:, t, :], op0=ALU.mult, op1=ALU.add)
                    mm.then_inc(out_free, 1)

            head = run(emit)
            head(0, 0)
            with dve.Fori(0, heads // 2 - 1) as i:
                head(2 * i + 1, 1)
                head(2 * i + 2, 0)
            head(heads - 1, 1)

def rotary_stage(nc, sh, w_dram, wv_dram, wo_dram, table_dram, heads):
    T = sh.tiles
    D = P
    PER = BANK // P
    N = T * P
    STEPS = causal_steps(T, PER)
    NS = len(STEPS)
    BLOCKS = T // PER
    HALVES = 2
    HT = PER // HALVES
    CHUNKS = [(t, c) for t in range(T) for c in range(t // PER + 1)]
    NC = len(CHUNKS)
    RW = BANK // 2
    RC = N // RW
    RB = BANK // RW
    SCALE = float(D) ** -0.5
    AHEAD = 4
    LAG = 2
    PREP = [("rotate", 0, 1.5), ("rotate", 1, 1.5)]
    for b in range(BLOCKS):
        PREP += [("rotate", RB * (b + 1) + r, 1.5) for r in range(RB)] if b + 1 < BLOCKS else []
        PREP += [("max", m, 0.6) for m, (t, c) in enumerate(CHUNKS) if t // PER == b]
    PREP += [("rowmax", 0, 1.0), ("mrow", 0, 1.0)]
    with nc.cleanup_on_exit(), ExitStack() as ctx:
        sb = lambda name, shape, dt=F32: ctx.enter_context(nc.sbuf_tensor("a0_" + name, shape, dt))
        psum = lambda name, shape: ctx.enter_context(nc.psum_tensor("a0_" + name, shape, F32))
        sem = lambda name: nc.alloc_semaphore("a0_" + name)
        norm = Norm(nc, ctx, "a0n", T)
        u = sb("u", [P, T, P])
        ut = sb("ut", [P, N])
        w = sb("w", [P, heads + 1, 2, D])
        wv = sb("wv", [P, D])
        wo = sb("wo", [P, heads, P])
        table = sb("table", [P, RC, 2, RW])
        hi = sb("hi", [P, heads + 1, N], F32R)
        lo = sb("lo", [P, heads + 1, N], F32R)
        product = [sb(f"product{i}", [P, 2, RW]) for i in range(2)]
        rotated = [sb(f"rotated{i}", [P, RW]) for i in range(2)]
        vh = sb("vh", [P, T, D], F32R)
        vl = sb("vl", [P, T, D], F32R)
        part_max = sb("part_max", [P, T, T // PER])
        row_max = sb("row_max", [P, T])
        turned_max = [sb(f"turned_max{i}", [T, P], F32R) for i in range(heads)]
        max_row = [sb(f"max_row{i}", [1, N], F32R) for i in range(heads)]
        minus_one = sb("minus_one", [1, P], F32R)
        one = sb("one", [P, 1])
        probs = [sb(f"probs{i}", [P, BANK]) for i in range(AHEAD)]
        ph = [sb(f"ph{i}", [P, BANK], F32R) for i in range(AHEAD)]
        pl = [sb(f"pl{i}", [P, BANK], F32R) for i in range(AHEAD)]
        prob_sum = [sb(f"prob_sum{i}", [P, BANK]) for i in range(2)]
        block_out = [sb(f"block_out{i}", [P, BANK]) for i in range(2)]
        rden = sb("rden", [P, HT])
        s1 = [psum(f"s1_{i}", [P, BANK]) for i in range(2)]
        s2 = [psum(f"s2_{i}", [P, BANK]) for i in range(2)]
        o = [psum(f"o{i}", [P, BANK]) for i in range(2)]
        pj = psum("pj", [P, 2, RW])
        ob = psum("ob", [P, HT, BANK // HT])

        def rotate_bank(h, n):
            return o[1][:].rearrange("p (s t) -> p s t", s=2) if h <= 0 and n % 2 else pj[:]

        def max_banks(h):
            return [s1[0], s1[1], s2[0], s2[1]] if h == 0 else s1

        u_ready = sem("u_ready")
        ut_psum = sem("ut_psum")
        ut_ready = sem("ut_ready")
        consts = sem("consts")
        w_loaded = sem("w_loaded")
        wv_loaded = sem("wv_loaded")
        wo_loaded = sem("wo_loaded")
        table_loaded = sem("table_loaded")
        v_psum = sem("v_psum")
        vh_ready = sem("vh_ready")
        vl_ready = sem("vl_ready")
        pair_ready = sem("pair_ready")
        product_done = sem("product_done")
        rotated_done = sem("rotated_done")
        hi_ready = sem("hi_ready")
        lo_ready = sem("lo_ready")
        s1_ready = sem("s1_ready")
        max_done = sem("max_done")
        m_ready = sem("m_ready")
        turned_ready = sem("turned_ready")
        turned_out = sem("turned_out")
        mrow_loaded = [sem(f"mrow_loaded{i}") for i in range(heads)]
        s2_ready = sem("s2_ready")
        exp_done = sem("exp_done")
        summed = sem("summed")
        ph_ready = sem("ph_ready")
        pl_ready = sem("pl_ready")
        pv_done = sem("pv_done")
        lo_done = sem("lo_done")
        fin_done = sem("fin_done")
        out_ready = sem("out_ready")
        rden_done = sem("rden_done")
        out_free = sem("out_free")
        block = ctx.enter_context(nc.Block())

        def run(emit):
            for n in range(RC):
                emit("rotate", n, -1)
            for what, n, _ in PREP:
                emit(what, n, 0)
            emit("qk", 0, 0)
            emit("qk", 1, 0)
            for h in range(heads):
                for what, n, d in head_order(STEPS, PER, HALVES, PREP, h == 0, h == heads - 1, LAG):
                    emit(what, n, h + d)

        last_of = lambda qb: max(i for i, s in enumerate(STEPS) if s[0] == qb)

        @block.sync
        def _(sp):
            sp.dma_start(w[:], w_dram).then_inc(w_loaded, 16)
            sp.dma_start(table[:], table_dram).then_inc(table_loaded, 16)
            sp.dma_start(wv[:], wv_dram).then_inc(wv_loaded, 16)
            sp.dma_start(wo[:], wo_dram).then_inc(wo_loaded, 16)
            for h in range(heads):
                sp.wait_ge(turned_out, h + 1)
                sp.dma_start(max_row[h][:].bitcast(F32), turned_max[h][:].bitcast(F32))\
                  .then_inc(mrow_loaded[h], 16)

        @block.gpsimd
        def _(pool):
            pool.memset(minus_one[:].bitcast(F32), -1.0).then_inc(consts, 1)
            pool.memset(one[:], 1.0).then_inc(consts, 1)
            pool.memset(part_max[:], LOWEST).then_inc(consts, 1)

            def emit(what, n, h):
                if what == "rotate":
                    use = RC * (h + 1) + n
                    ns = slice(n * RW, (n + 1) * RW)
                    pool.wait_ge(hi_ready, use + 1)
                    pool.tensor_tensor(lo[:, h + 1, ns], rotated[n % 2][:], hi[:, h + 1, ns].bitcast(F32),
                                       ALU.subtract).then_inc(lo_ready, 1)
                if what == "pv":
                    qb, k, r = STEPS[n]
                    block_no = BLOCKS * h + qb
                    pool.wait_ge(exp_done, NS * h + n + 1)
                    total = prob_sum[qb % 2]
                    if k == 0:
                        if block_no >= 2:
                            pool.wait_ge(out_ready, HALVES * (block_no - 1))
                        pool.tensor_copy(total[:], probs[n % AHEAD][:]).then_inc(summed, 1)
                    else:
                        pool.wait_ge(summed, NS * h + n)
                        pool.tensor_tensor(total[:, P * r:], total[:, P * r:], probs[n % AHEAD][:, 0:BANK - P * r],
                                           ALU.add).then_inc(summed, 1)

            run(emit)

        @block.scalar
        def _(act):
            norm_scalar(act, norm)
            turn_scalar(act, ut, s1, T, ut_psum, ut_ready)
            for g in range(BLOCKS):
                act.wait_ge(v_psum, g + 1)
                act.activation(vh[:, PER * g:PER * g + PER, :].rearrange("p t d -> p (t d)"), s2[g % 2][:],
                               ACT.Copy).then_inc(vh_ready, 1)

            def emit(what, n, h):
                if what == "rotate":
                    use = RC * (h + 1) + n
                    act.wait_ge(rotated_done, use + 1)
                    act.activation(hi[:, h + 1, n * RW:(n + 1) * RW], rotated[n % 2][:], ACT.Copy)\
                       .then_inc(hi_ready, 1)
                if what == "qk":
                    width = BANK - P * STEPS[n][2]
                    use = NS * h + n
                    act.wait_ge(s2_ready, use + 1)
                    if use >= AHEAD:
                        act.wait_ge(pv_done, use - AHEAD + 1)
                    act.activation(ph[n % AHEAD][:, 0:width], s2[n % 2][:, 0:width], ACT.Exp,
                                   scale=SCALE).then_inc(ph_ready, 1)
                    if use >= AHEAD:
                        act.wait_ge(pl_ready, use - AHEAD + 1)
                        act.wait_ge(summed, use - AHEAD + 1)
                    act.activation(probs[n % AHEAD][:, 0:width], s2[n % 2][:, 0:width], ACT.Exp,
                                   scale=SCALE).then_inc(exp_done, 1)
                if what == "fin":
                    block_no = BLOCKS * h + n
                    act.wait_ge(lo_done, NS * h + last_of(n) + 1)
                    if block_no >= 2:
                        act.wait_ge(out_ready, HALVES * (block_no - 1))
                    act.activation(block_out[n % 2][:], o[n % 2][:], ACT.Copy).then_inc(fin_done, 1)

            run(emit)

        @block.tensor
        def _(pe):
            turn_tensor(pe, sh, u, s1, T, u_ready, ut_psum, ut_ready)
            pe.wait_ge(ut_ready, T // PER)
            pe.wait_ge(wv_loaded, 16)
            for g in range(BLOCKS):
                if g >= 2:
                    pe.wait_ge(vl_ready, g - 1)
                for j in range(PER):
                    t = PER * g + j
                    mm = pe.matmul(s2[g % 2][:, j * P:(j + 1) * P], ut[:, t * P:(t + 1) * P], wv[:],
                                   start=True, stop=True)
                mm.then_inc(v_psum, 1)
            pe.wait_ge(vl_ready, BLOCKS)
            pe.wait_ge(w_loaded, 16)
            pe.wait_ge(consts, 3)

            def emit(what, n, h):
                if what == "rotate":
                    use = RC * (h + 1) + n
                    others = 1 if h <= 0 else 0
                    if use > others:
                        pe.wait_ge(product_done, use - others)
                    bank = rotate_bank(h, n)
                    for s in range(2):
                        mm = pe.matmul(bank[:, s, :], w[:, h + 1, s, :], ut[:, n * RW:(n + 1) * RW],
                                       start=True, stop=True)
                    mm.then_inc(pair_ready, 1)
                if what == "max":
                    t, c = CHUNKS[n]
                    width = min(BANK, (t + 1) * P - c * BANK)
                    diag = c == t // PER
                    if t % PER == 0 and c == 0:
                        pe.wait_ge(hi_ready, RC * (h + 1) + RB * (t // PER + 1))
                    banks = max_banks(h)
                    if n >= len(banks):
                        pe.wait_ge(max_done, NC * h + n + 1 - len(banks))
                    dst = banks[n % len(banks)]
                    mm = pe.matmul(dst[:, 0:width], hi[:, h + 1, t * P:(t + 1) * P],
                                   hi[:, 0, c * BANK:c * BANK + width], start=True, stop=not diag)
                    if diag:
                        mm = pe.matmul(dst[:, width - P:width], sh.identb[:], sh.mask_qk[:],
                                       start=False, stop=True)
                    mm.then_inc(s1_ready, 1)
                if what == "mrow":
                    pe.wait_ge(m_ready, h + 1)
                    pe.wait_ge(product_done, RC * (h + 2))
                    pe.transpose(pj[0:T, 0, 0:P], row_max[:], sh.ident[:]).then_inc(turned_ready, 1)
                if what == "qk":
                    qb, k, r = STEPS[n]
                    qs = slice((PER * qb + r) * P, (qb + 1) * BANK)
                    ks = slice(k * P, (k + 1) * P)
                    width = BANK - P * r
                    diag = k >= PER * qb
                    use = NS * h + n
                    if n == 0:
                        pe.wait_ge(mrow_loaded[h], 16)
                        pe.wait_ge(lo_ready, RC * (h + 2))
                    if use >= 2:
                        pe.wait_ge(exp_done, use - 1)
                    dst = s2[n % 2]
                    pe.matmul(dst[:, 0:width], hi[:, 0, ks], hi[:, h + 1, qs], start=True, stop=False)
                    pe.matmul(dst[:, 0:width], hi[:, 0, ks], lo[:, h + 1, qs], start=False, stop=False)
                    pe.matmul(dst[:, 0:width], lo[:, 0, ks], hi[:, h + 1, qs], start=False, stop=False)
                    mm = pe.matmul(dst[:, 0:width], minus_one[:], max_row[h][:, qs], start=False, stop=not diag)
                    if diag:
                        mm = pe.matmul(dst[:, 0:P], sh.identb[:], sh.mask_kq[:], start=False, stop=True)
                    mm.then_inc(s2_ready, 1)
                if what == "pv":
                    qb, k, r = STEPS[n]
                    pe.wait_ge(ph_ready, NS * h + n + 1)
                    if k == 0 and BLOCKS * h + qb >= 2:
                        pe.wait_ge(fin_done, BLOCKS * h + qb - 1)
                    pe.matmul(o[qb % 2][:, P * r:BANK], vh[:, k, :], ph[n % AHEAD][:, 0:BANK - P * r],
                              start=(k == 0), stop=False)
                    pe.matmul(o[qb % 2][:, P * r:BANK], vl[:, k, :], ph[n % AHEAD][:, 0:BANK - P * r],
                              start=False, stop=False).then_inc(pv_done, 1)
                if what == "lo":
                    qb, k, r = STEPS[n]
                    pe.wait_ge(pl_ready, NS * h + n + 1)
                    pe.matmul(o[qb % 2][:, P * r:BANK], vh[:, k, :], pl[n % AHEAD][:, 0:BANK - P * r],
                              start=False, stop=(k == PER * qb + PER - 1)).then_inc(lo_done, 1)
                if what == "out":
                    qb = n // HALVES
                    use = BLOCKS * HALVES * h + n
                    if use == 0:
                        pe.wait_ge(wo_loaded, 16)
                    pe.wait_ge(fin_done, BLOCKS * h + qb + 1)
                    pe.wait_ge(summed, NS * h + last_of(qb) + 1)
                    if use >= 1:
                        pe.wait_ge(out_free, use)
                    for j in range(HT):
                        q = (n % HALVES) * HT + j
                        pe.matmul(ob[:, j, 0:P], block_out[qb % 2][:, q * P:(q + 1) * P], wo[:, h, :],
                                  start=True, stop=True)
                        mm = pe.matmul(ob[:, j, P:P + 1], prob_sum[qb % 2][:, q * P:(q + 1) * P], one[:],
                                       start=True, stop=True)
                    mm.then_inc(out_ready, 1)

            run(emit)

        @block.vector
        def _(dve):
            norm_vector(dve, norm, sh.x)
            standardize(dve, norm, u, sh.x, u_ready)
            dve.wait_ge(consts, 3)
            for g in range(BLOCKS):
                dve.wait_ge(vh_ready, g + 1)
                ts = slice(PER * g, PER * g + PER)
                dve.tensor_tensor(vl[:, ts, :], s2[g % 2][:].rearrange("p (t d) -> p t d", d=D),
                                  vh[:, ts, :].bitcast(F32), ALU.subtract).then_inc(vl_ready, 1)
            dve.wait_ge(table_loaded, 16)

            def emit(what, n, h):
                if what == "rotate":
                    use = RC * (h + 1) + n
                    dve.wait_ge(pair_ready, use + 1)
                    dve.tensor_tensor(product[n % 2][:], rotate_bank(h, n), table[:, n], ALU.mult).then_inc(product_done, 1)
                    if use >= 2:
                        dve.wait_ge(lo_ready, use - 1)
                    dve.wait_ge(product_done, use + 1)
                    dve.tensor_tensor(rotated[n % 2][:], product[n % 2][:, 0, :], product[n % 2][:, 1, :],
                                      ALU.add).then_inc(rotated_done, 1)
                if what == "max":
                    t, c = CHUNKS[n]
                    width = min(BANK, (t + 1) * P - c * BANK)
                    dve.wait_ge(s1_ready, NC * h + n + 1)
                    bank = max_banks(h)[n % len(max_banks(h))]
                    dve.reduce_max(part_max[:, t, c:c + 1], bank[:, 0:width], AX.X).then_inc(max_done, 1)
                if what == "pv":
                    width = BANK - P * STEPS[n][2]
                    use = NS * h + n
                    dve.wait_ge(exp_done, use + 1)
                    dve.wait_ge(ph_ready, use + 1)
                    if use >= AHEAD:
                        dve.wait_ge(lo_done, use - AHEAD + 1)
                    dve.tensor_tensor(pl[n % AHEAD][:, 0:width], probs[n % AHEAD][:, 0:width],
                                      ph[n % AHEAD][:, 0:width].bitcast(F32), ALU.subtract).then_inc(pl_ready, 1)
                if what == "rowmax":
                    dve.wait_ge(max_done, NC * (h + 1))
                    dve.tensor_reduce(row_max[:], part_max[:], AX.X, ALU.max).then_inc(m_ready, 1)
                if what == "mrow":
                    dve.wait_ge(turned_ready, h + 1)
                    dve.tensor_copy(turned_max[h][:], pj[0:T, 0, 0:P]).then_inc(turned_out, 1)
                if what == "out":
                    use = BLOCKS * HALVES * h + n
                    dve.wait_ge(out_ready, use + 1)
                    dve.reciprocal(rden[:], ob[:, :, P]).then_inc(rden_done, 1)
                    dve.wait_ge(rden_done, use + 1)
                    for j in range(HT):
                        t = n * HT + j
                        mm = dve.scalar_tensor_tensor(out=sh.x[:, t, :], in0=ob[:, j, 0:P], scalar=rden[:, j:j + 1],
                                                      in1=sh.x[:, t, :], op0=ALU.mult, op1=ALU.add)
                    mm.then_inc(out_free, 1)

            run(emit)


def first_choice_stage(nc, sh, tag, router_dram, rbias_dram, we_dram, be_dram, experts):
    T = sh.tiles
    N = T * P
    E = experts
    H = E // 2
    PER = BANK // P
    BANKS = E * P // BANK
    with nc.cleanup_on_exit(), ExitStack() as ctx:
        sb = lambda name, shape, dt=F32: ctx.enter_context(nc.sbuf_tensor(f"{tag}_{name}", shape, dt))
        psum = lambda name, shape: ctx.enter_context(nc.psum_tensor(f"{tag}_{name}", shape, F32))
        sem = lambda name: nc.alloc_semaphore(f"{tag}_{name}")
        norm = Norm(nc, ctx, tag + "n", T)
        u = sb("u", [P, T, P])
        ut = sb("ut", [P, N])
        router = sb("router", [P, E])
        rbias = sb("rbias", [P, E])
        we = sb("we", [P, E * P])
        be = sb("be", [P, T, P])
        logits = sb("logits", [P, T, E])
        top = sb("top", [P, T])
        prob = sb("prob", [P, T, E])
        total = sb("total", [P, T])
        weight = sb("weight", [P, T])
        order = sb("order", [P, T, E])
        rank = sb("rank", [P, T, E])
        choice = sb("choice", [P, T, E])
        scaled = [sb(f"scaled{i}", [P, E - H, P]) for i in range(2)]
        pairs = sb("pairs", [P, (E - H) // 2, P])
        side = [sb(f"side{i}", [P, P]) for i in range(2)]
        beside = [sb(f"beside{i}", [P, P]) for i in range(2)]
        choice_t = sb("choice_t", [P, P])
        turn = [psum(f"turn{i}", [P, BANK]) for i in range(2)]
        y = [psum(f"y{i}", [P, E, P]) for i in range(2)]
        small = psum("small", [P, T, E])
        bias = psum("bias", [P, PER, P])

        loaded = sem("loaded")
        u_ready = sem("u_ready")
        ut_psum = sem("ut_psum")
        ut_ready = sem("ut_ready")
        consts = sem("consts")
        be_loaded = sem("be_loaded")
        logits_psum = sem("logits_psum")
        step = sem("step")
        shifted = sem("shifted")
        exp_done = sem("exp_done")
        choice_ready = sem("choice_ready")
        turned = sem("turned")
        turned_out = sem("turned_out")
        y_ready = sem("y_ready")
        y_used = sem("y_used")
        added = sem("added")
        scaled_ready = sem("scaled_ready")
        pairs_ready = sem("pairs_ready")
        side_ready = sem("side_ready")
        bias_ready = sem("bias_ready")
        bias_used = sem("bias_used")
        block = ctx.enter_context(nc.Block())

        @block.sync
        def _(sp):
            sp.dma_start(router[:], router_dram).then_inc(loaded, 16)
            sp.dma_start(rbias[:], rbias_dram.partition_broadcast(P)).then_inc(loaded, 16)
            sp.dma_start(we[:], we_dram).then_inc(loaded, 16)
            sp.wait_ge(consts, 1)
            for t in range(T):
                sp.dma_start(be[t * E:(t + 1) * E, t, :], be_dram).then_inc(be_loaded, 16)

        @block.gpsimd
        def _(pool):
            pool.memset(be[:], 0.0).then_inc(consts, 1)
            for e in range(E):
                pool.memset(order[:, :, e:e + 1], float(E - e)).then_inc(consts, 1)
            for t in range(T):
                pool.wait_ge(scaled_ready, t + 1)
                if t >= 1:
                    pool.wait_ge(side_ready, t)
                half = (E - H) // 2
                pool.tensor_tensor(pairs[:], scaled[t % 2][:, 0:half, :], scaled[t % 2][:, half:, :], ALU.add)\
                    .then_inc(pairs_ready, 1)
                pool.wait_ge(pairs_ready, t + 1)
                if t >= 2:
                    pool.wait_ge(added, t - 1)
                pool.tensor_tensor(side[t % 2][:], pairs[:, 0, :], pairs[:, 1, :], ALU.add).then_inc(side_ready, 1)

        @block.scalar
        def _(act):
            norm_scalar(act, norm)
            turn_scalar(act, ut, turn, T, ut_psum, ut_ready)
            act.wait_ge(shifted, 1)
            act.activation(prob[:], logits[:], ACT.Exp).then_inc(exp_done, 1)
            act.wait_ge(choice_ready, 1)
            for t in range(T):
                act.wait_ge(y_ready, t + 1)
                if t >= 2:
                    act.wait_ge(pairs_ready, t - 1)
                for e in range(H, E):
                    mul = act.activation(scaled[t % 2][:, e - H, :], y[t % 2][:, e, :], ACT.Copy,
                                         scale=choice[:, t, e:e + 1])
                mul.then_inc(scaled_ready, 1)

        @block.tensor
        def _(pe):
            turn_tensor(pe, sh, u, turn, T, u_ready, ut_psum, ut_ready)
            pe.wait_ge(ut_ready, T // PER)
            pe.wait_ge(loaded, 48)
            for t in range(T):
                mm = pe.matmul(small[:, t, :], ut[:, t * P:(t + 1) * P], router[:], start=True, stop=True)
            mm.then_inc(logits_psum, 1)

            def tile(t):
                if t >= 2:
                    pe.wait_ge(y_used, t - 1)
                    pe.wait_ge(scaled_ready, t - 1)
                for b in range(BANKS):
                    mm = pe.matmul(y[t % 2][:, b * PER:(b + 1) * PER, :].rearrange("p e o -> p (e o)"),
                                   ut[:, t * P:(t + 1) * P], we[:, b * BANK:(b + 1) * BANK], start=True, stop=True)
                mm.then_inc(y_ready, 1)

            tile(0)
            tile(1)
            pe.wait_ge(choice_ready, 1)
            pe.transpose(turn[0][:, 0:P], choice[:].rearrange("p t e -> p (t e)"), sh.ident[:]).then_inc(turned, 1)
            pe.wait_ge(turned_out, 1)
            pe.wait_ge(be_loaded, 16 * T)
            for g in range(T // PER):
                if g:
                    pe.wait_ge(bias_used, g)
                for j in range(PER):
                    mm = pe.matmul(bias[:, j, :], choice_t[:], be[:, PER * g + j, :], start=True, stop=True)
                mm.then_inc(bias_ready, 1)
                for t in range(PER * g, PER * g + PER):
                    if t >= 2:
                        tile(t)

        @block.vector
        def _(dve):
            norm_vector(dve, norm, sh.x)
            standardize(dve, norm, u, sh.x, u_ready)
            wide = lambda a: a[:].unsqueeze(2).broadcast_to([P, T, E])
            count = 0

            def post(instruction):
                nonlocal count
                instruction.then_inc(step, 1)
                count += 1

            def then(instruction):
                nonlocal count
                instruction.then_inc(step, 1)
                count += 1
                dve.wait_ge(step, count)

            dve.wait_ge(loaded, 48)
            dve.wait_ge(logits_psum, 1)
            then(dve.tensor_tensor(logits[:], small[:], rbias[:].unsqueeze(1).broadcast_to([P, T, E]), ALU.add))
            then(dve.tensor_reduce(top[:], logits[:], AX.X, ALU.max))
            dve.tensor_tensor(logits[:], logits[:], wide(top), ALU.subtract).then_inc(shifted, 1)
            dve.wait_ge(exp_done, 1)
            dve.wait_ge(consts, 1 + E)
            then(dve.tensor_reduce(top[:], prob[:], AX.X, ALU.max))
            then(dve.tensor_reduce(total[:], prob[:], AX.X, ALU.add))
            then(dve.reciprocal(total[:], total[:]))
            then(dve.tensor_tensor(rank[:], prob[:], wide(top), ALU.is_equal))
            then(dve.tensor_tensor(rank[:], rank[:], order[:], ALU.mult))
            then(dve.scalar_tensor_tensor(out=weight[:], in0=top[:], scalar=0.5, in1=total[:], op0=ALU.mult,
                                          op1=ALU.mult))
            then(dve.tensor_reduce(top[:], rank[:], AX.X, ALU.max))
            then(dve.tensor_tensor(rank[:], rank[:], wide(top), ALU.is_equal))
            dve.tensor_tensor(choice[:], rank[:], wide(weight), ALU.mult).then_inc(choice_ready, 1)
            dve.wait_ge(turned, 1)
            dve.tensor_copy(choice_t[:], turn[0][:, 0:P]).then_inc(turned_out, 1)
            dve.wait_ge(choice_ready, 1)

            def finish(t):
                dve.wait_ge(side_ready, t + 1)
                then(dve.tensor_tensor(sh.x[:, t, :], sh.x[:, t, :], side[t % 2][:], ALU.add))
                dve.wait_ge(y_used, t + 1)
                dve.tensor_tensor(sh.x[:, t, :], sh.x[:, t, :], beside[t % 2][:], ALU.add).then_inc(added, 1)
                dve.wait_ge(added, t + 1)

            for t in range(T):
                if t % PER == 0:
                    g = t // PER
                    xs = sh.x[:, t:t + PER, :]
                    dve.wait_ge(bias_ready, g + 1)
                    dve.tensor_tensor(xs, bias[:], xs, ALU.add).then_inc(bias_used, 1)
                    dve.wait_ge(bias_used, g + 1)
                dve.wait_ge(y_ready, t + 1)
                for e in range(H):
                    y_e, c_e = y[t % 2][:, e, :], choice[:, t, e:e + 1]
                    total_e = beside[t % 2][:] if e % 2 else sh.x[:, t, :]
                    if e >= 2:
                        dve.wait_ge(step, count - 1)
                    if e == 1:
                        post(dve.tensor_scalar(total_e, y_e, c_e, None, ALU.mult))
                    else:
                        add = dve.scalar_tensor_tensor(out=total_e, in0=y_e, scalar=c_e, in1=total_e,
                                                       op0=ALU.mult, op1=ALU.add)
                        if e < H - 1:
                            post(add)
                add.then_inc(y_used, 1)
                if t:
                    finish(t - 1)
            finish(T - 1)


def balanced_stage(nc, sh, tag, cent_dram, g_dram, b_dram, w1_dram, b1_dram, w2_dram, b2_dram, experts, hidden):
    T = sh.tiles
    N = T * P
    E = experts
    C = N // E
    CT = C // P
    PER = BANK // P
    F = hidden // P
    RADIX = 16
    G = P // RADIX
    GT = N // G
    HALF = 1 << 16
    STEPS = [HALF // RADIX ** (i + 1) for i in range(4)]
    CHAIN = 4 * len(STEPS) + 6
    LIST = 5
    ROUNDS = 2 * len(STEPS)
    TAKEN = -1e5
    with nc.cleanup_on_exit(), ExitStack() as ctx:
        sb = lambda name, shape, dt=F32: ctx.enter_context(nc.sbuf_tensor(f"{tag}_{name}", shape, dt))
        psum = lambda name, shape: ctx.enter_context(nc.psum_tensor(f"{tag}_{name}", shape, F32))
        sem = lambda name: nc.alloc_semaphore(f"{tag}_{name}")
        dram = lambda name, shape: nc.dram_tensor(f"{tag}_{name}", shape, F32, kind="Internal").ap()
        norm = Norm(nc, ctx, tag + "n", T)
        norm2 = Norm(nc, ctx, tag + "m", T)
        u = sb("u", [P, T, P])
        nrm = sb("nrm", [P, T, P])
        gain = sb("gain", [P, P])
        shift = sb("shift", [P, P])
        cent = sb("cent", [P, E])
        nt = sb("nt", [P, N])
        score = sb("score", [P, E, T])
        flip = sb("flip", [P, E * T], I32)
        key = sb("key", [P, E * T], I32)
        halves = sb("halves", [P, 2, E * T], I32)
        half = sb("half", [P, 2, E * T])
        half_t = sb("half_t", [P, 2, P])
        keys = sb("keys", [P, 2, E, GT])
        taken = sb("taken", [P, GT])
        high = sb("high", [P, GT])
        both = sb("both", [P, GT])
        junk = sb("junk", [P, GT])
        cnt = [sb(f"cnt{i}", [P, 1], BF16) for i in range(2)]
        weight = sb("weight", [P, ROUNDS, RADIX + 1])
        reach = sb("reach", [P, RADIX + 1])
        cand = sb("cand", [P, 2])
        cand0 = sb("cand0", [P, 2])
        move = sb("move", [P, ROUNDS])
        lane = sb("lane", [P, 1], I32)
        lane_f = sb("lane_f", [P, 1])
        group_i = sb("group_i", [P, 1], I32)
        lane_all = sb("lane_all", [P, 1])
        iota_i = sb("iota_i", [P, P], I32)
        iota_f = sb("iota_f", [P, P])
        pick = sb("pick", [P, RADIX + 1], BF16)
        before = sb("before", [P, P], BF16)
        minus_before = sb("minus_before", [P, P], BF16)
        minus_every = sb("minus_every", [P, P], BF16)
        pick_group = sb("pick_group", [P, G, P], BF16)
        place = sb("place", [P, CT])
        above = sb("above", [P, GT])
        equal = sb("equal", [P, GT])
        tied = sb("tied", [P, 2], BF16)
        equal_sum = sb("equal_sum", [P, GT])
        ones = sb("ones", [P, GT])
        ranks = sb("ranks", [P, 4])
        equal_taken = sb("equal_taken", [P, 1])
        fresh = sb("fresh", [P, GT])
        left = sb("left", [P, GT])
        full = sb("full", [P, 1])
        chosen = sb("chosen", [P, GT])
        chosen_sum = sb("chosen_sum", [P, GT])
        base = sb("base", [P, 1])
        chosen_upto = sb("chosen_upto", [P, GT], BF16)
        sign = [sb(f"sign{i}", [P, N], BF16) for i in range(CT)]
        balance = sb("balance", [P, CT])
        token = sb("token", [P, E, CT], U32)
        routed = [sb(f"routed{i}", [P, CT, P]) for i in range(2)]
        routed_t = [sb(f"routed_t{i}", [P, C]) for i in range(2)]
        w1 = [sb(f"w1_{i}", [P, hidden]) for i in range(2)]
        w2 = [sb(f"w2_{i}", [P, F, P]) for i in range(2)]
        b1 = sb("b1", [P, E, F])
        b2 = sb("b2", [P, E, P])
        hid = [sb(f"hid{i}", [P, F, C]) for i in range(2)]
        y = sb("y", [P, T, P])
        back = sb("back", [P, T, P])
        turn = [psum(f"turn{i}", [P, BANK]) for i in range(2)]
        counts = psum("counts", [P, BANK])
        upto = psum("upto", [P, N])
        hp = [turn[0], psum("hp", [P, BANK])]
        yp = turn[1][:, 0:C].rearrange("p (s d) -> p s d", d=P)
        keys_dram = dram("keys_dram", (2, E * T, P))
        nrm_dram = dram("nrm_dram", (N, P))
        y_dram = dram("y_dram", (N, P))

        loaded = sem("loaded")
        biases = sem("biases")
        u_ready = sem("u_ready")
        std2 = sem("std2")
        gained = sem("gained")
        nrm_ready = sem("nrm_ready")
        nt_psum = sem("nt_psum")
        nt_ready = sem("nt_ready")
        scored = sem("scored")
        prep = sem("prep")
        key_ready = sem("key_ready")
        key_psum = sem("key_psum")
        key_out = sem("key_out")
        key_stored = sem("key_stored")
        key_loaded = [sem(f"key_loaded{i}") for i in range(2)]
        consts = sem("consts")
        shapes = sem("shapes")
        chain = sem("chain")
        listed = sem("listed")
        above_ready = sem("above_ready")
        fresh_ready = sem("fresh_ready")
        cnt_ready = sem("cnt_ready")
        counts_ready = sem("counts_ready")
        tied_ready = sem("tied_ready")
        ranks_ready = sem("ranks_ready")
        chosen_ready = sem("chosen_ready")
        upto_ready = sem("upto_ready")
        sign_done = sem("sign_done")
        token_ready = sem("token_ready")
        nrm_stored = sem("nrm_stored")
        routed_loaded = [sem(f"routed_loaded{i}") for i in range(2)]
        rt_psum = sem("rt_psum")
        rt_ready = sem("rt_ready")
        w_loaded = [sem(f"w_loaded{i}") for i in range(2)]
        h_psum = sem("h_psum")
        h_ready = sem("h_ready")
        y_psum = sem("y_psum")
        y_ready = sem("y_ready")
        y_stored = sem("y_stored")
        y_back = sem("y_back")
        half_added = sem("half_added")
        SHAPES = 5 + 2 * (1 + 2 * len(STEPS)) + CT

        def stages(engine, body):
            for e in range(4):
                body(e, e % 2)
            with engine.Fori(2, E // 2) as i:
                body(2 * i, 0)
                body(2 * i + 1, 1)
            for e in range(E, E + 3):
                body(e, e % 2)

        block = ctx.enter_context(nc.Block())

        @block.sync
        def _(sp):
            sp.dma_start(gain[:], g_dram.partition_broadcast(P)).then_inc(loaded, 16)
            sp.dma_start(shift[:], b_dram.partition_broadcast(P)).then_inc(loaded, 16)
            sp.dma_start(cent[:], cent_dram).then_inc(loaded, 16)
            sp.dma_start(b1[:], b1_dram).then_inc(biases, 16)
            sp.dma_start(b2[:].rearrange("p e d -> p (e d)"), b2_dram.partition_broadcast(P)).then_inc(biases, 16)

            def weights(e, par):
                sp.dma_start(w1[par][:], w1_dram[bass.ds(e, 1)].rearrange("a p f -> (a p) f"))\
                  .then_inc(w_loaded[par], 16)
                sp.dma_start(w2[par][:], w2_dram[bass.ds(e, 1)].rearrange("a (c p) d -> (a p) c d", p=P))\
                  .then_inc(w_loaded[par], 16)

            weights(0, 0)
            weights(1, 1)
            sp.wait_ge(nrm_ready, T)
            sp.dma_start(nrm_dram.rearrange("(t p) d -> p t d", p=P), nrm[:]).then_inc(nrm_stored, 16)
            sp.wait_ge(key_out, 1)
            sp.dma_start(keys_dram.rearrange("h r p -> r h p"), half_t[:]).then_inc(key_stored, 16)
            sp.wait_ge(key_stored, 16)
            by_group = keys_dram.rearrange("h (e t) p -> h e (t p)", e=E)
            for g in range(G):
                gs, ts = slice(g * RADIX, (g + 1) * RADIX), slice(g * GT, (g + 1) * GT)
                sp.dma_start(keys[gs, :, 0], by_group[:, 0, ts].partition_broadcast(RADIX)).then_inc(key_loaded[0], 16)
            for h in range(2):
                for g in range(G):
                    gs, ts = slice(g * RADIX, (g + 1) * RADIX), slice(g * GT, (g + 1) * GT)
                    sp.dma_start(keys[gs, h, 1:], by_group[h, 1:, ts].partition_broadcast(RADIX))\
                      .then_inc(key_loaded[1], 16)
            with sp.Fori(0, E // 2 - 1) as i:
                for par in range(2):
                    e = 2 * i + par
                    sp.wait_ge(y_psum, e + 1)
                    weights(e + 2, par)
            sp.wait_ge(y_stored, 16 * E * CT)
            sp.dma_start(back[:], y_dram.rearrange("(t p) d -> p t d", p=P)).then_inc(y_back, 16)

        @block.gpsimd
        def _(pool):
            pool.iota(lane[:], pattern=[[0, 1]], base=0, channel_multiplier=1).then_inc(consts, 1)
            pool.iota(iota_i[:], pattern=[[1, P]], base=0, channel_multiplier=0).then_inc(consts, 1)
            pool.memset(minus_every[:], -1.0 / RADIX).then_inc(consts, 1)
            pool.memset(before[:], 1.0 / RADIX).then_inc(consts, 1)
            pool.memset(minus_before[:], -1.0 / RADIX).then_inc(consts, 1)
            pool.memset(pick[:], 1.0).then_inc(consts, 1)
            pool.memset(equal[:], 0.0).then_inc(consts, 1)
            pool.memset(pick_group[:], 0.0).then_inc(consts, 1)
            pool.memset(ones[:], 1.0).then_inc(consts, 1)
            pool.memset(full[:], float(C)).then_inc(consts, 1)
            pool.memset(taken[:], 0.0).then_inc(consts, 1)
            pool.wait_ge(consts, 11)
            for m in (before, minus_before):
                blocks = m[:].rearrange("p (b r) -> p b r", r=RADIX)
                pool.affine_select(out=blocks, in_=blocks, compare_op=ALU.is_gt, fill=0.0, base=0,
                                   pattern=[[RADIX, G], [0, RADIX]], channel_multiplier=-1).then_inc(consts, 1)
            pool.affine_select(out=pick_group[:], in_=pick_group[:], compare_op=ALU.not_equal, fill=1.0, base=0,
                               pattern=[[-RADIX, G], [0, P]], channel_multiplier=1).then_inc(consts, 1)

            def fetch(e):
                pool.wait_ge(token_ready, e + 1)
                if e >= 2:
                    pool.wait_ge(rt_psum, e - 1)
                for s in range(CT):
                    pool.indirect_dma_start(out=routed[e % 2][:, s, :], out_offset=None, in_=nrm_dram,
                                            in_offset=bass.IndirectOffsetOnAxis(ap=token[:, e, s:s + 1], axis=0))\
                        .then_inc(routed_loaded[e % 2], 16)

            def store(e):
                pool.wait_ge(y_ready, e + 1)
                for s in range(CT):
                    pool.indirect_dma_start(out=y_dram, out_offset=bass.IndirectOffsetOnAxis(ap=token[:, e, s:s + 1], axis=0),
                                            in_=y[:, e * CT + s, :], in_offset=None).then_inc(y_stored, 16)

            pool.wait_ge(nrm_stored, 16)
            for e in range(E + 2):
                if e < E:
                    fetch(e)
                if e >= 2:
                    store(e - 2)

        @block.scalar
        def _(act):
            norm_scalar(act, norm)
            norm_scalar(act, norm2)
            turn_scalar(act, nt, turn, T, nt_psum, nt_ready)
            act.wait_ge(key_psum, 1)
            act.activation(half_t[:].rearrange("p h q -> p (h q)"), turn[0][:, 0:2 * P], ACT.Copy).then_inc(key_out, 1)
            act.wait_ge(biases, 32)
            act.wait_ge(shapes, SHAPES)

            def find(e):
                if not (known(e) and e == 0):
                    act.wait_ge(token_ready, e)
                act.wait_ge(upto_ready, e + 1)
                for s in range(CT):
                    act.activation(sign[s][:], upto[:], ACT.Sign, bias=place[:, s:s + 1], accum_out=balance[:, s:s + 1])\
                       .then_inc(sign_done, 1)

            def found(e):
                act.wait_ge(sign_done, CT * e + CT)
                act.activation(token[:, bass.ds(e, 1), :].rearrange("p a s -> p (a s)"), balance[:], ACT.Copy,
                               scale=-0.5, bias=N / 2.0).then_inc(token_ready, 1)

            def turned(e, par):
                act.wait_ge(rt_psum, e + 1)
                act.activation(routed_t[par][:], turn[0][:, 0:C], ACT.Copy).then_inc(rt_ready, 1)

            def first_layer(e, par):
                for c in range(F):
                    act.wait_ge(h_psum, F * e + c + 1)
                    if not (known(e) and e < 2) and c == 0:
                        act.wait_ge(y_psum, e - 1)
                    act.activation(hid[par][:, c, :], hp[c % 2][:, 0:C], ACT.Gelu_apprx_tanh,
                                   bias=b1[:, bass.ds(e, 1), c:c + 1].rearrange("p a b -> p (a b)")).then_inc(h_ready, 1)

            def body(e, par):
                if not known(e) or 3 <= e:
                    first_layer(e - 3, 1 - par)
                if not known(e) or 2 <= e <= E + 1:
                    turned(e - 2, par)
                if not known(e) or 1 <= e <= E:
                    find(e - 1)
                    found(e - 1)

            stages(act, body)

        @block.tensor
        def _(pe):
            pe.wait_ge(loaded, 48)
            for g in range(T // PER + 1):
                if g < T // PER:
                    pe.wait_ge(nrm_ready, PER * (g + 1))
                    if g >= 2:
                        pe.wait_ge(nt_ready, g - 1)
                    for t in range(PER * g, PER * (g + 1)):
                        mm = pe.transpose(turn[g % 2][:, t % PER * P:(t % PER + 1) * P], nrm[:, t, :], sh.ident[:])
                    mm.then_inc(nt_psum, 1)
                if g >= 1:
                    pe.wait_ge(nt_ready, g)
                    for t in range(PER * (g - 1), PER * g):
                        mm = pe.matmul(counts[:, t * E:(t + 1) * E], nt[:, t * P:(t + 1) * P], cent[:],
                                       start=True, stop=True)
            mm.then_inc(scored, 1)
            pe.wait_ge(key_ready, 1)
            for h in range(2):
                mm = pe.transpose(turn[0][:, h * P:(h + 1) * P], half[:, h, :], sh.ident[:])
            mm.then_inc(key_psum, 1)

            def count(e, r):
                if not known(e) or e < E:
                    pe.wait_ge(cnt_ready, ROUNDS * e + r + 1)
                    pe.matmul(counts[:, 0:RADIX + 1], cnt[r % 2][:].broadcast_to([P, P]), pick[:], start=True, stop=True)\
                      .then_inc(counts_ready, 1)

            def spread(e, gs):
                if not known(e) or 0 <= e < E:
                    if gs[0] == 0:
                        pe.wait_ge(chosen_ready, e + 1)
                        if not (known(e) and e == 0):
                            pe.wait_ge(sign_done, CT * e)
                    for g in gs:
                        mm = pe.matmul(upto[:, g * GT:(g + 1) * GT], pick_group[:, g, :], chosen_upto[:],
                                       start=True, stop=True)
                    if gs[-1] == G - 1:
                        mm.then_inc(upto_ready, 1)

            def turn_routed(e, par):
                if not known(e) or 0 <= e < E:
                    pe.wait_ge(routed_loaded[par], 16 * (e - par) + 32)
                    if not (known(e) and e == 0):
                        pe.wait_ge(rt_ready, e)
                        pe.wait_ge(h_ready, F * e - 1)
                    for s in range(CT):
                        mm = pe.transpose(turn[0][:, s * P:(s + 1) * P], routed[par][:, s, :], sh.ident[:])
                    mm.then_inc(rt_psum, 1)

            def up(e, par, c):
                if not known(e) or 0 <= e < E:
                    if c == 0:
                        pe.wait_ge(w_loaded[par], 16 * (e - par) + 32)
                        pe.wait_ge(rt_ready, e + 1)
                    if not (known(e) and e == 0 and c < 2):
                        pe.wait_ge(h_ready, F * e + c - 1)
                    pe.matmul(hp[c % 2][:, 0:C], w1[par][:, c * P:(c + 1) * P], routed_t[par][:], start=True,
                              stop=True).then_inc(h_psum, 1)

            def down(e, par, pieces):
                if not known(e) or 0 <= e < E:
                    if pieces[0] == 0:
                        if not (known(e) and e == 0):
                            pe.wait_ge(y_ready, e)
                        pe.wait_ge(h_ready, F * e + F)
                    for piece in pieces:
                        s, c = divmod(piece, F)
                        mm = pe.matmul(yp[:, s, :], hid[par][:, c, s * P:(s + 1) * P], w2[par][:, c, :],
                                       start=(c == 0), stop=(c == F - 1))
                    if pieces[-1] == CT * F - 1:
                        mm.then_inc(y_psum, 1)

            def body(e, par):
                for c in range(F):
                    count(e, c)
                    up(e - 3, 1 - par, c)
                for part in range(2):
                    count(e, F + part)
                    spread(e - 1, range(part * G // 2, (part + 1) * G // 2))
                count(e, F + 2)
                turn_routed(e - 2, par)
                down(e - 3, 1 - par, range(0, 2))
                count(e, F + 3)
                down(e - 3, 1 - par, range(2, 4))
                if not known(e) or e < E:
                    pe.wait_ge(tied_ready, e + 1)
                    pe.matmul(counts[:, 0:2], before[:], tied[:], start=True, stop=True)
                    pe.matmul(counts[:, 2:3], minus_every[:], tied[:, 0:1], start=True, stop=False)
                    pe.matmul(counts[:, 2:3], minus_before[:], tied[:, 1:2], start=False, stop=True)
                    pe.matmul(counts[:, 3:4], minus_every[:], tied[:, 0:1], start=True, stop=True)\
                      .then_inc(ranks_ready, 1)
                down(e - 3, 1 - par, range(4, CT * F))

            pe.wait_ge(consts, 14)
            pe.wait_ge(key_out, 1)
            stages(pe, body)

        @block.vector
        def _(dve):
            norm_vector(dve, norm, sh.x)
            standardize(dve, norm, u, sh.x, u_ready)
            dve.wait_ge(u_ready, T)
            norm_vector(dve, norm2, u)
            standardize(dve, norm2, nrm, u, std2)
            dve.wait_ge(loaded, 48)
            for g in range(T // PER):
                ts = slice(PER * g, PER * g + PER)
                dve.wait_ge(std2, PER * (g + 1))
                dve.tensor_tensor(nrm[:, ts], nrm[:, ts], gain[:].unsqueeze(1).broadcast_to([P, PER, P]), ALU.mult)\
                   .then_inc(gained, 1)
                dve.wait_ge(gained, g + 1)
                dve.tensor_tensor(nrm[:, ts], nrm[:, ts], shift[:].unsqueeze(1).broadcast_to([P, PER, P]), ALU.add)\
                   .then_inc(nrm_ready, PER)
            count = 0

            def then(instruction):
                nonlocal count
                instruction.then_inc(prep, 1)
                count += 1
                dve.wait_ge(prep, count)

            dve.wait_ge(scored, 1)
            then(dve.tensor_copy(score[:].rearrange("p e t -> p t e"),
                                 counts[:, 0:T * E].rearrange("p (t e) -> p t e", e=E)))
            bits = score[:].rearrange("p e t -> p (e t)").bitcast(I32)
            then(dve.tensor_scalar(flip[:], bits, 31, 0x7FFFFFFF, ALU.arith_shift_right, ALU.bitwise_and))
            then(dve.tensor_tensor(key[:], bits, flip[:], ALU.bitwise_xor))
            then(dve.tensor_single_scalar(halves[:, 0, :], key[:], 16, ALU.arith_shift_right))
            then(dve.tensor_single_scalar(halves[:, 1, :], key[:], HALF - 1, ALU.bitwise_and))
            then(dve.tensor_copy(half[:, 0, :], halves[:, 0, :]))
            then(dve.tensor_copy(half[:, 1, :], halves[:, 1, :]))
            dve.tensor_scalar(half[:, 1, :], half[:, 1, :], 1.0 / HALF, None, ALU.mult).then_inc(key_ready, 1)
            dve.scalar_tensor_tensor(out=sh.x[:], in0=u[:], scalar=0.5, in1=sh.x[:], op0=ALU.mult, op1=ALU.add)\
               .then_inc(half_added, 1)

            count = 0

            def made(instruction):
                nonlocal count
                instruction.then_inc(shapes, 1)
                count += 1
                dve.wait_ge(shapes, count)

            dve.wait_ge(consts, 14)
            made(dve.tensor_copy(lane_all[:], lane[:]))
            made(dve.tensor_single_scalar(group_i[:], lane[:], RADIX - 1, ALU.bitwise_and))
            made(dve.tensor_copy(lane_f[:], group_i[:]))
            made(dve.tensor_copy(iota_f[:], iota_i[:]))
            made(dve.tensor_scalar(pick[:, 0:RADIX], iota_f[:, 0:RADIX], lane_f[:, 0:1], None, ALU.is_equal))
            for i in range(2):
                scale = 1.0 / HALF if i else 1.0
                made(dve.tensor_scalar(cand0[:, i:i + 1], lane_f[:], STEPS[0] * scale, 0.0 if i else -HALF / 2,
                                       ALU.mult, ALU.add))
                for s, step in enumerate(STEPS):
                    made(dve.tensor_scalar(weight[:, 4 * i + s, :], iota_f[:, 0:RADIX + 1], 0.0, step * scale, ALU.mult,
                                           ALU.add))
                    following = STEPS[s + 1] if s + 1 < len(STEPS) else 0
                    made(dve.tensor_scalar(move[:, 4 * i + s:4 * i + s + 1], lane_f[:], (following - step) * scale,
                                           -step * scale, ALU.mult, ALU.add))

            for s in range(CT):
                made(dve.tensor_scalar(place[:, s:s + 1], lane_all[:], -1.0, -(s * P + 0.5), ALU.mult, ALU.add))
            assert count == SHAPES

            dve.wait_ge(key_loaded[0], 16 * G)

            key_of = lambda h, e: keys[:, h, bass.ds(e, 1), :].rearrange("p a t -> p (a t)")

            def list_tokens(e, part):
                if part == 0:
                    dve.tensor_tensor(chosen[:], above[:], equal[:], ALU.add).then_inc(listed, 1)
                    dve.tensor_tensor(equal_taken[:], ranks[:, 3:4], full[:], ALU.add).then_inc(listed, 1)
                if part == 1:
                    dve.wait_ge(listed, LIST * e + 2)
                    dve.tensor_tensor_scan(chosen_sum[:], ones[:], chosen[:], 0.0, ALU.mult, ALU.add)\
                       .then_inc(listed, 1)
                    dve.scalar_tensor_tensor(out=base[:], in0=ranks[:, 1:2], scalar=equal_taken[:, 0:1],
                                             in1=ranks[:, 0:1], op0=ALU.min, op1=ALU.add).then_inc(listed, 1)
                if part == 2:
                    dve.wait_ge(listed, LIST * e + 4)
                    if not (known(e) and e == 0):
                        dve.wait_ge(upto_ready, e)
                    dve.tensor_tensor(chosen_upto[:], chosen_sum[:], base[:].broadcast_to([P, GT]), ALU.add)\
                       .then_inc(chosen_ready, 1)
                if part == 3:
                    dve.scalar_tensor_tensor(out=taken[:], in0=chosen[:], scalar=TAKEN, in1=taken[:],
                                             op0=ALU.mult, op1=ALU.add).then_inc(listed, 1)

            def body(e):
                done = 0

                def then(instruction):
                    nonlocal done
                    instruction.then_inc(chain, 1)
                    done += 1
                    dve.wait_ge(chain, CHAIN * e + done + 1)

                for i in range(2):
                    if i:
                        then(dve.scalar_tensor_tensor(out=both[:], in0=high[:], scalar=cand[:, 0:1], in1=key_of(1, e),
                                                      op0=ALU.subtract, op1=ALU.add))
                    for s in range(len(STEPS)):
                        r = len(STEPS) * i + s
                        now = cand0[:, i:i + 1] if s == 0 else cand[:, i:i + 1]
                        dve.tensor_scalar(junk[:], (both if i else high)[:], now, 0.0, ALU.is_ge, ALU.add,
                                          accum_out=cnt[r % 2][:]).then_inc(cnt_ready, 1)
                        dve.tensor_tensor(weight[:, r, RADIX:RADIX + 1], now, move[:, r:r + 1], ALU.add)\
                           .then_inc(chain, 1)
                        done += 1
                        if r < 4 and (not known(e) or e >= 1):
                            list_tokens(e - 1, r)
                        if r == 4 and not (known(e) and e == E - 1):
                            if known(e) and e == 0:
                                dve.wait_ge(key_loaded[1], 32 * G)
                            else:
                                dve.wait_ge(listed, LIST * e)
                            dve.tensor_tensor(fresh[:], key_of(0, e + 1), taken[:], ALU.add).then_inc(fresh_ready, 1)
                        if r == 5 and (not known(e) or e >= 4):
                            add_bias(e - 4)
                        dve.wait_ge(counts_ready, ROUNDS * e + r + 1)
                        dve.wait_ge(chain, CHAIN * e + done + 1)
                        then(dve.scalar_tensor_tensor(out=reach[:], in0=counts[:, 0:RADIX + 1], scalar=float(C),
                                                      in1=weight[:, r, :], op0=ALU.is_ge, op1=ALU.mult,
                                                      accum_out=cand[:, i:i + 1]))
                if not (known(e) and e == 0):
                    dve.wait_ge(listed, LIST * e)
                dve.tensor_scalar(above[:], both[:], cand[:, 1:2], 0.0, ALU.is_gt, ALU.add, accum_out=tied[:, 0:1])\
                   .then_inc(above_ready, 1)
                dve.tensor_scalar(equal[:], both[:], cand[:, 1:2], 0.0, ALU.is_equal, ALU.add,
                                  accum_out=tied[:, 1:2]).then_inc(tied_ready, 1)
                dve.wait_ge(tied_ready, e + 1)
                then(dve.tensor_tensor_scan(equal_sum[:], ones[:], equal[:], -float(C), ALU.mult, ALU.add))
                if not (known(e) and e == E - 1):
                    dve.wait_ge(above_ready, e + 1)
                    dve.wait_ge(fresh_ready, e + 1)
                    then(dve.scalar_tensor_tensor(out=left[:], in0=above[:], scalar=TAKEN, in1=fresh[:],
                                                  op0=ALU.mult, op1=ALU.add))
                dve.wait_ge(ranks_ready, e + 1)
                dve.tensor_copy(ranks[:], counts[:, 0:4]).then_inc(chain, 1)
                done += 1
                then(dve.scalar_tensor_tensor(out=equal[:], in0=equal_sum[:], scalar=counts[:, 2:3], in1=equal[:],
                                              op0=ALU.is_le, op1=ALU.mult))
                if not (known(e) and e == E - 1):
                    then(dve.scalar_tensor_tensor(out=high[:], in0=equal[:], scalar=TAKEN, in1=left[:],
                                                  op0=ALU.mult, op1=ALU.add))
                    assert done == CHAIN

            def add_bias(e):
                dve.wait_ge(y_psum, e + 1)
                dve.tensor_tensor(y[:, bass.ds(e * CT, CT), :], yp, b2[:, bass.ds(e, 1), :].broadcast_to([P, CT, P]),
                                  ALU.add).then_inc(y_ready, 1)

            dve.wait_ge(biases, 32)
            dve.tensor_copy(high[:], key_of(0, 0)).then_inc(chain, 1)
            dve.wait_ge(chain, 1)
            for e in range(4):
                body(e)
            with dve.Fori(4, E - 1) as e:
                body(e)
            body(E - 1)
            for part in range(3):
                list_tokens(E - 1, part)
            for e in range(E - 4, E):
                add_bias(e)
            dve.wait_ge(half_added, 1)
            dve.wait_ge(y_back, 16)
            dve.scalar_tensor_tensor(out=sh.x[:], in0=back[:], scalar=0.5, in1=sh.x[:], op0=ALU.mult, op1=ALU.add)\
               .then_inc(half_added, 1)

def rotary_table(tokens, width, chunk):
    import numpy as np
    positions = np.arange(0, width, 2, dtype=np.float64)
    theta = np.power(10000.0, -2.0 * positions / width).astype(np.float32)
    angles = (np.arange(tokens, dtype=np.float32)[:, None] * theta[None, :]).astype(np.float32)
    cos = np.repeat(np.cos(angles).astype(np.float32).T, 2, axis=0)
    sin = np.repeat(np.sin(angles).astype(np.float32).T, 2, axis=0)
    sin[0::2] = -sin[0::2]
    both = np.stack([cos.reshape(width, -1, chunk), sin.reshape(width, -1, chunk)], axis=2)
    return np.ascontiguousarray(both)


def build(nc, x, cent, ln_g, ln_b, w1, b1, w2, b2, rot_w, rot_wv, rot_wo, rot_table, heads_w, heads_wv, wo, router, rbias, we, be,
          out):
    tokens, width = x.shape[1], x.shape[2]
    experts, _, hidden = w1.shape
    with ExitStack() as ctx:
        sh = Shared(nc, ctx, tokens, width)
        load_stage(nc, sh, x)
        balanced_stage(nc, sh, "f0a", cent, ln_g, ln_b, w1, b1, w2, b2, experts, hidden)
        rotary_stage(nc, sh, rot_w, rot_wv, rot_wo, rot_table, rot_wo.shape[1])
        balanced_stage(nc, sh, "f0b", cent, ln_g, ln_b, w1, b1, w2, b2, experts, hidden)
        first_choice_stage(nc, sh, "f1a", router, rbias, we, be, router.shape[1])
        heads_stage(nc, sh, heads_w, heads_wv, wo, wo.shape[0])
        first_choice_stage(nc, sh, "f1b", router, rbias, we, be, router.shape[1])
        store_stage(nc, sh, out)

def kernel(L0_attn_x, L0_attn_Wq, L0_attn_Wk, L0_attn_Wv, L0_attn_Wo, L0_ffn_centroids, L0_ffn_ln_g, L0_ffn_ln_b,
           L0_ffn_w1, L0_ffn_b1, L0_ffn_w2, L0_ffn_b2, L1_attn_w_q, L1_attn_w_k, L1_attn_w_v, L1_attn_w_o,
           L1_ffn_router_w, L1_ffn_router_b, L1_ffn_expert_w, L1_ffn_expert_b):
    import numpy as np
    import concourse.bacc as _bacc
    from concourse.bass_utils import run_bass_kernel_spmd as _run

    x = np.asarray(L0_attn_x)
    _, tokens, width = x.shape
    experts, _, hidden = L0_ffn_w1.shape
    heads, dh, _ = L1_attn_w_q.shape
    rot_heads = L0_attn_Wq.shape[0]
    plain = np.concatenate([np.asarray(L0_attn_Wk)[None], np.asarray(L0_attn_Wq)])
    swapped = plain.reshape(-1, width // 2, 2, width)[:, :, ::-1].reshape(plain.shape)
    arrays = {
        "x": x,
        "cent": np.asarray(L0_ffn_centroids).T,
        "ln_g": np.asarray(L0_ffn_ln_g),
        "ln_b": np.asarray(L0_ffn_ln_b),
        "w1": np.asarray(L0_ffn_w1),
        "b1": np.asarray(L0_ffn_b1).reshape(experts, hidden // P, P).transpose(2, 0, 1),
        "w2": np.asarray(L0_ffn_w2),
        "b2": np.asarray(L0_ffn_b2).reshape(-1),
        "rot_w": np.stack([plain, swapped], axis=1).transpose(3, 0, 1, 2),
        "rot_wv": np.asarray(L0_attn_Wv).T,
        "rot_wo": np.asarray(L0_attn_Wo).reshape(width, rot_heads, width).transpose(2, 1, 0),
        "rot_table": rotary_table(tokens, width, 256),
        "heads_w": np.concatenate([np.asarray(L1_attn_w_q), np.asarray(L1_attn_w_k)], axis=1).transpose(0, 2, 1),
        "heads_wv": np.asarray(L1_attn_w_v).reshape(heads // 2, 2 * dh, width).transpose(0, 2, 1),
        "wo": np.asarray(L1_attn_w_o).T.reshape(heads, dh, width),
        "router": np.asarray(L1_ffn_router_w).T,
        "rbias": np.asarray(L1_ffn_router_b),
        "we": np.asarray(L1_ffn_expert_w).transpose(2, 0, 1).reshape(width, -1),
        "be": np.asarray(L1_ffn_expert_b),
    }
    nc = _bacc.Bacc("TRN2", target_bir_lowering=False, num_devices=1)
    arrays = {name: np.ascontiguousarray(a) for name, a in arrays.items()}
    args = [nc.dram_tensor(name, a.shape, mybir.dt.from_np(a.dtype), kind="ExternalInput").ap()
            for name, a in arrays.items()]
    out = nc.dram_tensor("out", x.shape, F32, kind="ExternalOutput").ap()
    build(nc, *args, out)
    result = _run(nc, [arrays], core_ids=[0])
    return result.results[0]["out"]
```
